# Optimizing a Trainium2 kernel written in Bass

```python
import numpy as np
import jax
import jax.numpy as jnp

def _softmax(x, axis=-1):
    return jax.nn.softmax(x, axis=axis)
def _gelu(x):
    return jax.nn.gelu(x, approximate=True)
def _silu(x):
    return jax.nn.silu(x)
def _sigmoid(x):
    return jax.nn.sigmoid(x)
def _layernorm(x, axis=-1, eps=1e-5):
    m = jnp.mean(x, axis=axis, keepdims=True)
    v = jnp.var(x, axis=axis, keepdims=True)
    return (x - m) / jnp.sqrt(v + eps)
def _scatter_add(tgt, idx, src, axis=0):
    return tgt.at[idx].add(src)
def _segment_sum(src, seg, n):
    return jax.ops.segment_sum(src, seg, n)

kernel_name = 'mk_metaformer_d1_conv_nchw512_5c4457'

def setup_inputs(seed: int = 0):
    np.random.seed(seed)
    _w = jnp.asarray
    def _rec_inputs():
        import jax
        import jax.numpy as jnp
        _gk = jax.random.key(seed)
        x = -0.0002928 + 1 * jax.random.normal(jax.random.fold_in(_gk, 1), (2, 512, 64, 64), jnp.float32)
        return x
    x = _rec_inputs()
    def _L0_conv_setup():
        import jax, jax.numpy as jnp
        import numpy as np
        DIM = 512
        D_STATE = 16
        D_CONV = 4
        D_INNER = 1024
        DT_RANK = 32
        EPS = 1e-05

        def _selective_scan(u, delta, A, Bm, Cm, D_skip):

            def step(h, inp):
                u_t, d_t, b_t, c_t = inp
                dA = jnp.exp(d_t[..., None] * A)
                dBu = (d_t * u_t)[..., None] * b_t[:, None, :]
                h = dA * h + dBu
                y = jnp.einsum('bdn,bn->bd', h, c_t)
                return (h, y)
            B, L, d = u.shape
            h0 = jnp.zeros((B, d, A.shape[1]), u.dtype)
            xs = (u.transpose(1, 0, 2), delta.transpose(1, 0, 2), Bm.transpose(1, 0, 2), Cm.transpose(1, 0, 2))
            _, ys = jax.lax.scan(step, h0, xs)
            y = ys.transpose(1, 0, 2)
            return y + u * D_skip

        def _mamba_layer(x, ln_w, ln_b, in_proj_w, conv_w, conv_b, x_proj_w, dt_proj_w, dt_proj_b, A_log, D_skip, out_proj_w):
            B, C = x.shape[:2]
            img_dims = x.shape[2:]
            xf = x.reshape(B, C, -1).transpose(0, 2, 1)
            mu = jnp.mean(xf, -1, keepdims=True)
            var = jnp.mean(jnp.square(xf - mu), -1, keepdims=True)
            xn = (xf - mu) * jax.lax.rsqrt(var + EPS) * ln_w + ln_b
            xz = xn @ in_proj_w.T
            xin, z = jnp.split(xz, 2, axis=-1)
            xc = xin.transpose(0, 2, 1)
            w = conv_w[:, None, :]
            xc = jax.lax.conv_general_dilated(xc, w, window_strides=(1,), padding=[(D_CONV - 1, 0)], feature_group_count=D_INNER, dimension_numbers=('NCH', 'OIH', 'NCH'))
            xc = jax.nn.silu(xc + conv_b[None, :, None])
            xs = xc.transpose(0, 2, 1)
            x_dbl = xs @ x_proj_w.T
            dt = x_dbl[..., :DT_RANK]
            Bm = x_dbl[..., DT_RANK:DT_RANK + D_STATE]
            Cm = x_dbl[..., DT_RANK + D_STATE:]
            delta = jax.nn.softplus(dt @ dt_proj_w.T + dt_proj_b)
            A = -jnp.exp(A_log)
            y = _selective_scan(xs, delta, A, Bm, Cm, D_skip)
            y = y * jax.nn.silu(z)
            out = y @ out_proj_w.T
            return out.transpose(0, 2, 1).reshape(B, C, *img_dims)
        key = jax.random.key(seed)
        ks = jax.random.split(key, 8)
        s = 0.02
        x = jax.random.normal(ks[0], (2, DIM, 64, 64), jnp.float32)
        in_proj_w = jax.random.normal(ks[1], (2 * D_INNER, DIM), jnp.float32) * s
        conv_w = jax.random.normal(ks[2], (D_INNER, D_CONV), jnp.float32) * 0.25
        conv_b = jnp.zeros((D_INNER,), jnp.float32)
        x_proj_w = jax.random.normal(ks[3], (DT_RANK + 2 * D_STATE, D_INNER), jnp.float32) * s
        dt_proj_w = jax.random.normal(ks[4], (D_INNER, DT_RANK), jnp.float32) * DT_RANK ** (-0.5)
        dt_proj_b = jnp.full((D_INNER,), -4.0, jnp.float32)
        A_log = jnp.log(jnp.broadcast_to(jnp.arange(1, D_STATE + 1, dtype=jnp.float32), (D_INNER, D_STATE)))
        D_skip = jnp.ones((D_INNER,), jnp.float32)
        out_proj_w = jax.random.normal(ks[5], (DIM, D_INNER), jnp.float32) * s
        ln_w = jnp.ones((DIM,), jnp.float32)
        ln_b = jnp.zeros((DIM,), jnp.float32)
        return {'x': x, 'ln_w': ln_w, 'ln_b': ln_b, 'in_proj_w': in_proj_w, 'conv_w': conv_w, 'conv_b': conv_b, 'x_proj_w': x_proj_w, 'dt_proj_w': dt_proj_w, 'dt_proj_b': dt_proj_b, 'A_log': A_log, 'D_skip': D_skip, 'out_proj_w': out_proj_w}
    _L0_conv_all = _L0_conv_setup()
    _L0_conv_in = {k: v for k, v in _L0_conv_all.items() if k in ('ln_w', 'ln_b', 'in_proj_w', 'conv_w', 'conv_b', 'x_proj_w', 'dt_proj_w', 'dt_proj_b', 'A_log', 'D_skip', 'out_proj_w', )}
    del _L0_conv_all

    def _L0_ffn_setup():
        import jax, jax.numpy as jnp
        import numpy as np
        N_CONST = 6
        PARTITIONS_OF_6 = [(6,), (5, 1), (4, 2), (4, 1, 1), (3, 3), (3, 2, 1), (3, 1, 1, 1), (2, 2, 2), (2, 2, 1, 1), (2, 1, 1, 1, 1), (1, 1, 1, 1, 1, 1)]
        N_EXPERTS = 6
        TOP_K = 2

        def _partition_weights():
            w = np.zeros((len(PARTITIONS_OF_6), N_EXPERTS), dtype=np.float32)
            for i, partition in enumerate(PARTITIONS_OF_6):
                for j, part in enumerate(partition):
                    if j < N_EXPERTS:
                        w[i, j] = part / N_CONST
            return jnp.asarray(w)
        key = jax.random.key(seed)
        ks = jax.random.split(key, 6)
        B, S, D, F, E, P = (32, 2048, 512, 341, 6, 11)
        scale_in = 1.0 / np.sqrt(D)
        scale_hid = 1.0 / np.sqrt(F)
        return {'x': jax.random.normal(ks[0], (B, S, D), dtype=jnp.float32), 'router_w': jax.random.normal(ks[1], (P, D), dtype=jnp.float32) * scale_in, 'W1': jax.random.normal(ks[2], (E, D, F), dtype=jnp.float32) * scale_in, 'b1': jax.random.normal(ks[3], (E, F), dtype=jnp.float32) * 0.01, 'W2': jax.random.normal(ks[4], (E, F, D), dtype=jnp.float32) * scale_hid, 'b2': jax.random.normal(ks[5], (E, D), dtype=jnp.float32) * 0.01}
    _L0_ffn_all = _L0_ffn_setup()
    _L0_ffn_in = {k: v for k, v in _L0_ffn_all.items() if k in ('router_w', 'W1', 'b1', 'W2', 'b2', )}
    del _L0_ffn_all

    return {
        "x": x,
        "L0_conv_ln_w": _L0_conv_in["ln_w"],
        "L0_conv_ln_b": _L0_conv_in["ln_b"],
        "L0_conv_in_proj_w": _L0_conv_in["in_proj_w"],
        "L0_conv_conv_w": _L0_conv_in["conv_w"],
        "L0_conv_conv_b": _L0_conv_in["conv_b"],
        "L0_conv_x_proj_w": _L0_conv_in["x_proj_w"],
        "L0_conv_dt_proj_w": _L0_conv_in["dt_proj_w"],
        "L0_conv_dt_proj_b": _L0_conv_in["dt_proj_b"],
        "L0_conv_A_log": _L0_conv_in["A_log"],
        "L0_conv_D_skip": _L0_conv_in["D_skip"],
        "L0_conv_out_proj_w": _L0_conv_in["out_proj_w"],
        "L0_ffn_router_w": _L0_ffn_in["router_w"],
        "L0_ffn_W1": _L0_ffn_in["W1"],
        "L0_ffn_b1": _L0_ffn_in["b1"],
        "L0_ffn_W2": _L0_ffn_in["W2"],
        "L0_ffn_b2": _L0_ffn_in["b2"],
    }

def reference(x, L0_conv_ln_w, L0_conv_ln_b, L0_conv_in_proj_w, L0_conv_conv_w, L0_conv_conv_b, L0_conv_x_proj_w, L0_conv_dt_proj_w, L0_conv_dt_proj_b, L0_conv_A_log, L0_conv_D_skip, L0_conv_out_proj_w, L0_ffn_router_w, L0_ffn_W1, L0_ffn_b1, L0_ffn_W2, L0_ffn_b2):
    import jax
    import jax.numpy as jnp
    def _L0_conv_ref(x, ln_w, ln_b, in_proj_w, conv_w, conv_b, x_proj_w, dt_proj_w, dt_proj_b, A_log, D_skip, out_proj_w):
        import jax, jax.numpy as jnp
        import numpy as np
        DIM = 512
        D_STATE = 16
        D_CONV = 4
        D_INNER = 1024
        DT_RANK = 32
        EPS = 1e-05

        def _selective_scan(u, delta, A, Bm, Cm, D_skip):

            def step(h, inp):
                u_t, d_t, b_t, c_t = inp
                dA = jnp.exp(d_t[..., None] * A)
                dBu = (d_t * u_t)[..., None] * b_t[:, None, :]
                h = dA * h + dBu
                y = jnp.einsum('bdn,bn->bd', h, c_t)
                return (h, y)
            B, L, d = u.shape
            h0 = jnp.zeros((B, d, A.shape[1]), u.dtype)
            xs = (u.transpose(1, 0, 2), delta.transpose(1, 0, 2), Bm.transpose(1, 0, 2), Cm.transpose(1, 0, 2))
            _, ys = jax.lax.scan(step, h0, xs)
            y = ys.transpose(1, 0, 2)
            return y + u * D_skip

        def _mamba_layer(x, ln_w, ln_b, in_proj_w, conv_w, conv_b, x_proj_w, dt_proj_w, dt_proj_b, A_log, D_skip, out_proj_w):
            B, C = x.shape[:2]
            img_dims = x.shape[2:]
            xf = x.reshape(B, C, -1).transpose(0, 2, 1)
            mu = jnp.mean(xf, -1, keepdims=True)
            var = jnp.mean(jnp.square(xf - mu), -1, keepdims=True)
            xn = (xf - mu) * jax.lax.rsqrt(var + EPS) * ln_w + ln_b
            xz = xn @ in_proj_w.T
            xin, z = jnp.split(xz, 2, axis=-1)
            xc = xin.transpose(0, 2, 1)
            w = conv_w[:, None, :]
            xc = jax.lax.conv_general_dilated(xc, w, window_strides=(1,), padding=[(D_CONV - 1, 0)], feature_group_count=D_INNER, dimension_numbers=('NCH', 'OIH', 'NCH'))
            xc = jax.nn.silu(xc + conv_b[None, :, None])
            xs = xc.transpose(0, 2, 1)
            x_dbl = xs @ x_proj_w.T
            dt = x_dbl[..., :DT_RANK]
            Bm = x_dbl[..., DT_RANK:DT_RANK + D_STATE]
            Cm = x_dbl[..., DT_RANK + D_STATE:]
            delta = jax.nn.softplus(dt @ dt_proj_w.T + dt_proj_b)
            A = -jnp.exp(A_log)
            y = _selective_scan(xs, delta, A, Bm, Cm, D_skip)
            y = y * jax.nn.silu(z)
            out = y @ out_proj_w.T
            return out.transpose(0, 2, 1).reshape(B, C, *img_dims)
        return _mamba_layer(x, ln_w, ln_b, in_proj_w, conv_w, conv_b, x_proj_w, dt_proj_w, dt_proj_b, A_log, D_skip, out_proj_w)

    def _L0_ffn_ref(x, router_w, W1, b1, W2, b2):
        import jax, jax.numpy as jnp
        import numpy as np
        N_CONST = 6
        PARTITIONS_OF_6 = [(6,), (5, 1), (4, 2), (4, 1, 1), (3, 3), (3, 2, 1), (3, 1, 1, 1), (2, 2, 2), (2, 2, 1, 1), (2, 1, 1, 1, 1), (1, 1, 1, 1, 1, 1)]
        N_EXPERTS = 6
        TOP_K = 2

        def _partition_weights():
            w = np.zeros((len(PARTITIONS_OF_6), N_EXPERTS), dtype=np.float32)
            for i, partition in enumerate(PARTITIONS_OF_6):
                for j, part in enumerate(partition):
                    if j < N_EXPERTS:
                        w[i, j] = part / N_CONST
            return jnp.asarray(w)
        pw = _partition_weights()
        token_repr = x.mean(axis=1)
        logits = token_repr @ router_w.T
        probs = jax.nn.softmax(logits, axis=-1)
        topk_vals, topk_idx = jax.lax.top_k(probs, TOP_K)
        topk_vals = topk_vals / topk_vals.sum(axis=-1, keepdims=True)
        expert_weights = jnp.einsum('bk,bke->be', topk_vals, pw[topk_idx])
        expert_weights = jnp.where(expert_weights > 1e-06, expert_weights, 0.0)
        h = jax.nn.gelu(jnp.einsum('bsd,edf->ebsf', x, W1) + b1[:, None, None, :], approximate=False)
        out_e = jnp.einsum('ebsf,efd->ebsd', h, W2) + b2[:, None, None, :]
        return jnp.einsum('be,ebsd->bsd', expert_weights, out_e)

    def _gn(v, G=32, eps=1e-5):
        B_, C_, H_, W_ = v.shape
        g = v.reshape(B_, G, C_ // G, H_, W_)
        m = jnp.mean(g, axis=(2, 3, 4), keepdims=True)
        s = jnp.var(g, axis=(2, 3, 4), keepdims=True)
        return ((g - m) / jnp.sqrt(s + eps)).reshape(v.shape)

    def _ln_c(v, eps=1e-6):
        m = jnp.mean(v, axis=1, keepdims=True)
        s = jnp.var(v, axis=1, keepdims=True)
        return (v - m) / jnp.sqrt(s + eps)

    def _ln_t(v, eps=1e-5):
        m = jnp.mean(v, axis=-1, keepdims=True)
        s = jnp.var(v, axis=-1, keepdims=True)
        return (v - m) / jnp.sqrt(s + eps)

    def _to_tokens(v):
        B_, C_, H_, W_ = v.shape
        return v.reshape(B_, C_, H_ * W_).transpose(0, 2, 1)
    def _from_tokens(t, like):
        B_, C_, H_, W_ = like.shape
        return t.transpose(0, 2, 1).reshape(B_, C_, H_, W_)

    x = x + _L0_conv_ref(_ln_c(x), L0_conv_ln_w, L0_conv_ln_b, L0_conv_in_proj_w, L0_conv_conv_w, L0_conv_conv_b, L0_conv_x_proj_w, L0_conv_dt_proj_w, L0_conv_dt_proj_b, L0_conv_A_log, L0_conv_D_skip, L0_conv_out_proj_w)
    t = _to_tokens(x)
    t = t + _L0_ffn_ref(_ln_t(t), L0_ffn_router_w, L0_ffn_W1, L0_ffn_b1, L0_ffn_W2, L0_ffn_b2)
    x = _from_tokens(t, x)
    return x


_drawn_inputs = setup_inputs


def setup_inputs(seed=0):
    import zlib

    import numpy as np

    out = dict(_drawn_inputs(seed))
    spreads = {'L0_conv_ln_w': (1.0, 0.6),
     'L0_conv_ln_b': (0.0, 0.8),
     'L0_conv_conv_b': (0.0, 0.8),
     'L0_conv_dt_proj_b': (-4.0, 0.6),
     'L0_conv_D_skip': (1.0, 0.6)}
    factors = {'L0_conv_conv_w': 2.72,
     'L0_conv_x_proj_w': 8.0,
     'L0_conv_dt_proj_w': 8.0,
     'L0_conv_A_log': 8.0,
     'L0_ffn_b1': 64.0,
     'L0_ffn_b2': 64.0,
     'L0_ffn_router_w': 8.0,
     'L0_ffn_W1': 8.0,
     'L0_ffn_W2': 8.0}
    for name, (base, spread) in spreads.items():
        noise = np.random.default_rng([zlib.crc32(name.encode()), seed]).standard_normal(out[name].shape)
        drawn = base * np.exp(spread * noise) if base else spread * noise
        out[name] = jnp.asarray(drawn.astype(out[name].dtype))
    for name, factor in factors.items():
        out[name] = (out[name] * factor).astype(out[name].dtype)
    return out
```

```python
from contextlib import ExitStack

import numpy as np

import concourse.bass as bass
from concourse import mybir

P = 128
BATCH, DIM, TOKENS = 2, 512, 4096
INNER, STATES, TAPS, RANK = 1024, 16, 4, 32
EXPERTS, HIDDEN, PARTS = 6, 341, 11
KT = DIM // P
DT = INNER // P
HT = DT // 2
T = 256
TS = T // P
CPB = TOKENS // T
CHUNKS = BATCH * CPB
UNITS = 2 * STATES
XR = 96
ONE_ROW, C_ROW, B_ROW = 32, 64, 80
SEG = T + 1
HS = 4
BP = 4
TF = 512
FCPB = TOKENS // TF
FT = 16
FPAD = FT * P

F32 = mybir.dt.float32
F32R = mybir.dt.float32r
ACT = mybir.ActivationFunctionType
ALU = mybir.AluOpType
AX_X = mybir.AxisListType.X

V_LNW, V_LNB, V_CW, V_CB, V_D, V_AL, V_XB = 0, 4, 8, 40, 48, 56, 184
V_COLS = 185


HALF_ROOT = 0.5 ** 0.5


def ge(eng, sem, value):
    if isinstance(value, int) and value <= 0:
        return
    eng.wait_ge(sem, value)


def build_mixer(nc, x, vecs, ident_in, mean_in, wi_in, wo_in, wx_in, wdt_in, tsum, b_scr, x2_scr, tn_scr):
    with ExitStack() as ctx:
        def sb(name, shape, dt=F32):
            return ctx.enter_context(nc.sbuf_tensor(name, shape, dt))

        def sem(name):
            return ctx.enter_context(nc.semaphore(name))

        w_in = sb("w_in", [P, KT, 2 * INNER])
        w_out = sb("w_out", [P, DT, DIM])
        w_x = sb("w_x", [P, DT, XR])
        w_dt = sb("w_dt", [RANK + 1, INNER])
        vec = sb("vec", [P, V_COLS])
        ident = sb("ident", [P, P])
        mean_w = sb("mean_w", [P, P])
        neg_a = sb("neg_a", [P, DT, STATES])
        eps = sb("eps", [P, 2])
        x_t = sb("x_t", [P, KT, T])
        xn = sb("xn", [P, KT, T])
        sq = sb("sq", [P, KT, T])
        ln_l = sb("ln_l", [P, T])
        ln_r1 = sb("ln_r1", [P, T])
        ln_r2 = sb("ln_r2", [P, T])
        ln_v = sb("ln_v", [P, T])
        xin = sb("xin", [P, DT, TAPS - 1 + T])
        u = sb("u", [P, 2, DT, T])
        zs = sb("zs", [P, 2, DT, T])
        xd = sb("xd", [XR, 2, T])
        sp_t = sb("sp_t", [P, 2, 2 * T])
        sp_l = sb("sp_l", [P, 2, 2 * T])
        sp_w = sb("sp_w", [P, 2, 2 * T])
        sp_q = sb("sp_q", [P, 2, 2 * T])
        delta = sb("delta", [P, 2, HT, T])
        du = sb("du", [P, 2, HT, T])
        b_rep = sb("b_rep", [P, BP, 2, T])
        c_tok = sb("c_tok", [P, 2, TS, STATES])
        da = sb("da", [P, 2, HT, SEG])
        dbh = sb("dbh", [P, HS, HT, SEG])
        state = sb("state", [P, 2, STATES, HT])
        y_t = sb("y_t", [P, 2, TS, HT * P])
        x2 = sb("x2", [P, KT, T])
        d2 = sb("d2", [P, KT, T])
        sq2 = sb("sq2", [P, KT, T])
        ln2_l = sb("ln2_l", [P, T])
        ln2_r = sb("ln2_r", [P, T])
        t_red = sb("t_red", [P, KT])

        h_tok = ctx.enter_context(nc.psum_tensor("h_tok", [P, 4, HT * P], F32))
        pre = ctx.enter_context(nc.psum_tensor("pre", [P, 2, 2 * T], F32))
        fin = ctx.enter_context(nc.psum_tensor("fin", [P, 2, 2 * T], F32))

        consts_in, wi_sem, wrest_in = sem("consts_in"), sem("wi_sem"), sem("wrest_in")
        set_dve, set_act = sem("set_dve"), sem("set_act")
        x_in, xres_in, stored = sem("x_in"), sem("xres_in"), sem("stored")
        b_stored = sem("b_stored")
        b_in = [sem(f"b_in{i}") for i in range(BP)]
        pre_mm, fin_mm = sem("pre_mm"), sem("fin_mm")
        pre_read = [sem(f"pre_read{i}") for i in range(2)]
        fin_read = [sem(f"fin_read{i}") for i in range(2)]
        squared, rstd_act, rstd_dve, xn_ready = sem("squared"), sem("rstd_act"), sem("rstd_dve"), sem("xn_ready")
        tail_kept, conv_step, u_ready = sem("tail_kept"), sem("conv_step"), sem("u_ready")
        soft_act, soft_dve, soft_pool, delta_ready = (
            sem("soft_act"), sem("soft_dve"), sem("soft_pool"), sem("delta_ready"))
        z_ready, du_ready = sem("z_ready"), sem("du_ready")
        da_ready, db_ready, h_ready, h_turned, y_added, state_saved = (
            sem("da_ready"), sem("db_ready"), sem("h_ready"), sem("h_turned"), sem("y_added"), sem("state_saved"))
        y_gated, squared2, ln2_ready, tok_step = sem("y_gated"), sem("squared2"), sem("ln2_ready"), sem("tok_step")

        def pre_bank_read(c, j):
            return pre_read[j % 2], c * 8 + j // 2 + 1

        def fin_bank_read(c, j):
            return fin_read[j % 2], c * 4 + j // 2 + 1

        def iterations(eng, body):
            body(0, 0, True, True, True, False)
            body(1, 1, False, True, True, True)
            with eng.Fori(0, CPB // 2 - 2) as i:
                body(i * 2 + 2, 0, False, True, True, True)
                body(i * 2 + 3, 1, False, True, True, True)
            body(CPB - 2, 0, False, True, True, True)
            body(CPB - 1, 1, False, True, True, True, turn=True)
            body(CPB, 0, True, True, True, True)
            with eng.Fori(0, CPB // 2 - 1) as i:
                body(i * 2 + CPB + 1, 1, False, True, True, True, image=1)
                body(i * 2 + CPB + 2, 0, False, True, True, True, image=1)
            body(CHUNKS - 1, 1, False, True, False, True, image=1)
            body(CHUNKS, 0, False, False, False, True, image=1)

        block = ctx.enter_context(nc.Block())

        @block.sync
        def _(sp):
            sp.dma_start(vec[:, :], vecs).then_inc(consts_in, 16)
            sp.dma_start(mean_w[:, :], mean_in).then_inc(consts_in, 16)
            sp.dma_start(ident[:, :], ident_in).then_inc(consts_in, 16)

            def chunk_of(dram, b, c):
                t0 = (c - b * CPB) * T
                if isinstance(c, int):
                    return dram[b].rearrange("(k p) t -> p k t", p=P)[:, :, t0:t0 + T]
                return dram[b].rearrange("(k p) t -> p k t", p=P)[:, :, bass.ds(t0, T)]

            def load_x(b, c):
                s, count = pre_bank_read(c - 1, 0)
                ge(sp, s, count if not isinstance(c, int) or c else 0)
                sp.dma_start(x_t[:, :, :], chunk_of(x, b, c)).then_inc(x_in, 16)

            def load_residual(b, c):
                ge(sp, stored, c * 32)
                sp.dma_start(x2[:, :, :], chunk_of(x, b, c)).then_inc(xres_in, 16)

            def store(b, c):
                sp.wait_ge(tok_step, c * 3 + 1)
                sp.dma_start(chunk_of(x2_scr, b, c), x2[:, :, :]).then_inc(stored, 16)
                sp.dma_start(chunk_of(tn_scr, b, c), d2[:, :, :]).then_inc(stored, 16)

            def b_rows(c):
                return b_scr[c] if isinstance(c, int) else b_scr[bass.ds(c, 1)].rearrange("a n t -> (a n) t")

            def store_b(c, parity):
                sp.wait_ge(*pre_bank_read(c, 8))
                sp.dma_start(b_rows(c), xd[B_ROW:B_ROW + STATES, parity, :]).then_inc(b_stored, 16)

            def load_b_piece(c, p):
                if p == 0:
                    sp.wait_ge(b_stored, (c + 1) * 16)
                else:
                    ge(sp, db_ready, c * UNITS + 2 * p - (4 if p == UNITS // 2 - 1 else 6))
                n = 2 * p % STATES
                rows = b_rows(c)[n:n + 2, :]
                src = bass.AP(tensor=rows.tensor, offset=rows.offset, ap=[[0, P]] + list(rows.ap))
                sp.dma_start(b_rep[:, p % BP], src).then_inc(b_in[p % BP], 16)

            load_x(0, 0)
            sp.dma_start(w_in[:, :, :], wi_in).then_inc(wi_sem, 16)
            sp.dma_start(w_x[:, :, :], wx_in).then_inc(wrest_in, 16)
            sp.dma_start(w_dt[:, :], wdt_in).then_inc(wrest_in, 16)
            sp.dma_start(w_out[:, :, :], wo_in).then_inc(wrest_in, 16)
            store_b(0, 0)

            def body(k, parity, first, scan, prepare, finish, image=0, turn=False):
                fb = image if not isinstance(k, int) else (k - 1) // CPB
                pb = image if not isinstance(k, int) else (k + 1) // CPB
                if prepare:
                    load_x(pb, k + 1)
                if finish:
                    load_residual(fb, k - 1)
                for p in range(UNITS // 2):
                    if scan:
                        load_b_piece(k, p)
                    if p == 11 and finish:
                        store(fb, k - 1)
                if prepare:
                    store_b(k + 1, 1 - parity)

            iterations(sp, body)
            sp.wait_ge(stored, CHUNKS * 32)

        @block.gpsimd
        def _(pool):
            def soften(c, q):
                half, pair = q // 2, q % 2
                d = delta[:, half, 2 * pair:2 * pair + 2, :].rearrange("p a t -> p (a t)")
                l = sp_l[:, q % 2, :]
                pool.wait_ge(soft_dve, (c * 4 + q) * 2 + 2)
                pool.tensor_tensor(d, d, l, ALU.subtract).then_inc(delta_ready, 1)

            def make_du(c, parity, half):
                ge(pool, db_ready, (c - 1) * UNITS + STATES * (half + 1))
                pool.wait_ge(delta_ready, c * 4 + 2 * half + 2)
                pool.wait_ge(u_ready, c + 1)
                pool.tensor_tensor(du[:, half], delta[:, half], u[:, parity, HT * half:HT * half + HT, :],
                                   ALU.mult).then_inc(du_ready, 1)

            def inject(k, unit, first):
                half, n = unit // STATES, unit % STATES
                g = k * UNITS + unit
                slot = dbh[:, unit % HS]
                ge(pool, h_turned, g * 2 - 6)
                ge(pool, state_saved, g - 3)
                if n == 0:
                    pool.wait_ge(du_ready, k * 2 + half + 1)
                if n % 2 == 0:
                    pool.wait_ge(b_in[(unit // 2) % BP], (k * (UNITS // 2 // BP) + unit // 2 // BP + 1) * 16)
                rep = b_rep[:, (unit // 2) % BP, n % 2:n % 2 + 1, :].broadcast_to((P, HT, T))
                pool.tensor_tensor(slot[:, :, 1:SEG], du[:, half], rep, ALU.mult)
                if first:
                    pool.memset(slot[:, :, 0:1], 0.0).then_inc(db_ready, 1)
                else:
                    pool.tensor_copy(slot[:, :, 0:1], state[:, half, n, :].rearrange("p (a b) -> p a b", b=1))\
                        .then_inc(db_ready, 1)

            def gate(c, parity, j):
                pool.wait_ge(*fin_bank_read(c, j))
                if j == 0:
                    pool.wait_ge(z_ready, c + 1)
                y = u[:, parity, 2 * j:2 * j + 2, :]
                pool.tensor_tensor(y, y, zs[:, parity, 2 * j:2 * j + 2, :], ALU.mult).then_inc(y_gated, 1)

            soften(0, 0)
            soften(0, 1)

            def body(k, parity, first, scan, prepare, finish, image=0, turn=False):
                if scan:
                    make_du(k, parity, 0)
                for unit in range(UNITS):
                    if scan:
                        inject(k, unit, first)
                        if unit in (2, 3):
                            soften(k, unit)
                        if unit == 5:
                            make_du(k, parity, 1)
                        if unit in (19, 20):
                            gate(k, parity, unit - 19)
                    if finish and unit in (3, 4):
                        gate(k - 1, 1 - parity, unit - 1)
                    if prepare and unit in (29, 30):
                        soften(k + 1, unit - 29)

            iterations(pool, body)

        @block.tensor
        def _(pe):
            def pre_bank(c, j):
                s, count = pre_bank_read(c, j)
                ge(pe, s, count - 1)
                return pre[:, j % 2, :]

            def fin_bank(c, j):
                s, count = fin_bank_read(c, j)
                ge(pe, s, count - 1)
                return fin[:, j % 2, :]

            def token_mean(bank, src, signal):
                for kt in range(KT):
                    mm = pe.matmul(bank[:, 0:T], mean_w[:, :], src[:, kt, :], start=kt == 0, stop=kt == KT - 1)
                mm.then_inc(signal, 1)

            def mean1(c):
                pe.wait_ge(x_in, (c + 1) * 16)
                token_mean(pre_bank(c, 0), x_t, pre_mm)

            def var1(c):
                bank = pre_bank(c, 1)
                pe.wait_ge(squared, c + 1)
                token_mean(bank, sq, pre_mm)

            def in_tile(c, j, m, tile):
                if tile == 0:
                    bank = pre_bank(c, j)
                else:
                    bank = pre[:, j % 2, :]
                pe.wait_ge(xn_ready, c + 1)
                for kt in range(KT):
                    mm = pe.matmul(bank[:, tile * T:tile * T + T], w_in[:, kt, m * P:m * P + P], xn[:, kt, :],
                                   start=kt == 0, stop=kt == KT - 1)
                if tile == 1:
                    mm.then_inc(pre_mm, 1)

            def x_proj(c, parity):
                bank = pre_bank(c, 8)
                pe.wait_ge(u_ready, c + 1)
                for d in range(DT):
                    mm = pe.matmul(bank[0:XR, 0:T], w_x[:, d, :], u[:, parity, d, :], start=d == 0, stop=d == DT - 1)
                mm.then_inc(pre_mm, 1)

            def turn_c(c, parity):
                bank = pre_bank(c, 9)
                pe.wait_ge(*pre_bank_read(c, 8))
                for ts in range(TS):
                    mm = pe.transpose(bank[:, ts * XR:ts * XR + XR], xd[:, parity, ts * P:ts * P + P],
                                      ident[0:XR, 0:XR])
                mm.then_inc(pre_mm, 1)

            def dt_pair(c, parity, q):
                bank = pre_bank(c, 10 + q if q < 2 else 12 + q)
                pe.wait_ge(*pre_bank_read(c, 8))
                for tile in range(2):
                    m = 2 * q + tile
                    mm = pe.matmul(bank[:, tile * T:tile * T + T], w_dt[:, m * P:m * P + P],
                                   xd[0:RANK + 1, parity, :], start=True, stop=True)
                mm.then_inc(pre_mm, 1)

            def turn_h(k, unit):
                g = k * UNITS + unit
                pe.wait_ge(h_ready, g + 1)
                for ts in range(TS):
                    ge(pe, y_added, g * 2 + ts - 3)
                    for d in range(HT):
                        mm = pe.transpose(h_tok[:, (2 * unit + ts) % 4, d * P:d * P + P],
                                          dbh[:, unit % HS, d, 1 + ts * P:1 + ts * P + P], ident[:, :])
                    mm.then_inc(h_turned, 1)

            def turn_back(c, j):
                half, pair = j // 2, j % 2
                bank = fin_bank(c, j)
                pe.wait_ge(y_added, (c * UNITS + STATES * (half + 1)) * 2)
                for d in range(2):
                    for ts in range(TS):
                        mm = pe.transpose(bank[:, d * T + ts * P:d * T + ts * P + P],
                                          y_t[:, half, ts, (2 * pair + d) * P:(2 * pair + d + 1) * P], ident[:, :])
                mm.then_inc(fin_mm, 1)

            def out_tile(c, parity, m):
                j = 4 + m // 2
                bank = fin_bank(c, j) if m % 2 == 0 else fin[:, j % 2, :]
                pe.wait_ge(y_gated, c * 4 + 4)
                for d in range(DT):
                    mm = pe.matmul(bank[:, (m % 2) * T:(m % 2) * T + T], w_out[:, d, m * P:m * P + P],
                                   u[:, parity, d, :], start=d == 0, stop=d == DT - 1)
                if m % 2 == 1:
                    mm.then_inc(fin_mm, 1)

            def mean2(c):
                bank = fin_bank(c, 6)
                pe.wait_ge(*fin_bank_read(c, 4))
                pe.wait_ge(*fin_bank_read(c, 5))
                token_mean(bank, x2, fin_mm)

            def var2(c):
                bank = fin_bank(c, 7)
                pe.wait_ge(squared2, c + 1)
                token_mean(bank, sq2, fin_mm)

            pe.wait_ge(consts_in, 48)
            mean1(0)
            var1(0)
            pe.wait_ge(wi_sem, 16)
            for m in range(8):
                in_tile(0, 2 + m // 2, m, m % 2)
            for m in range(8, 12):
                in_tile(0, 2 + m // 2, m, m % 2)
            pe.wait_ge(wrest_in, 48)
            x_proj(0, 0)
            turn_c(0, 0)
            dt_pair(0, 0, 0)
            dt_pair(0, 0, 1)
            for m in range(12, 16):
                in_tile(0, 6 + m // 2, m, m % 2)

            def body(k, parity, first, scan, prepare, finish, image=0, turn=False):
                for unit in range(UNITS):
                    if scan:
                        turn_h(k, unit)
                        if unit in (0, 1):
                            dt_pair(k, parity, 2 + unit)
                        if unit in (17, 18):
                            turn_back(k, unit - 17)
                    if finish:
                        if unit in (1, 2):
                            turn_back(k - 1, unit + 1)
                        if unit in (4, 5, 6, 7):
                            out_tile(k - 1, 1 - parity, unit - 4)
                        if unit == 8:
                            mean2(k - 1)
                        if unit == 10:
                            var2(k - 1)
                    if prepare:
                        if unit == 9:
                            mean1(k + 1)
                        if unit == 11:
                            var1(k + 1)
                        if 15 <= unit < 23:
                            in_tile(k + 1, 2 + (unit - 15) // 2, unit - 15, (unit - 15) % 2)
                        if unit in (23, 24):
                            for m in (2 * unit - 38, 2 * unit - 37):
                                in_tile(k + 1, 2 + m // 2, m, m % 2)
                        if unit == 25:
                            x_proj(k + 1, 1 - parity)
                        if unit == 26:
                            turn_c(k + 1, 1 - parity)
                        if unit in (26, 27):
                            dt_pair(k + 1, 1 - parity, unit - 26)
                        if unit >= 28:
                            m = unit - 16
                            in_tile(k + 1, 6 + m // 2, m, m % 2)

            iterations(pe, body)

        @block.scalar
        def _(act):
            act.wait_ge(consts_in, 48)
            act.preload_act_table_set("natural_log_exp_and_others")
            act.activation(neg_a[:, :, :], vec[:, V_AL:V_AL + DT * STATES].rearrange("p (d n) -> p d n", d=DT),
                           ACT.Exp).then_inc(set_act, 1)
            act.wait_ge(set_act, 1)
            act.activation(neg_a[:, :, :], neg_a[:, :, :], ACT.Copy, scale=-1.0).then_inc(set_act, 1)
            act.wait_ge(set_act, 2)
            act.wait_ge(set_dve, 6)

            def square1(c):
                act.wait_ge(*pre_bank_read(c, 0))
                act.activation(sq[:, :, :], xn[:, :, :], ACT.Square).then_inc(squared, 1)

            def rstd1(c):
                act.wait_ge(pre_mm, c * 16 + 2)
                act.activation(ln_l[:, :], pre[:, 1, 0:T], ACT.Ln, bias=eps[:, 0:1]).then_inc(rstd_act, 1)
                act.wait_ge(rstd_act, c * 4 + 1)
                act.activation(ln_r1[:, :], ln_l[:, :], ACT.Exp, scale=-0.5).then_inc(rstd_act, 1)

            def rstd1_again(c):
                act.wait_ge(rstd_dve, c * 3 + 1)
                act.activation(ln_l[:, :], ln_v[:, :], ACT.Ln, bias=eps[:, 1:2]).then_inc(rstd_act, 1)
                act.wait_ge(rstd_act, c * 4 + 3)
                act.activation(ln_r2[:, :], ln_l[:, :], ACT.Exp, scale=-0.5).then_inc(rstd_act, 1)

            def affine(c):
                act.wait_ge(rstd_dve, c * 3 + 3)
                for kt in range(KT):
                    last = act.activation(xn[:, kt, :], xn[:, kt, :], ACT.Identity,
                                          bias=vec[:, V_LNB + kt:V_LNB + kt + 1],
                                          scale=vec[:, V_LNW + kt:V_LNW + kt + 1])
                last.then_inc(xn_ready, 1)

            def take_xin(c, q):
                act.wait_ge(tail_kept, c + 1)
                act.wait_ge(pre_mm, c * 16 + 3 + q)
                act.activation(xin[:, 2 * q:2 * q + 2, TAPS - 1:TAPS - 1 + T],
                               pre[:, q % 2, :].rearrange("p (a t) -> p a t", a=2), ACT.Copy).then_inc(pre_read[q % 2], 1)

            def silu_u(c, parity):
                act.wait_ge(conv_step, (c + 1) * 32)
                act.activation(u[:, parity], u[:, parity], ACT.Silu).then_inc(u_ready, 1)

            def take_z(c, parity, q):
                ge(act, y_gated, (c - 1) * 4)
                j = 6 + q if q < 2 else 10 + q
                act.wait_ge(pre_mm, c * 16 + j + 1)
                act.activation(zs[:, parity, 2 * q:2 * q + 2, :],
                               pre[:, j % 2, :].rearrange("p (a t) -> p a t", a=2),
                               ACT.Copy).then_inc(pre_read[j % 2], 1)

            def silu_z(c, parity):
                act.wait_ge(*pre_bank_read(c, 12))
                act.wait_ge(*pre_bank_read(c, 13))
                act.activation(zs[:, parity], zs[:, parity], ACT.Silu).then_inc(z_ready, 1)
                act.preload_act_table_set("natural_log_exp_and_others")

            def take_xd(c, parity):
                ge(act, b_stored, (c - 1) * 16)
                act.wait_ge(pre_mm, c * 16 + 9)
                act.activation(xd[:, parity, :], pre[0:XR, 0, 0:T], ACT.Identity,
                               bias=vec[0:XR, V_XB:V_XB + 1]).then_inc(pre_read[0], 1)

            def take_c(c, parity):
                ge(act, y_added, (c - 1) * UNITS * 2)
                act.wait_ge(pre_mm, c * 16 + 10)
                src = pre[:, 1, 0:TS * XR].rearrange("p (s r) -> p s r", s=TS)[:, :, C_ROW:C_ROW + STATES]
                act.activation(c_tok[:, parity], src, ACT.Copy).then_inc(pre_read[1], 1)

            def soft(c, q):
                t, l, w = sp_t[:, q % 2, :], sp_l[:, q % 2, :], sp_w[:, q % 2, :]
                j = 10 + q if q < 2 else 12 + q
                count, bank = c * 16 + j + 1, j % 2
                steps = (c * 4 + q) * 5
                ge(act, delta_ready, c * 4 + q - 1)
                act.wait_ge(pre_mm, count)
                act.activation(t, pre[:, bank, :], ACT.Abs).then_inc(soft_act, 1)
                act.wait_ge(soft_act, steps + 1)
                act.activation(t, t, ACT.Exp, scale=-1.0).then_inc(soft_act, 1)
                act.wait_ge(soft_act, steps + 2)
                act.activation(w, t, ACT.Identity, bias=1.0).then_inc(soft_act, 1)
                act.activation(sp_q[:, q % 2, :], t, ACT.Square, scale=HALF_ROOT).then_inc(soft_act, 1)
                act.wait_ge(soft_act, steps + 3)
                act.activation(l, w, ACT.Ln).then_inc(soft_act, 1)

            def decay(k, unit):
                half, n = unit // STATES, unit % STATES
                g = k * UNITS + unit
                ge(act, h_ready, g - 1)
                if n == 0:
                    act.wait_ge(delta_ready, k * 4 + 2 * half + 2)
                for d in range(HT):
                    last = act.activation(da[:, unit % 2, d, 1:SEG], delta[:, half, d, :], ACT.Exp,
                                          scale=neg_a[:, HT * half + d, n:n + 1])
                last.then_inc(da_ready, 1)

            def save_state(unit):
                half, n = unit // STATES, unit % STATES
                act.activation(state[:, half, n, :].rearrange("p (a b) -> p a b", b=1),
                               dbh[:, unit % HS, :, T:T + 1], ACT.Copy).then_inc(state_saved, 1)

            def square2(c):
                act.wait_ge(*fin_bank_read(c, 6))
                act.activation(sq2[:, :, :], d2[:, :, :], ACT.Square).then_inc(squared2, 1)

            def rstd2(c):
                act.wait_ge(fin_mm, c * 8 + 8)
                act.activation(ln2_l[:, :], fin[:, 1, 0:T], ACT.Ln, bias=eps[:, 1:2]).then_inc(fin_read[1], 1)
                act.wait_ge(*fin_bank_read(c, 7))
                act.activation(ln2_r[:, :], ln2_l[:, :], ACT.Exp, scale=-0.5).then_inc(ln2_ready, 1)

            square1(0)
            rstd1(0)
            rstd1_again(0)
            affine(0)
            for q in range(4):
                take_xin(0, q)
            for q in range(2):
                take_z(0, 0, q)
            silu_u(0, 0)
            take_xd(0, 0)
            take_c(0, 0)
            act.preload_act_table_set("natural_log_exp_and_others")
            soft(0, 0)
            soft(0, 1)
            for q in range(2, 4):
                take_z(0, 0, q)

            def body(k, parity, first, scan, prepare, finish, image=0, turn=False):
                for unit in range(UNITS):
                    if scan:
                        decay(k, unit)
                        if unit >= 2:
                            save_state(unit - 2)
                        elif not (isinstance(k, int) and k == 0):
                            save_state(unit + UNITS - 2)
                        if unit in (0, 1):
                            soft(k, 2 + unit)
                        if unit == 2:
                            silu_z(k, parity)
                    if finish:
                        if unit == 9:
                            square2(k - 1)
                        if unit == 11:
                            rstd2(k - 1)
                    if prepare:
                        if unit == 10:
                            square1(k + 1)
                        if unit == 12:
                            rstd1(k + 1)
                        if unit == 13:
                            rstd1_again(k + 1)
                        if unit == 14:
                            affine(k + 1)
                        if unit in (17, 19, 21, 23):
                            take_xin(k + 1, (unit - 17) // 2)
                        if unit in (24, 25):
                            take_z(k + 1, 1 - parity, unit - 24)
                        if unit == 25:
                            silu_u(k + 1, 1 - parity)
                            act.preload_act_table_set("natural_log_exp_and_others")
                        if unit == 26:
                            take_xd(k + 1, 1 - parity)
                        if unit == 27:
                            take_c(k + 1, 1 - parity)
                        if unit in (27, 28):
                            soft(k + 1, unit - 27)
                        if unit in (30, 31):
                            take_z(k + 1, 1 - parity, unit - 28)

            iterations(act, body)

        @block.vector
        def _(dve):
            for i, (dst, value) in enumerate(((eps[:, 0:1], 1e-6), (eps[:, 1:2], 1e-5), (tsum[:, :, :], 0.0),
                                              (da[:, 0, :, 0:1], 0.0), (da[:, 1, :, 0:1], 0.0))):
                dve.memset(dst, value).then_inc(set_dve, 1)
            dve.wait_ge(set_dve, 5)
            dve.memset(t_red[:, :], 0.0).then_inc(set_dve, 1)
            dve.wait_ge(consts_in, 48)

            def centre1(c):
                ge(dve, pre_mm, (c - 1) * 16 + 14)
                dve.wait_ge(pre_mm, c * 16 + 1)
                dve.tensor_tensor(xn[:, :, :], x_t[:, :, :], pre[:, 0:1, 0:T].broadcast_to((P, KT, T)),
                                  ALU.subtract).then_inc(pre_read[0], 1)

            def var_of_normed(c):
                dve.wait_ge(rstd_act, c * 4 + 2)
                dve.tensor_tensor(ln_v[:, :], pre[:, 1, 0:T], ln_r1[:, :], ALU.mult).then_inc(pre_read[1], 1)
                dve.wait_ge(*pre_bank_read(c, 1))
                dve.tensor_tensor(ln_v[:, :], ln_v[:, :], ln_r1[:, :], ALU.mult).then_inc(rstd_dve, 1)

            def scale1(c):
                dve.wait_ge(rstd_act, c * 4 + 4)
                dve.tensor_tensor(ln_r2[:, :], ln_r2[:, :], ln_r1[:, :], ALU.mult).then_inc(rstd_dve, 1)
                dve.wait_ge(rstd_dve, c * 3 + 2)        
                dve.tensor_tensor(xn[:, :, :], xn[:, :, :],
                                  ln_r2[:, :].rearrange("p (a t) -> p a t", a=1).broadcast_to((P, KT, T)),
                                  ALU.mult).then_inc(rstd_dve, 1)

            def keep_tail(c, first):
                ge(dve, conv_step, c * 32)
                if first:
                    dve.memset(xin[:, :, 0:TAPS - 1], 0.0).then_inc(tail_kept, 1)
                else:
                    dve.tensor_copy(xin[:, :, 0:TAPS - 1], xin[:, :, T:T + TAPS - 1]).then_inc(tail_kept, 1)

            def conv(c, parity, q):
                dve.wait_ge(*pre_bank_read(c, 2 + q))
                if q == 0:
                    dve.wait_ge(tail_kept, c + 1)
                    ge(dve, fin_mm, (c - 2) * 8 + 6)
                for j in range(TAPS):
                    for tile in range(2):
                        d = 2 * q + tile
                        acc = u[:, parity, d, :]
                        w = vec[:, V_CW + d * TAPS + j:V_CW + d * TAPS + j + 1]
                        if j == 0:
                            dve.tensor_scalar(acc, xin[:, d, j:j + T], w, vec[:, V_CB + d:V_CB + d + 1],
                                              ALU.mult, ALU.add).then_inc(conv_step, 1)
                        else:
                            dve.wait_ge(conv_step, c * 32 + q * 8 + 2 * j - 1 + tile)
                            dve.scalar_tensor_tensor(acc, xin[:, d, j:j + T], w, acc, ALU.mult,
                                                     ALU.add).then_inc(conv_step, 1)

            def soften(c, q):
                half, pair = q // 2, q % 2
                bank = q % 2
                dve.wait_ge(soft_act, (c * 4 + q) * 5 + 5)
                dve.scalar_tensor_tensor(delta[:, half, 2 * pair:2 * pair + 2, :].rearrange("p a t -> p (a t)"),
                                         pre[:, bank, :], 0.0, sp_t[:, q % 2, :], ALU.max,
                                         ALU.add).then_inc(pre_read[bank], 1)
                l = sp_l[:, q % 2, :]
                dve.scalar_tensor_tensor(l, sp_w[:, q % 2, :], -1.0, l, ALU.add, ALU.subtract).then_inc(soft_dve, 1)
                dve.wait_ge(soft_dve, (c * 4 + q) * 2 + 1)
                dve.scalar_tensor_tensor(l, l, 0.0, sp_q[:, q % 2, :], ALU.max, ALU.min).then_inc(soft_dve, 1)

            def scan(k, unit):
                g = k * UNITS + unit
                h = dbh[:, unit % HS].rearrange("p a t -> p (a t)")
                dve.wait_ge(da_ready, g + 1)
                dve.wait_ge(db_ready, g + 1)
                dve.tensor_tensor_scan(h, da[:, unit % 2].rearrange("p a t -> p (a t)"), h, 0.0, ALU.mult,
                                       ALU.add).then_inc(h_ready, 1)

            def add_y(k, unit, parity):
                half, n = unit // STATES, unit % STATES
                g = k * UNITS + unit
                if unit == 0:
                    dve.wait_ge(*pre_bank_read(k, 9))
                for ts in range(TS):
                    dve.wait_ge(h_turned, g * 2 + ts + 1)
                    src, acc, cn = h_tok[:, (2 * unit + ts) % 4, :], y_t[:, half, ts, :], c_tok[:, parity, ts, n:n + 1]
                    if n == 0:
                        if ts == 0:
                            ge(dve, fin_mm, (k - 1) * 8 + 2 * half + 2)
                        dve.tensor_scalar(acc, src, cn, None, ALU.mult).then_inc(y_added, 1)
                    else:
                        dve.wait_ge(y_added, g * 2 + ts - 1)
                        dve.scalar_tensor_tensor(acc, src, cn, acc, ALU.mult, ALU.add).then_inc(y_added, 1)

            def skip(c, parity, j):
                dve.wait_ge(fin_mm, c * 8 + j + 1)
                for tile in range(2):
                    d = 2 * j + tile
                    y = u[:, parity, d, :]
                    last = dve.scalar_tensor_tensor(y, y, vec[:, V_D + d:V_D + d + 1],
                                                    fin[:, j % 2, tile * T:tile * T + T], ALU.mult, ALU.add)
                last.then_inc(fin_read[j % 2], 1)

            def residual(c, j):
                dve.wait_ge(xres_in, (c + 1) * 16)
                dve.wait_ge(fin_mm, c * 8 + j + 1)
                xr = x2[:, 2 * (j - 4):2 * (j - 4) + 2, :].rearrange("p a t -> p (a t)")
                dve.tensor_tensor(xr, xr, fin[:, j % 2, :], ALU.add).then_inc(fin_read[j % 2], 1)

            def centre2(c):
                dve.wait_ge(fin_mm, c * 8 + 7)
                dve.wait_ge(*fin_bank_read(c, 4))
                dve.wait_ge(*fin_bank_read(c, 5))
                dve.tensor_tensor(d2[:, :, :], x2[:, :, :], fin[:, 0:1, 0:T].broadcast_to((P, KT, T)),
                                  ALU.subtract).then_inc(fin_read[0], 1)

            def scale2(c):
                dve.wait_ge(ln2_ready, c + 1)
                dve.tensor_tensor(d2[:, :, :], d2[:, :, :],
                                  ln2_r[:, :].rearrange("p (a t) -> p a t", a=1).broadcast_to((P, KT, T)),
                                  ALU.mult).then_inc(tok_step, 1)

            def sum_tokens(c, b):
                dve.wait_ge(tok_step, c * 3 + 1)
                dve.tensor_reduce(t_red[:, :], d2[:, :, :], AX_X, ALU.add).then_inc(tok_step, 1)
                dve.wait_ge(tok_step, c * 3 + 2)
                dve.tensor_tensor(tsum[:, :, b], tsum[:, :, b], t_red[:, :], ALU.add).then_inc(tok_step, 1)

            centre1(0)
            var_of_normed(0)
            scale1(0)
            keep_tail(0, True)
            for q in range(4):
                conv(0, 0, q)
            soften(0, 0)
            soften(0, 1)

            def body(k, parity, first, scan_, prepare, finish, image=0, turn=False):
                fb = image if not isinstance(k, int) else (k - 1) // CPB
                for unit in range(UNITS):
                    if scan_:
                        scan(k, unit)
                        if unit >= 1:
                            add_y(k, unit - 1, parity)
                    if finish and unit == 0:
                        add_y(k - 1, UNITS - 1, 1 - parity)
                    if scan_:
                        if unit in (1, 2):
                            soften(k, 1 + unit)
                        if unit in (18, 19):
                            skip(k, parity, unit - 18)
                    if finish:
                        if unit in (2, 3):
                            skip(k - 1, 1 - parity, unit)
                        if unit in (6, 8):
                            residual(k - 1, 4 + (unit - 6) // 2)
                        if unit == 9:
                            centre2(k - 1)
                        if unit == 12:
                            scale2(k - 1)
                        if unit == 15:
                            sum_tokens(k - 1, fb)
                    if prepare:
                        if unit == 10:
                            centre1(k + 1)
                        if unit == 13:
                            var_of_normed(k + 1)
                        if unit == 14:
                            scale1(k + 1)
                            keep_tail(k + 1, turn)
                        if unit in (18, 20, 22, 24):
                            conv(k + 1, 1 - parity, (unit - 18) // 2)
                        if unit in (28, 29):
                            soften(k + 1, unit - 28)

            iterations(dve, body)


R_B1, R_RW, R_B2 = 0, FT, FT + KT * PARTS
R_SEL = R_B2 + DIM
R_PW = R_SEL + FT * P
R_REV = R_PW + EXPERTS
R_COLS = R_REV + PARTS + BATCH


def build_experts(nc, tsum, x2_scr, tn_scr, w1_in, w2_in, r_in, ident_in, out):
    with ExitStack() as ctx:
        def sb(name, shape, dt=F32):
            return ctx.enter_context(nc.sbuf_tensor(name, shape, dt))

        def sem(name):
            return ctx.enter_context(nc.semaphore(name))

        w1_hi = sb("w1_hi", [P, KT, FPAD], F32R)
        w1_lo = sb("w1_lo", [P, KT, FPAD], F32R)
        w2_hi = sb("w2_hi", [P, FT, DIM], F32R)
        w2_lo = sb("w2_lo", [P, FT, DIM], F32R)
        raw = sb("raw", [P, 2, TF])
        tn = sb("tn", [P, KT, TF])
        t_hi = sb("t_hi", [P, 2, KT, TF], F32R)
        t_lo = sb("t_lo", [P, 2, KT, TF], F32R)
        x2t = sb("x2t", [P, 2, KT, TF])
        g = sb("g", [P, 2, TF])
        g_hi = sb("g_hi", [P, 2, TF], F32R)
        g_lo = sb("g_lo", [P, 2, TF], F32R)
        wf = sb("wf", [P, FT + KT, BATCH])
        b1 = sb("b1", [P, FT])
        h_ps = ctx.enter_context(nc.psum_tensor("h_ps", [P, 4, TF], F32))
        acc = ctx.enter_context(nc.psum_tensor("acc", [P, KT, TF], F32))
        r_all = x2t[:, :, :, :].rearrange("p a k t -> p (a k t)")

        r_sem, tn_in, raw_read, router_pe, router_dve, router_act, routed = (
            sem("r_sem"), sem("tn_in"), sem("raw_read"), sem("router_pe"), sem("router_dve"),
            sem("router_act"), sem("routed"))
        raw_in = [sem(f"raw_in{i}") for i in range(2)]
        x2_in = [sem(f"x2_in{i}") for i in range(2)]
        out_stored = [sem(f"out_stored{i}") for i in range(2)]
        raw_scaled, split_hi = sem("raw_scaled"), sem("split_hi")
        tok_hi, tok_split = sem("tok_hi"), sem("tok_split")
        h_mm, h_read, g_hi_ready, g_lo_ready, o_mm, acc_read = (
            sem("h_mm"), sem("h_read"), sem("g_hi_ready"), sem("g_lo_ready"), sem("o_mm"), sem("acc_read"))
        last = BATCH * FCPB - 1

        def chunks(eng, body):
            body(0, 0, 0, False, True, False, False)
            with eng.Fori(0, FCPB // 2 - 1) as i:
                body(i * 2 + 1, 1, 0, True, True, False, False)
                body(i * 2 + 2, 0, 0, True, True, False, False)
            body(FCPB - 1, 1, 0, True, True, True, False)
            body(FCPB, 0, 1, True, True, False, True)
            with eng.Fori(0, FCPB // 2 - 1) as i:
                body(i * 2 + FCPB + 1, 1, 1, True, True, False, False)
                body(i * 2 + FCPB + 2, 0, 1, True, True, False, False)
            body(last, 1, 1, True, False, False, False)

        block = ctx.enter_context(nc.Block())

        @block.sync
        def _(sp):
            def chunk_of(dram, b, c):
                t0 = (c - b * FCPB) * TF
                view = dram[b].rearrange("(k p) t -> p k t", p=P)
                return view[:, :, t0:t0 + TF] if isinstance(c, int) else view[:, :, bass.ds(t0, TF)]

            def load_piece(r):
                ge(sp, raw_read, r - 1)
                src = w1_in[:, r // KT, (r % KT) * TF:(r % KT + 1) * TF] if r < FT else w2_in[:, r % FT, :]
                sp.dma_start(raw[:, r % 2, :], src).then_inc(raw_in[r % 2], 16)

            def load_tn(b, c):
                ge(sp, tok_split, c * KT)
                sp.dma_start(tn[:, :, :], chunk_of(tn_scr, b, c)).then_inc(tn_in, 16)

            def load_x2(b, c, parity):
                ge(sp, out_stored[parity], (c - parity) // 2 * 16 if isinstance(c, int) else (c - parity) * 8)
                sp.dma_start(x2t[:, parity], chunk_of(x2_scr, b, c)).then_inc(x2_in[parity], 16)

            def store(b, c, parity):
                sp.wait_ge(acc_read, (c + 1) * KT)
                sp.dma_start(chunk_of(out, b, c), x2t[:, parity]).then_inc(out_stored[parity], 16)

            sp.dma_start(r_all[:, 0:R_COLS - FT], r_in[:, FT:R_COLS]).then_inc(r_sem, 16)
            sp.dma_start(b1[:, :], r_in[:, R_B1:R_B1 + FT]).then_inc(r_sem, 16)
            load_tn(0, 0)
            for r in range(2 * FT):
                load_piece(r)
            sp.wait_ge(routed, 2)
            load_x2(0, 0, 0)

            def body(c, parity, image, prev, nxt, closing, opening):
                after = image if not isinstance(c, int) else (c + 1) // FCPB
                before = image if not isinstance(c, int) else (c - 1) // FCPB
                if opening:
                    for r in range(3 * FT - 2, 3 * FT):
                        load_piece(r)
                if prev:
                    store(before, c - 1, 1 - parity)
                if nxt:
                    load_tn(after, c + 1)
                    load_x2(after, c + 1, 1 - parity)
                if closing:
                    for r in range(2 * FT, 3 * FT - 2):
                        load_piece(r)

            chunks(sp, body)
            store(1, last, 1)
            sp.wait_ge(out_stored[0], (last + 1) * 8)
            sp.wait_ge(out_stored[1], (last + 1) * 8)

        def table(col, width, rows):
            return r_all[0:rows, col - FT:col - FT + width]

        def small(i, rows=BATCH, cols=PARTS):
            return g[0:rows, 0, 16 * i:16 * i + cols]

        logits, probs, sel1, sel2, mix, hot, rest = (small(i) for i in range(7))
        top, neg_top, total, m1, m2, r1, r2 = (small(7 + i, cols=1) for i in range(7))
        mix_t, w_e = small(14, PARTS, BATCH), small(15, EXPERTS, BATCH)

        @block.tensor
        def _(pe):
            pe.wait_ge(r_sem, 32)
            for kt in range(KT):
                mm = pe.matmul(h_ps[0:BATCH, 0, 0:PARTS], tsum[:, kt, :], table(R_RW + kt * PARTS, PARTS, P),
                               start=kt == 0, stop=kt == KT - 1)
            mm.then_inc(router_pe, 1)
            pe.wait_ge(routed, 1)
            pe.transpose(h_ps[0:PARTS, 1, 0:BATCH], mix, table(R_REV + PARTS, BATCH, BATCH)).then_inc(router_pe, 1)
            pe.wait_ge(router_act, 2)
            pe.matmul(h_ps[0:EXPERTS, 2, 0:BATCH], table(R_PW, EXPERTS, PARTS), mix_t, start=True,
                      stop=True).then_inc(router_pe, 1)
            pe.wait_ge(router_act, 3)
            for f in range(FT):
                pe.matmul(h_ps[:, 3, 2 * f:2 * f + 2], table(R_SEL + f * P, P, EXPERTS), w_e, start=True, stop=True)
            for m in range(KT):
                mm = pe.matmul(h_ps[:, 3, 2 * (FT + m):2 * (FT + m) + 2], table(R_B2 + m * P, P, EXPERTS), w_e,
                               start=True, stop=True)
            mm.then_inc(router_pe, 1)
            pe.wait_ge(raw_read, FT)
            pe.wait_ge(routed, 2)

            def hidden(c, parity, f):
                ge(pe, h_read, c * FT + f - 3)
                if f == 0:
                    pe.wait_ge(tok_split, (c + 1) * KT)
                cols = slice(f * P, f * P + P)
                terms = [(w, t, kt) for w, t in ((w1_hi, t_hi), (w1_lo, t_hi), (w1_hi, t_lo)) for kt in range(KT)]
                for i, (w, t, kt) in enumerate(terms):
                    mm = pe.matmul(h_ps[:, f % 4, :], w[:, kt, cols], t[:, parity, kt, :], start=i == 0,
                                   stop=i == len(terms) - 1)
                mm.then_inc(h_mm, 1)

            def project(c, image, f):
                pe.wait_ge(g_lo_ready, c * FT + f + 1)
                pe.wait_ge(raw_read, (image + 1) * FT + f + 1)
                for m in range(KT):
                    if f == 0:
                        ge(pe, acc_read, (c - 1) * KT + m + 1)
                    cols = slice(m * P, m * P + P)
                    for i, (w, t) in enumerate(((w2_hi, g_hi), (w2_lo, g_hi), (w2_hi, g_lo))):
                        mm = pe.matmul(acc[:, m, :], w[:, f, cols], t[:, f % 2, :], start=f == 0 and i == 0,
                                       stop=f == FT - 1 and i == 2)
                mm.then_inc(o_mm, 1)

            def body(c, parity, image, prev, nxt, closing, opening):
                before = image if not isinstance(c, int) else (c - 1) // FCPB
                for f in range(FT):
                    hidden(c, parity, f)
                    if f:
                        project(c, image, f - 1)
                    elif prev:
                        project(c - 1, before, FT - 1)

            chunks(pe, body)
            project(last, 1, FT - 1)

        @block.scalar
        def _(act):
            act.wait_ge(router_dve, 3)
            act.activation(probs, logits, ACT.Exp, bias=neg_top).then_inc(router_act, 1)
            act.wait_ge(router_pe, 2)
            act.activation(mix_t, h_ps[0:PARTS, 1, 0:BATCH], ACT.Copy).then_inc(router_act, 1)
            act.wait_ge(router_dve, 20)
            act.activation(w_e, small(16, EXPERTS, BATCH), ACT.Copy).then_inc(router_act, 1)
            act.wait_ge(routed, 2)
            act.preload_act_table_set("gelu_and_others")

            def gelu(c, f):
                ge(act, g_lo_ready, c * FT + f - 1)
                act.wait_ge(h_mm, c * FT + f + 1)
                act.activation(g[:, f % 2, :], h_ps[:, f % 4, :], ACT.Gelu, bias=b1[:, f:f + 1]).then_inc(h_read, 1)
                ge(act, o_mm, c * FT + f - 1)
                act.wait_ge(h_read, c * FT + f + 1)
                act.activation(g_hi[:, f % 2, :], g[:, f % 2, :], ACT.Copy).then_inc(g_hi_ready, 1)

            def body(c, parity, image, prev, nxt, closing, opening):
                for f in range(FT):
                    gelu(c, f)

            chunks(act, body)

        @block.vector
        def _(dve):
            steps = [0]

            def step(ins):
                steps[0] += 1
                ins.then_inc(router_dve, 1)
                dve.wait_ge(router_dve, steps[0])

            dve.wait_ge(router_pe, 1)
            rev = table(R_REV, PARTS, BATCH)
            step(dve.tensor_scalar(logits, h_ps[0:BATCH, 0, 0:PARTS], 1.0 / TOKENS, None, ALU.mult))
            step(dve.tensor_reduce(top, logits, AX_X, ALU.max))
            step(dve.tensor_scalar(neg_top, top, -1.0, None, ALU.mult))
            dve.wait_ge(router_act, 1)
            step(dve.tensor_reduce(total, probs, AX_X, ALU.add))
            step(dve.reciprocal(total, total))
            step(dve.tensor_scalar(probs, probs, total, None, ALU.mult))
            step(dve.tensor_reduce(m1, probs, AX_X, ALU.max))
            step(dve.scalar_tensor_tensor(hot, probs, m1, rev, ALU.is_equal, ALU.mult))
            step(dve.tensor_reduce(r1, hot, AX_X, ALU.max))
            step(dve.tensor_scalar(sel1, rev, r1, None, ALU.is_equal))
            step(dve.scalar_tensor_tensor(rest, sel1, -2.0, probs, ALU.mult, ALU.add))
            step(dve.tensor_reduce(m2, rest, AX_X, ALU.max))
            step(dve.scalar_tensor_tensor(hot, rest, m2, rev, ALU.is_equal, ALU.mult))
            step(dve.tensor_reduce(r2, hot, AX_X, ALU.max))
            step(dve.tensor_scalar(sel2, rev, r2, m2, ALU.is_equal, ALU.mult))
            step(dve.scalar_tensor_tensor(mix, sel1, m1, sel2, ALU.mult, ALU.add))
            step(dve.tensor_tensor(m1, m1, m2, ALU.add))
            step(dve.reciprocal(m1, m1))
            dve.tensor_scalar(mix, mix, m1, None, ALU.mult).then_inc(routed, 1)
            dve.wait_ge(router_pe, 3)
            raw_w = small(17, EXPERTS, BATCH)
            step(dve.tensor_copy(raw_w, h_ps[0:EXPERTS, 2, 0:BATCH]))
            step(dve.scalar_tensor_tensor(small(16, EXPERTS, BATCH), raw_w, 1e-6, raw_w, ALU.is_gt, ALU.mult))
            assert steps[0] == 20
            dve.wait_ge(router_pe, 4)
            dve.tensor_copy(wf[:, :, :], h_ps[:, 3, 0:2 * (FT + KT)].rearrange("p (f b) -> p f b", b=2))\
               .then_inc(routed, 1)

            def split_w1(r):
                kt, col = r // KT, (r % KT) * TF
                hi, lo = w1_hi[:, kt, col:col + TF], w1_lo[:, kt, col:col + TF]
                dve.wait_ge(raw_in[r % 2], (r // 2 + 1) * 16)
                dve.tensor_copy(hi, raw[:, r % 2, :]).then_inc(split_hi, 1)
                dve.wait_ge(split_hi, r + 1)
                dve.tensor_tensor(lo, raw[:, r % 2, :], hi, ALU.subtract).then_inc(raw_read, 1)

            def split_w2(image, f):
                r = FT * (1 + image) + f
                slot = raw[:, r % 2, :]
                dve.wait_ge(raw_in[r % 2], (r // 2 + 1) * 16)
                ge(dve, o_mm, (image * FCPB - 1) * FT + f + 1)
                dve.tensor_scalar(slot, slot, wf[:, f, image:image + 1], None, ALU.mult).then_inc(raw_scaled, 1)
                dve.wait_ge(raw_scaled, image * FT + f + 1)
                dve.tensor_copy(w2_hi[:, f, :], slot).then_inc(split_hi, 1)
                dve.wait_ge(split_hi, r + 1)
                dve.tensor_tensor(w2_lo[:, f, :], slot, w2_hi[:, f, :], ALU.subtract).then_inc(raw_read, 1)

            def split_tokens(c, parity, kt):
                if kt == 0:
                    ge(dve, h_mm, (c - 1) * FT)
                    dve.wait_ge(tn_in, (c + 1) * 16)
                dve.tensor_copy(t_hi[:, parity, kt, :], tn[:, kt, :]).then_inc(tok_hi, 1)
                dve.wait_ge(tok_hi, c * KT + kt + 1)
                dve.tensor_tensor(t_lo[:, parity, kt, :], tn[:, kt, :], t_hi[:, parity, kt, :],
                                  ALU.subtract).then_inc(tok_split, 1)

            def low_half(c, f):
                dve.wait_ge(g_hi_ready, c * FT + f + 1)
                dve.tensor_tensor(g_lo[:, f % 2, :], g[:, f % 2, :], g_hi[:, f % 2, :],
                                  ALU.subtract).then_inc(g_lo_ready, 1)

            def drain(c, parity, image, m):
                if m == 0:
                    dve.wait_ge(o_mm, (c + 1) * FT)
                    dve.wait_ge(x2_in[parity], (c - parity) * 8 + 16)
                x = x2t[:, parity, m, :]
                dve.scalar_tensor_tensor(x, acc[:, m, :], wf[:, FT + m, image:image + 1], x, ALU.add,
                                         ALU.add).then_inc(acc_read, 1)

            for r in range(FT):
                split_w1(r)
            dve.wait_ge(routed, 2)
            for kt in range(KT):
                split_tokens(0, 0, kt)
            for f in range(FT):
                split_w2(0, f)

            def body(c, parity, image, prev, nxt, closing, opening):
                before = image if not isinstance(c, int) else (c - 1) // FCPB
                for f in range(FT):
                    low_half(c, f)
                    if f == 1 and prev:
                        for m in range(KT):
                            drain(c - 1, 1 - parity, before, m)
                    if 4 <= f < 4 + KT and nxt:
                        split_tokens(c + 1, 1 - parity, f - 4)
                    if closing and f >= 2:
                        split_w2(1, f - 2)
                    if opening and f < 2:
                        split_w2(1, FT - 2 + f)

            chunks(dve, body)
            for m in range(KT):
                drain(last, 1, 1, m)


def build(nc, x, vecs, ident, mean_w, wi, wo, wx, wdt, w1, w2, router, out):
    b_scr = nc.dram_tensor("b_scr", (CHUNKS, STATES, T), F32, kind="Internal").ap()
    x2_scr = nc.dram_tensor("x2_scr", (BATCH, DIM, TOKENS), F32, kind="Internal").ap()
    tn_scr = nc.dram_tensor("tn_scr", (BATCH, DIM, TOKENS), F32, kind="Internal").ap()
    with nc.sbuf_tensor("tsum", [P, KT, BATCH], F32) as tsum:
        build_mixer(nc, x, vecs, ident, mean_w, wi, wo, wx, wdt, tsum, b_scr, x2_scr, tn_scr)
        build_experts(nc, tsum, x2_scr, tn_scr, w1, w2, router, ident, out)


def kernel(x, L0_conv_ln_w, L0_conv_ln_b, L0_conv_in_proj_w, L0_conv_conv_w, L0_conv_conv_b, L0_conv_x_proj_w,
           L0_conv_dt_proj_w, L0_conv_dt_proj_b, L0_conv_A_log, L0_conv_D_skip, L0_conv_out_proj_w,
           L0_ffn_router_w, L0_ffn_W1, L0_ffn_b1, L0_ffn_W2, L0_ffn_b2):
    import concourse.bacc as bacc
    from concourse.bass_utils import run_bass_kernel_spmd

    f32 = np.float32

    def tiles(a, rows):
        a = np.asarray(a, f32)
        return np.ascontiguousarray(a.reshape(rows // P, P, -1).transpose(1, 0, 2))

    xb = np.zeros((P, 1), f32)
    xb[ONE_ROW] = 1.0
    vecs = np.concatenate([tiles(L0_conv_ln_w, DIM).reshape(P, -1), tiles(L0_conv_ln_b, DIM).reshape(P, -1),
                           tiles(L0_conv_conv_w, INNER).reshape(P, -1), tiles(L0_conv_conv_b, INNER).reshape(P, -1),
                           tiles(L0_conv_D_skip, INNER).reshape(P, -1), tiles(L0_conv_A_log, INNER).reshape(P, -1),
                           xb], axis=1)
    xp = np.asarray(L0_conv_x_proj_w, f32)
    wx = np.zeros((INNER, XR), f32)
    wx[:, 0:RANK] = xp[0:RANK].T
    wx[:, B_ROW:B_ROW + STATES] = xp[RANK:RANK + STATES].T
    wx[:, C_ROW:C_ROW + STATES] = xp[RANK + STATES:].T
    wdt = np.concatenate([np.asarray(L0_conv_dt_proj_w, f32).T, np.asarray(L0_conv_dt_proj_b, f32)[None]], axis=0)
    w1 = np.zeros((DIM, FPAD), f32)
    w1[:, :EXPERTS * HIDDEN] = np.asarray(L0_ffn_W1, f32).transpose(1, 0, 2).reshape(DIM, -1)
    w2 = np.zeros((FPAD, DIM), f32)
    w2[:EXPERTS * HIDDEN] = np.asarray(L0_ffn_W2, f32).reshape(-1, DIM)
    b1 = np.zeros((FPAD, 1), f32)
    b1[:EXPERTS * HIDDEN, 0] = np.asarray(L0_ffn_b1, f32).reshape(-1)

    partitions = [(6,), (5, 1), (4, 2), (4, 1, 1), (3, 3), (3, 2, 1), (3, 1, 1, 1), (2, 2, 2), (2, 2, 1, 1),
                  (2, 1, 1, 1, 1), (1, 1, 1, 1, 1, 1)]
    router = np.zeros((P, R_COLS), f32)
    router[:, R_B1:R_B1 + FT] = tiles(b1, FPAD).reshape(P, -1)
    router[:, R_RW:R_RW + KT * PARTS] = tiles(np.asarray(L0_ffn_router_w, f32).T, DIM).reshape(P, -1)
    router[0:EXPERTS, R_B2:R_B2 + DIM] = np.asarray(L0_ffn_b2, f32)
    for e in range(EXPERTS):
        router[e, R_SEL + e * HIDDEN:R_SEL + (e + 1) * HIDDEN] = 1.0
    for i, parts in enumerate(partitions):
        for j, part in enumerate(parts):
            router[i, R_PW + j] = f32(part / 6)
    router[0:BATCH, R_REV:R_REV + PARTS] = np.arange(PARTS, 0, -1, dtype=f32)
    router[0:BATCH, R_REV + PARTS:R_REV + PARTS + BATCH] = np.eye(BATCH, dtype=f32)

    arrays = {
        "x": np.ascontiguousarray(np.asarray(x, f32).reshape(BATCH, DIM, TOKENS)), "vecs": vecs,
        "ident": np.eye(P, dtype=f32), "mean_w": np.full((P, P), 1.0 / DIM, f32),
        "wi": tiles(np.asarray(L0_conv_in_proj_w, f32).T, DIM), "wo": tiles(np.asarray(L0_conv_out_proj_w, f32).T, INNER),
        "wx": tiles(wx, INNER), "wdt": np.ascontiguousarray(wdt), "w1": tiles(w1, DIM), "w2": tiles(w2, FPAD),
        "router": router,
    }
    nc = bacc.Bacc("TRN2", target_bir_lowering=False, num_devices=1)
    args = [nc.dram_tensor("in_" + name, a.shape, F32, kind="ExternalInput").ap() for name, a in arrays.items()]
    out = nc.dram_tensor("out", (BATCH, DIM, TOKENS), F32, kind="ExternalOutput").ap()
    build(nc, *args, out)
    r = run_bass_kernel_spmd(nc, [{"in_" + name: a for name, a in arrays.items()}], core_ids=[0])
    return r.results[0]["out"].reshape(BATCH, DIM, 64, 64)
```

```python
from contextlib import ExitStack

import numpy as np

import concourse.bass as bass
from concourse import mybir

P = 128
BATCH, DIM, TOKENS = 2, 512, 4096
INNER, STATES, TAPS, RANK = 1024, 16, 4, 32
EXPERTS, HIDDEN, PARTS = 6, 341, 11
KT = DIM // P
DT = INNER // P
HT = DT // 2
T = 256
TS = T // P
CPB = TOKENS // T
CHUNKS = BATCH * CPB
UNITS = 2 * STATES
XR = 96
ONE_ROW, C_ROW, B_ROW = 32, 64, 80
SEG = T + 1
HS = 4
BP = 2
TF = 512
FCPB = TOKENS // TF
FT = 16
FPAD = FT * P

F32 = mybir.dt.float32
F32R = mybir.dt.float32r
ACT = mybir.ActivationFunctionType
ALU = mybir.AluOpType
AX_X = mybir.AxisListType.X

V_LNW, V_LNB, V_CW, V_CB, V_D, V_AL, V_XB = 0, 4, 8, 40, 48, 56, 184
V_COLS = 185

HALF_ROOT = 0.5 ** 0.5
XIN, Z01, Z23, DT0, DT1, Z45, Z67, DT2, DT3 = 0, 4, 5, 6, 7, 8, 9, 10, 11
PRE = 12
Z_GROUP = (Z01, Z23, Z45, Z67)
DT_GROUP = (DT0, DT1, DT2, DT3)
TB2, TB3, OUT01, OUT23, X_PROJ, MEANS, TB0, VARS, TB1, TURN_C = range(10)
FIN = 10


def ge(eng, sem, value):
    if isinstance(value, int) and value <= 0:
        return
    eng.wait_ge(sem, value)


def build_mixer(nc, x, vecs, ident_in, mean_in, wi_in, wo_in, wx_in, wdt_in, tsum, b_scr, x2_scr, tn_scr):
    with ExitStack() as ctx:
        def sb(name, shape, dt=F32):
            return ctx.enter_context(nc.sbuf_tensor(name, shape, dt))

        def sem(name):
            return ctx.enter_context(nc.semaphore(name))

        w_in = sb("w_in", [P, KT, 2 * INNER])
        w_out = sb("w_out", [P, DT, DIM])
        w_x = sb("w_x", [P, DT, XR])
        w_dt = sb("w_dt", [RANK + 1, INNER])
        vec = sb("vec", [P, V_COLS])
        ident = sb("ident", [P, P])
        mean_w = sb("mean_w", [P, P])
        neg_a = sb("neg_a", [P, DT, STATES])
        eps = sb("eps", [P, 2])
        x_t = sb("x_t", [P, KT, T])
        xn = sb("xn", [P, KT, T])
        cv = sb("cv", [P, DT, T])
        sq, sq2 = cv[:, 0:KT, :], cv[:, KT:2 * KT, :]
        ln_l = sb("ln_l", [P, T])
        ln_r1 = sb("ln_r1", [P, T])
        ln_r2 = sb("ln_r2", [P, T])
        ln_v = sb("ln_v", [P, T])
        xin = sb("xin", [P, DT, TAPS - 1 + T])
        u = sb("u", [P, 2, DT, T])
        zs = sb("zs", [P, 2, DT, T])
        xd = sb("xd", [XR, 2, T])
        sp_t = sb("sp_t", [P, 2, 2 * T])
        sp_l = sb("sp_l", [P, 2, 2 * T])
        sp_w = sb("sp_w", [P, 2, 2 * T])
        sp_q = sb("sp_q", [P, 2, 2 * T])
        delta = sb("delta", [P, 2, HT, T])
        du = sb("du", [P, HT, T])
        b_rep = sb("b_rep", [P, BP, 2, T])
        c_tok = sb("c_tok", [P, 2, TS, STATES])
        da = sb("da", [P, 2, HT, SEG])
        dbh = sb("dbh", [P, HS, HT, SEG])
        state = sb("state", [P, 2, STATES, HT])
        y_t = sb("y_t", [P, 2, TS, HT * P])
        x2 = sb("x2", [P, KT, T])
        d2 = sb("d2", [P, KT, T])
        ln2_l = sb("ln2_l", [P, T])
        ln2_r = sb("ln2_r", [P, T])
        t_red = sb("t_red", [P, KT])

        h_tok = ctx.enter_context(nc.psum_tensor("h_tok", [P, 4, HT * P], F32))
        pre = ctx.enter_context(nc.psum_tensor("pre", [P, 2, 2 * T], F32))
        fin = ctx.enter_context(nc.psum_tensor("fin", [P, 2, 2 * T], F32))

        consts_in, wi_sem, wrest_in = sem("consts_in"), sem("wi_sem"), sem("wrest_in")
        set_dve, set_act = sem("set_dve"), sem("set_act")
        x_in, xres_in, stored = sem("x_in"), sem("xres_in"), sem("stored")
        b_stored = sem("b_stored")
        b_in = [sem(f"b_in{i}") for i in range(BP)]
        pre_mm, fin_mm = sem("pre_mm"), sem("fin_mm")
        pre_read = [sem(f"pre_read{i}") for i in range(2)]
        fin_read = [sem(f"fin_read{i}") for i in range(2)]
        squared, rstd_act, rstd_dve, xn_ready = sem("squared"), sem("rstd_act"), sem("rstd_dve"), sem("xn_ready")
        centred2, ln2_log = sem("centred2"), sem("ln2_log")
        tail_kept, conv_step, u_ready = sem("tail_kept"), sem("conv_step"), sem("u_ready")
        soft_act = [sem(f"soft_act{i}") for i in range(2)]
        soft_dve, soft_pool, delta_ready = sem("soft_dve"), sem("soft_pool"), sem("delta_ready")
        z_ready, du_ready = sem("z_ready"), sem("du_ready")
        da_ready, db_ready, h_ready, h_turned, y_added, state_saved = (
            sem("da_ready"), sem("db_ready"), sem("h_ready"), sem("h_turned"), sem("y_added"), sem("state_saved"))
        y_gated, squared2, ln2_ready, tok_step = sem("y_gated"), sem("squared2"), sem("ln2_ready"), sem("tok_step")

        def pre_made(c, j):
            return c * PRE + j + 1

        def pre_bank_read(c, j):
            return pre_read[j % 2], c * (PRE // 2) + j // 2 + 1

        def absent(k):
            if not isinstance(k, int):
                return ()
            return (CHUNKS - 1, X_PROJ), (CHUNKS - 1, TURN_C), (CHUNKS, X_PROJ), (CHUNKS, TB0)

        def fin_made(k, j):
            if isinstance(k, int) and k < 0:
                return {(-2, MEANS): 1, (-2, VARS): 2, (-1, X_PROJ): 3, (-1, TURN_C): 4, (-1, MEANS): 5,
                        (-1, VARS): 6}[k, j]
            return k * FIN + j + 3 - sum(a < (k, j) for a in absent(k))

        def fin_bank(k, j):
            return (fin_made(k, j) - 1) % 2 if isinstance(k, int) and k < 0 else j % 2

        def fin_bank_read(k, j):
            if isinstance(k, int) and k < 0:
                return fin_read[fin_bank(k, j)], (fin_made(k, j) + 1) // 2
            return (fin_read[j % 2],
                    k * (FIN // 2) + j // 2 + 2 - sum(a < (k, j) and a[1] % 2 == j % 2 for a in absent(k)))

        def iterations(eng, body):
            for k in range(2):
                body(k, k, 0)
            with eng.Fori(0, CPB // 2 - 2) as i:
                body(i * 2 + 2, 0, 0)
                body(i * 2 + 3, 1, 0)
            for k in range(CPB - 2, CPB + 1):
                body(k, k % 2, 0)
            with eng.Fori(0, CPB // 2 - 2) as i:
                body(i * 2 + CPB + 1, 1, 1)
                body(i * 2 + CPB + 2, 0, 1)
            for k in range(CHUNKS - 3, CHUNKS + 1):
                body(k, k % 2, 1)

        def runs(k):
            if not isinstance(k, int):
                return True, True, True, True
            return k < CHUNKS, k + 1 < CHUNKS, k + 2 < CHUNKS, k >= 1

        block = ctx.enter_context(nc.Block())

        @block.sync
        def _(sp):
            sp.dma_start(vec[:, :], vecs).then_inc(consts_in, 16)
            sp.dma_start(mean_w[:, :], mean_in).then_inc(consts_in, 16)
            sp.dma_start(ident[:, :], ident_in).then_inc(consts_in, 16)

            def chunk_at(dram, c):
                return dram[c] if isinstance(c, int) else dram[bass.ds(c, 1)].rearrange("a p k t -> (a p) k t")

            def load_x(c):
                ge(sp, rstd_dve, (c - 1) * 3 + 3)
                sp.dma_start(x_t[:, :, :], chunk_at(x, c)).then_inc(x_in, 16)

            def load_residual(c):
                ge(sp, stored, c * 32)
                sp.dma_start(x2[:, :, :], chunk_at(x, c)).then_inc(xres_in, 16)

            def store_x2(c):
                sp.wait_ge(tok_step, c * 3 + 1)
                sp.dma_start(chunk_at(x2_scr, c), x2[:, :, :]).then_inc(stored, 16)

            def store_tn(c):
                sp.dma_start(chunk_at(tn_scr, c), d2[:, :, :]).then_inc(stored, 16)

            def b_rows(c):
                return b_scr[c] if isinstance(c, int) else b_scr[bass.ds(c, 1)].rearrange("a n t -> (a n) t")

            def store_b(c, parity):
                sp.wait_ge(*fin_bank_read(c - 1, X_PROJ))
                sp.dma_start(b_rows(c), xd[B_ROW:B_ROW + STATES, parity, :]).then_inc(b_stored, 16)

            def load_b_piece(c, p):
                if p == 0:
                    sp.wait_ge(b_stored, (c + 1) * 16)
                else:
                    ge(sp, db_ready, c * UNITS + 2 * p - 2)
                n = 2 * p % STATES
                rows = b_rows(c)[n:n + 2, :]
                src = bass.AP(tensor=rows.tensor, offset=rows.offset, ap=[[0, P]] + list(rows.ap))
                sp.dma_start(b_rep[:, p % BP], src).then_inc(b_in[p % BP], 16)

            load_x(0)
            sp.dma_start(w_in[:, :, :], wi_in).then_inc(wi_sem, 16)
            sp.dma_start(w_x[:, :, :], wx_in).then_inc(wrest_in, 16)
            sp.dma_start(w_dt[:, :], wdt_in).then_inc(wrest_in, 16)
            sp.dma_start(w_out[:, :, :], wo_in).then_inc(wrest_in, 16)
            load_x(1)
            store_b(0, 0)

            def body(k, parity, image):
                scan, prepare, normalize, finish = runs(k)
                for p in range(UNITS // 2):
                    if scan:
                        load_b_piece(k, p)
                    if p == 1 and normalize:
                        load_x(k + 2)
                    if p == 2 and finish:
                        load_residual(k - 1)
                    if p == 12 and prepare:
                        store_b(k + 1, 1 - parity)
                if finish:
                    store_x2(k - 1)
                if prepare:
                    sp.wait_ge(db_ready, k * UNITS + UNITS - 2)
                if finish:
                    store_tn(k - 1)

            iterations(sp, body)
            sp.wait_ge(stored, CHUNKS * 32)

        @block.gpsimd
        def _(pool):
            def soften(c, q, step):
                half, pair = q // 2, q % 2
                d = delta[:, half, 2 * pair:2 * pair + 2, :].rearrange("p a t -> p (a t)")
                if step == 0:
                    pool.wait_ge(soft_act[pair], (c * 2 + half) * 4 + 4)
                    pool.tensor_tensor(d, d, sp_t[:, q % 2, :], ALU.add).then_inc(soft_pool, 1)
                else:
                    pool.wait_ge(soft_pool, c * 4 + q + 1)
                    pool.wait_ge(soft_dve, (c * 4 + q) * 2 + 2)
                    pool.tensor_tensor(d, d, sp_l[:, q % 2, :], ALU.subtract).then_inc(delta_ready, 1)

            def make_du(c, parity, half):
                ge(pool, db_ready, c * UNITS + STATES * half)
                pool.wait_ge(delta_ready, c * 4 + 2 * half + 2)
                pool.wait_ge(u_ready, c + 1)
                pool.tensor_tensor(du[:, :, :], delta[:, half], u[:, parity, HT * half:HT * half + HT, :],
                                   ALU.mult).then_inc(du_ready, 1)

            def inject(k, unit, first):
                half, n = unit // STATES, unit % STATES
                g = k * UNITS + unit
                slot = dbh[:, unit % HS]
                ge(pool, h_turned, g * 2 - 6)
                ge(pool, state_saved, g - 3)
                if n == 0:
                    pool.wait_ge(du_ready, k * 2 + half + 1)
                if n % 2 == 0:
                    pool.wait_ge(b_in[(unit // 2) % BP], (k * (UNITS // 2 // BP) + unit // 2 // BP + 1) * 16)
                rep = b_rep[:, (unit // 2) % BP, n % 2:n % 2 + 1, :].broadcast_to((P, HT, T))
                pool.tensor_tensor(slot[:, :, 1:SEG], du[:, :, :], rep, ALU.mult)
                if first:
                    pool.memset(slot[:, :, 0:1], 0.0).then_inc(db_ready, 1)
                else:
                    pool.tensor_copy(slot[:, :, 0:1], state[:, half, n, :].rearrange("p (a b) -> p a b", b=1))\
                        .then_inc(db_ready, 1)

            def gate(c, parity, j):
                pool.wait_ge(*(fin_bank_read(c, (TB0, TB1)[j]) if j < 2 else fin_bank_read(c + 1, (TB2, TB3)[j - 2])))
                if j == 0:
                    pool.wait_ge(z_ready, c + 1)
                y = u[:, parity, 2 * j:2 * j + 2, :]
                pool.tensor_tensor(y, y, zs[:, parity, 2 * j:2 * j + 2, :], ALU.mult).then_inc(y_gated, 1)

            for q in range(2):
                soften(0, q, 0)
                soften(0, q, 1)

            def body(k, parity, image):
                scan, prepare, normalize, finish = runs(k)
                for unit in range(UNITS):
                    if scan:
                        if unit % STATES == 0:
                            make_du(k, parity, unit // STATES)
                        inject(k, unit, isinstance(k, int) and k % CPB == 0)
                        if unit in (8, 9):
                            soften(k, unit - 6, 0)
                        if unit in (10, 11):
                            soften(k, unit - 8, 1)
                        if unit in (27, 30):
                            gate(k, parity, (unit - 27) // 3)
                    if finish and unit in (7, 8):
                        gate(k - 1, 1 - parity, unit - 5)
                    if prepare:
                        if unit in (26, 28):
                            soften(k + 1, (unit - 26) // 2, 0)
                        if unit in (29, 31):
                            soften(k + 1, (unit - 29) // 2, 1)

            iterations(pool, body)

        @block.tensor
        def _(pe):
            def pre_free(c, j):
                s, count = pre_bank_read(c, j)
                ge(pe, s, count - 1)
                return pre[:, j % 2, :]

            def fin_free(k, j):
                s, count = fin_bank_read(k, j)
                ge(pe, s, count - 1)
                return fin[:, fin_bank(k, j), :]

            def token_mean(dst, src, last):
                for kt in range(KT):
                    mm = pe.matmul(dst, mean_w[:, :], src[:, kt, :], start=kt == 0, stop=kt == KT - 1)
                if last:
                    mm.then_inc(fin_mm, 1)

            def means(k, finish, normalize):
                bank = fin_free(k, MEANS)
                if finish:
                    pe.wait_ge(*fin_bank_read(k, OUT01))
                    pe.wait_ge(*fin_bank_read(k, OUT23))
                    token_mean(bank[:, 0:T], x2, not normalize)
                if normalize:
                    pe.wait_ge(x_in, (k + 3) * 16)
                    token_mean(bank[:, T:2 * T], x_t, True)

            def variances(k, finish, normalize, chunk):
                bank = fin_free(k, VARS) if chunk == 1 or not normalize else fin[:, fin_bank(k, VARS), :]
                if chunk == 1:
                    pe.wait_ge(squared, k + 3)
                    token_mean(bank[:, T:2 * T], sq, not finish)
                else:
                    pe.wait_ge(squared2, k)
                    token_mean(bank[:, 0:T], sq2, True)

            def in_tile(c, m):
                j, tile = XIN + m // 2 if m < DT else Z_GROUP[(m - DT) // 2], m % 2
                bank = pre[:, j % 2, :] if tile else pre_free(c, j)
                pe.wait_ge(xn_ready, c + 1)
                for kt in range(KT):
                    mm = pe.matmul(bank[:, tile * T:tile * T + T], w_in[:, kt, m * P:m * P + P], xn[:, kt, :],
                                   start=kt == 0, stop=kt == KT - 1)
                if tile == 1:
                    mm.then_inc(pre_mm, 1)

            def x_proj(c, parity, half):
                bank = fin[:, fin_bank(c - 1, X_PROJ), :] if half else fin_free(c - 1, X_PROJ)
                pe.wait_ge(u_ready, c + 1)
                for d in range(HT * half, HT * half + HT):
                    mm = pe.matmul(bank[0:XR, 0:T], w_x[:, d, :], u[:, parity, d, :], start=d == 0, stop=d == DT - 1)
                if half:
                    mm.then_inc(fin_mm, 1)

            def turn_c(c, parity):
                bank = fin_free(c - 1, TURN_C)
                pe.wait_ge(*fin_bank_read(c - 1, X_PROJ))
                for ts in range(TS):
                    mm = pe.transpose(bank[:, ts * XR:ts * XR + XR], xd[:, parity, ts * P:ts * P + P],
                                      ident[0:XR, 0:XR])
                mm.then_inc(fin_mm, 1)

            def dt_pair(c, parity, q):
                bank = pre_free(c, DT_GROUP[q])
                pe.wait_ge(*fin_bank_read(c - 1, X_PROJ))
                for tile in range(2):
                    m = 2 * q + tile
                    mm = pe.matmul(bank[:, tile * T:tile * T + T], w_dt[:, m * P:m * P + P],
                                   xd[0:RANK + 1, parity, :], start=True, stop=True)
                mm.then_inc(pre_mm, 1)

            def turn_h(k, unit):
                g = k * UNITS + unit
                pe.wait_ge(h_ready, g + 1)
                for ts in range(TS):
                    ge(pe, y_added, g * 2 + ts - 3)
                    for d in range(HT):
                        mm = pe.transpose(h_tok[:, (2 * unit + ts) % 4, d * P:d * P + P],
                                          dbh[:, unit % HS, d, 1 + ts * P:1 + ts * P + P], ident[:, :])
                    mm.then_inc(h_turned, 1)

            def turn_back(c, j):
                half, pair = j // 2, j % 2
                bank = fin_free(c, (TB0, TB1)[j]) if j < 2 else fin_free(c + 1, (TB2, TB3)[j - 2])
                pe.wait_ge(y_added, (c * UNITS + STATES * (half + 1)) * 2)
                for d in range(2):
                    for ts in range(TS):
                        mm = pe.transpose(bank[:, d * T + ts * P:d * T + ts * P + P],
                                          y_t[:, half, ts, (2 * pair + d) * P:(2 * pair + d + 1) * P], ident[:, :])
                mm.then_inc(fin_mm, 1)

            def out_tile(c, parity, m, half):
                j = OUT01 if m < 2 else OUT23
                bank = fin_free(c + 1, j) if m % 2 == 0 and half == 0 else fin[:, j % 2, :]
                pe.wait_ge(y_gated, c * 4 + 2 * half + 2)
                for d in range(HT * half, HT * half + HT):
                    mm = pe.matmul(bank[:, (m % 2) * T:(m % 2) * T + T], w_out[:, d, m * P:m * P + P],
                                   u[:, parity, d, :], start=m % 2 == 0 and d == 0,
                                   stop=m % 2 == 1 and d == DT - 1)
                if m % 2 == 1 and half:
                    mm.then_inc(fin_mm, 1)

            pe.wait_ge(consts_in, 48)
            means(-2, False, True)
            variances(-2, False, True, 1)
            pe.wait_ge(wi_sem, 16)
            for m in range(12):
                in_tile(0, m)
            pe.wait_ge(wrest_in, 48)
            x_proj(0, 0, 0)
            x_proj(0, 0, 1)
            turn_c(0, 0)
            dt_pair(0, 0, 0)
            dt_pair(0, 0, 1)
            for m in range(12, 16):
                in_tile(0, m)
            means(-1, False, True)
            variances(-1, False, True, 1)
            dt_pair(0, 0, 2)
            dt_pair(0, 0, 3)

            in_at = {0: (0,), 1: (1,), 2: (2,), 3: (3,), 4: (4,), 7: (5,), 8: (6,), 9: (7,), 14: (8,), 15: (9,),
                     16: (10,), 19: (11,), 23: (12,), 24: (13,), 25: (14,), 26: (15,)}
            out_at = {5: ((0, 0),), 6: ((1, 0),), 9: ((2, 0),), 10: ((3, 0), (0, 1)), 11: ((1, 1),), 12: ((2, 1),),
                      13: ((3, 1),)}

            def body(k, parity, image):
                scan, prepare, normalize, finish = runs(k)
                for unit in range(UNITS):
                    if scan:
                        turn_h(k, unit)
                        if unit in (21, 24):
                            turn_back(k, (unit - 21) // 3)
                    if finish:
                        if unit in (1, 2):
                            turn_back(k - 1, unit + 1)
                        for m, half in out_at.get(unit, ()):
                            out_tile(k - 1, 1 - parity, m, half)
                    if prepare:
                        for m in in_at.get(unit, ()):
                            in_tile(k + 1, m)
                        if unit in (16, 17):
                            x_proj(k + 1, 1 - parity, unit - 16)
                        if unit in (20, 22):
                            dt_pair(k + 1, 1 - parity, (unit - 20) // 2)
                        if unit == 26:
                            turn_c(k + 1, 1 - parity)
                        if unit in (28, 29):
                            dt_pair(k + 1, 1 - parity, unit - 26)
                    if unit == 18 and (finish or normalize):
                        means(k, finish, normalize)
                    if unit == 22 and normalize:
                        variances(k, finish, normalize, 1)
                    if unit == 23 and finish:
                        variances(k, finish, normalize, 2)

            iterations(pe, body)

        @block.scalar
        def _(act):
            act.wait_ge(consts_in, 48)
            act.preload_act_table_set("natural_log_exp_and_others")
            act.activation(neg_a[:, :, :], vec[:, V_AL:V_AL + DT * STATES].rearrange("p (d n) -> p d n", d=DT),
                           ACT.Exp).then_inc(set_act, 1)
            act.wait_ge(set_act, 1)
            act.activation(neg_a[:, :, :], neg_a[:, :, :], ACT.Copy, scale=-1.0).then_inc(set_act, 1)
            act.wait_ge(set_act, 2)
            act.wait_ge(set_dve, 6)

            def square1(c):
                act.wait_ge(*fin_bank_read(c - 2, MEANS))
                act.activation(sq, x_t[:, :, :], ACT.Square).then_inc(squared, 1)

            def rstd1(c):
                act.wait_ge(fin_mm, fin_made(c - 2, VARS))
                act.activation(ln_l[:, :], fin[:, fin_bank(c - 2, VARS), T:2 * T], ACT.Ln,
                               bias=eps[:, 0:1]).then_inc(rstd_act, 1)
                act.wait_ge(rstd_act, c * 4 + 1)
                act.activation(ln_r1[:, :], ln_l[:, :], ACT.Exp, scale=-0.5).then_inc(rstd_act, 1)

            def rstd1_again(c):
                act.wait_ge(rstd_dve, c * 3 + 1)
                act.activation(ln_l[:, :], ln_v[:, :], ACT.Ln, bias=eps[:, 1:2]).then_inc(rstd_act, 1)
                act.wait_ge(rstd_act, c * 4 + 3)
                act.activation(ln_r2[:, :], ln_l[:, :], ACT.Exp, scale=-0.5).then_inc(rstd_act, 1)

            def affine(c):
                act.wait_ge(rstd_dve, c * 3 + 3)
                for kt in range(KT):
                    last = act.activation(xn[:, kt, :], xn[:, kt, :], ACT.Identity,
                                          bias=vec[:, V_LNB + kt:V_LNB + kt + 1],
                                          scale=vec[:, V_LNW + kt:V_LNW + kt + 1])
                last.then_inc(xn_ready, 1)

            def take_xin(c, q):
                act.wait_ge(tail_kept, c + 1)
                act.wait_ge(pre_mm, pre_made(c, XIN + q))
                act.activation(xin[:, 2 * q:2 * q + 2, TAPS - 1:TAPS - 1 + T],
                               pre[:, q % 2, :].rearrange("p (a t) -> p a t", a=2), ACT.Copy).then_inc(pre_read[q % 2], 1)

            def silu_u(c, parity):
                act.wait_ge(conv_step, (c + 1) * 32)
                if not isinstance(c, int) or c >= 2:
                    act.wait_ge(fin_mm, fin_made(c - 1, OUT23))
                act.activation(u[:, parity], cv[:, :, :], ACT.Silu).then_inc(u_ready, 1)

            def take_z(c, parity, q):
                ge(act, y_gated, (c - 1) * 4)
                j = Z_GROUP[q]
                act.wait_ge(pre_mm, pre_made(c, j))
                act.activation(zs[:, parity, 2 * q:2 * q + 2, :],
                               pre[:, j % 2, :].rearrange("p (a t) -> p a t", a=2),
                               ACT.Copy).then_inc(pre_read[j % 2], 1)

            def silu_z(c, parity):
                act.wait_ge(*pre_bank_read(c, Z45))
                act.wait_ge(*pre_bank_read(c, Z67))
                act.activation(zs[:, parity], zs[:, parity], ACT.Silu).then_inc(z_ready, 1)

            def take_xd(c, parity):
                ge(act, b_stored, (c - 1) * 16)
                act.wait_ge(fin_mm, fin_made(c - 1, X_PROJ))
                bank = fin_bank(c - 1, X_PROJ)
                act.activation(xd[:, parity, :], fin[0:XR, bank, 0:T], ACT.Identity,
                               bias=vec[0:XR, V_XB:V_XB + 1]).then_inc(fin_read[bank], 1)

            def take_c(c, parity):
                ge(act, y_added, (c - 1) * UNITS * 2)
                act.wait_ge(fin_mm, fin_made(c - 1, TURN_C))
                bank = fin_bank(c - 1, TURN_C)
                src = fin[:, bank, 0:TS * XR].rearrange("p (s r) -> p s r", s=TS)[:, :, C_ROW:C_ROW + STATES]
                act.activation(c_tok[:, parity], src, ACT.Copy).then_inc(fin_read[bank], 1)

            def soft(c, q, step):
                half, pair = q // 2, q % 2
                t, l, w = sp_t[:, q % 2, :], sp_l[:, q % 2, :], sp_w[:, q % 2, :]
                j = DT_GROUP[q]
                steps = (c * 2 + half) * 4
                if step == 0:
                    ge(act, delta_ready, c * 4 + q - 1)
                    ge(act, da_ready, (c - 1) * UNITS + STATES * (half + 1))
                    ge(act, du_ready, (c - 1) * 2 + half + 1)
                    act.wait_ge(pre_mm, pre_made(c, j))
                    act.activation(t, pre[:, j % 2, :], ACT.Abs).then_inc(soft_act[pair], 1)
                    act.activation(delta[:, half, 2 * pair:2 * pair + 2, :].rearrange("p a t -> p (a t)"),
                                   pre[:, j % 2, :], ACT.Relu).then_inc(pre_read[j % 2], 1)
                elif step == 1:
                    act.wait_ge(soft_act[pair], steps + 1)
                    act.activation(t, t, ACT.Exp, scale=-1.0).then_inc(soft_act[pair], 1)
                    act.wait_ge(soft_act[pair], steps + 2)
                    act.activation(w, t, ACT.Identity, bias=1.0).then_inc(soft_act[pair], 1)
                else:
                    act.activation(sp_q[:, q % 2, :], t, ACT.Square, scale=HALF_ROOT)
                    act.wait_ge(soft_act[pair], steps + 3)
                    act.activation(l, w, ACT.Ln).then_inc(soft_act[pair], 1)

            def decay(k, unit):
                half, n = unit // STATES, unit % STATES
                g = k * UNITS + unit
                ge(act, h_ready, g - 1)
                if n == 0:
                    act.wait_ge(delta_ready, k * 4 + 2 * half + 2)
                for d in range(HT):
                    last = act.activation(da[:, unit % 2, d, 1:SEG], delta[:, half, d, :], ACT.Exp,
                                          scale=neg_a[:, HT * half + d, n:n + 1])
                last.then_inc(da_ready, 1)

            def save_state(unit):
                half, n = unit // STATES, unit % STATES
                act.activation(state[:, half, n, :].rearrange("p (a b) -> p a b", b=1),
                               dbh[:, unit % HS, :, T:T + 1], ACT.Copy).then_inc(state_saved, 1)

            def square2(c, alone):
                if alone:
                    act.wait_ge(*fin_bank_read(c + 1, MEANS))
                else:
                    act.wait_ge(centred2, c + 1)
                act.activation(sq2, d2[:, :, :], ACT.Square).then_inc(squared2, 1)

            def rstd2(c, alone):
                act.wait_ge(fin_mm, fin_made(c + 1, VARS))
                act.activation(ln2_l[:, :], fin[:, 1, 0:T], ACT.Ln,
                               bias=eps[:, 1:2]).then_inc(fin_read[1] if alone else ln2_log, 1)
                if alone:
                    act.wait_ge(*fin_bank_read(c + 1, VARS))
                else:
                    act.wait_ge(ln2_log, c + 1)
                act.activation(ln2_r[:, :], ln2_l[:, :], ACT.Exp, scale=-0.5).then_inc(ln2_ready, 1)

            def norm1(c):
                square1(c)
                rstd1(c)
                rstd1_again(c)
                affine(c)

            exps = "natural_log_exp_and_others"
            norm1(0)
            for q in range(4):
                take_xin(0, q)
            for q in range(2):
                take_z(0, 0, q)
            silu_u(0, 0)
            take_xd(0, 0)
            take_c(0, 0)
            act.preload_act_table_set(exps)
            for q in range(2):
                for step in range(3):
                    soft(0, q, step)
            for q in range(2, 4):
                take_z(0, 0, q)
            norm1(1)

            soft_at = {23: ((0, 0), (0, 1)), 24: ((0, 2),), 25: ((1, 0), (1, 1)), 26: ((1, 2),)}
            late_at = {0: ((2, 0), (3, 0)), 1: ((2, 1),), 2: ((2, 2),), 3: ((3, 1),), 4: ((3, 2),)}
            z_at = {18: 0, 22: 1, 27: 2, 29: 3}

            def body(k, parity, image):
                scan, prepare, normalize, finish = runs(k)
                for unit in range(UNITS):
                    if scan:
                        decay(k, unit)
                        if unit >= 2:
                            save_state(unit - 2)
                        elif not (isinstance(k, int) and k == 0):
                            save_state(unit + UNITS - 2)
                        for q, step in late_at.get(unit, ()):
                            soft(k, q, step)
                        if unit == 16 and not prepare:
                            silu_z(k, parity)
                    if prepare:
                        if unit in (4, 6, 10, 12):
                            take_xin(k + 1, (4, 6, 10, 12).index(unit))
                        if unit == 16:
                            silu_u(k + 1, 1 - parity)
                            silu_z(k, parity)
                            act.preload_act_table_set(exps)
                        if unit in z_at:
                            take_z(k + 1, 1 - parity, z_at[unit])
                        if unit == 20:
                            take_xd(k + 1, 1 - parity)
                        for q, step in soft_at.get(unit, ()):
                            soft(k + 1, q, step)
                        if unit == 29:
                            take_c(k + 1, 1 - parity)
                    if normalize and unit == 22:
                        square1(k + 2)
                    if finish:
                        if unit == 22:
                            square2(k - 1, not normalize)
                        if unit == 25:
                            rstd2(k - 1, not normalize)
                    if normalize:
                        if unit == 25:
                            rstd1(k + 2)
                        if unit == 28:
                            rstd1_again(k + 2)
                        if unit == 31:
                            affine(k + 2)

            iterations(act, body)

        @block.vector
        def _(dve):
            for i, (dst, value) in enumerate(((eps[:, 0:1], 1e-6), (eps[:, 1:2], 1e-5), (tsum[:, :, :], 0.0),
                                              (da[:, 0, :, 0:1], 0.0), (da[:, 1, :, 0:1], 0.0))):
                dve.memset(dst, value).then_inc(set_dve, 1)
            dve.wait_ge(set_dve, 5)
            dve.memset(t_red[:, :], 0.0).then_inc(set_dve, 1)
            dve.wait_ge(consts_in, 48)

            def centre1(c):
                dve.wait_ge(fin_mm, fin_made(c - 2, MEANS))
                bank = fin_bank(c - 2, MEANS)
                dve.tensor_tensor(x_t[:, :, :], x_t[:, :, :], fin[:, bank:bank + 1, T:2 * T].broadcast_to((P, KT, T)),
                                  ALU.subtract).then_inc(fin_read[bank], 1)

            def var_of_normed(c):
                bank = fin_bank(c - 2, VARS)
                dve.wait_ge(rstd_act, c * 4 + 2)
                dve.tensor_tensor(ln_v[:, :], fin[:, bank, T:2 * T], ln_r1[:, :], ALU.mult).then_inc(fin_read[bank], 1)
                dve.wait_ge(*fin_bank_read(c - 2, VARS))
                dve.tensor_tensor(ln_v[:, :], ln_v[:, :], ln_r1[:, :], ALU.mult).then_inc(rstd_dve, 1)

            def scale1(c):
                dve.wait_ge(rstd_act, c * 4 + 4)
                ge(dve, pre_mm, pre_made(c - 1, Z67))
                dve.tensor_tensor(ln_r2[:, :], ln_r2[:, :], ln_r1[:, :], ALU.mult).then_inc(rstd_dve, 1)
                dve.wait_ge(rstd_dve, c * 3 + 2)
                dve.tensor_tensor(xn[:, :, :], x_t[:, :, :],
                                  ln_r2[:, :].rearrange("p (a t) -> p a t", a=1).broadcast_to((P, KT, T)),
                                  ALU.mult).then_inc(rstd_dve, 1)

            def keep_tail(c, first):
                ge(dve, conv_step, c * 32)
                if first:
                    dve.memset(xin[:, :, 0:TAPS - 1], 0.0).then_inc(tail_kept, 1)
                else:
                    dve.tensor_copy(xin[:, :, 0:TAPS - 1], xin[:, :, T:T + TAPS - 1]).then_inc(tail_kept, 1)

            def conv(c, q):
                dve.wait_ge(*pre_bank_read(c, XIN + q))
                if q == 0:
                    dve.wait_ge(tail_kept, c + 1)
                    ge(dve, u_ready, c)
                    dve.wait_ge(fin_mm, fin_made(c - 2, VARS))
                for j in range(TAPS):
                    for tile in range(2):
                        d = 2 * q + tile
                        acc = cv[:, d, :]
                        w = vec[:, V_CW + d * TAPS + j:V_CW + d * TAPS + j + 1]
                        if j == 0:
                            dve.tensor_scalar(acc, xin[:, d, j:j + T], w, vec[:, V_CB + d:V_CB + d + 1],
                                              ALU.mult, ALU.add).then_inc(conv_step, 1)
                        else:
                            dve.wait_ge(conv_step, c * 32 + q * 8 + 2 * j - 1 + tile)
                            dve.scalar_tensor_tensor(acc, xin[:, d, j:j + T], w, acc, ALU.mult,
                                                     ALU.add).then_inc(conv_step, 1)

            def soften(c, q):
                l = sp_l[:, q % 2, :]
                steps = (c * 4 + q) * 2
                dve.wait_ge(soft_act[q % 2], (c * 2 + q // 2) * 4 + 4)
                dve.scalar_tensor_tensor(l, sp_w[:, q % 2, :], -1.0, l, ALU.add, ALU.subtract).then_inc(soft_dve, 1)
                dve.wait_ge(soft_dve, steps + 1)
                dve.scalar_tensor_tensor(l, l, 0.0, sp_q[:, q % 2, :], ALU.max, ALU.min).then_inc(soft_dve, 1)

            def scan(k, unit):
                g = k * UNITS + unit
                h = dbh[:, unit % HS].rearrange("p a t -> p (a t)")
                dve.wait_ge(da_ready, g + 1)
                dve.wait_ge(db_ready, g + 1)
                dve.tensor_tensor_scan(h, da[:, unit % 2].rearrange("p a t -> p (a t)"), h, 0.0, ALU.mult,
                                       ALU.add).then_inc(h_ready, 1)

            def add_y(k, unit, parity):
                half, n = unit // STATES, unit % STATES
                g = k * UNITS + unit
                if unit == 0:
                    dve.wait_ge(*fin_bank_read(k - 1, TURN_C))
                for ts in range(TS):
                    dve.wait_ge(h_turned, g * 2 + ts + 1)
                    src, acc, cn = h_tok[:, (2 * unit + ts) % 4, :], y_t[:, half, ts, :], c_tok[:, parity, ts, n:n + 1]
                    if n == 0:
                        if ts == 0:
                            if not isinstance(k, int) or k:
                                dve.wait_ge(fin_mm, fin_made(k, TB3) if half else fin_made(k - 1, TB1))
                        dve.tensor_scalar(acc, src, cn, None, ALU.mult).then_inc(y_added, 1)
                    else:
                        dve.wait_ge(y_added, g * 2 + ts - 1)
                        dve.scalar_tensor_tensor(acc, src, cn, acc, ALU.mult, ALU.add).then_inc(y_added, 1)

            def skip(c, parity, j):
                k, group = (c, (TB0, TB1)[j]) if j < 2 else (c + 1, (TB2, TB3)[j - 2])
                dve.wait_ge(fin_mm, fin_made(k, group))
                for tile in range(2):
                    d = 2 * j + tile
                    y = u[:, parity, d, :]
                    last = dve.scalar_tensor_tensor(y, y, vec[:, V_D + d:V_D + d + 1],
                                                    fin[:, group % 2, tile * T:tile * T + T], ALU.mult, ALU.add)
                last.then_inc(fin_read[group % 2], 1)

            def residual(c, i):
                j = (OUT01, OUT23)[i]
                dve.wait_ge(xres_in, (c + 1) * 16)
                dve.wait_ge(fin_mm, fin_made(c + 1, j))
                xr = x2[:, 2 * i:2 * i + 2, :].rearrange("p a t -> p (a t)")
                dve.tensor_tensor(xr, xr, fin[:, j % 2, :], ALU.add).then_inc(fin_read[j % 2], 1)

            def centre2(c, alone):
                dve.wait_ge(fin_mm, fin_made(c + 1, MEANS))
                dve.wait_ge(*fin_bank_read(c + 1, OUT01))
                dve.wait_ge(*fin_bank_read(c + 1, OUT23))
                ge(dve, stored, c * 32)
                dve.tensor_tensor(d2[:, :, :], x2[:, :, :], fin[:, 1:2, 0:T].broadcast_to((P, KT, T)),
                                  ALU.subtract).then_inc(fin_read[1] if alone else centred2, 1)

            def scale2(c):
                dve.wait_ge(ln2_ready, c + 1)
                dve.tensor_tensor(d2[:, :, :], d2[:, :, :],
                                  ln2_r[:, :].rearrange("p (a t) -> p a t", a=1).broadcast_to((P, KT, T)),
                                  ALU.mult).then_inc(tok_step, 1)

            def sum_tokens(c, b):
                dve.wait_ge(tok_step, c * 3 + 1)
                dve.tensor_reduce(t_red[:, :], d2[:, :, :], AX_X, ALU.add).then_inc(tok_step, 1)
                dve.wait_ge(tok_step, c * 3 + 2)
                dve.tensor_tensor(tsum[:, :, b], tsum[:, :, b], t_red[:, :], ALU.add).then_inc(tok_step, 1)

            def norm1(c):
                centre1(c)
                var_of_normed(c)
                scale1(c)

            norm1(0)
            keep_tail(0, True)
            for q in range(4):
                conv(0, q)
            soften(0, 0)
            soften(0, 1)
            norm1(1)

            def body(k, parity, image):
                scans, prepare, normalize, finish = runs(k)
                b = image if not isinstance(k, int) else (k - 1) // CPB
                for unit in range(UNITS):
                    if scans:
                        scan(k, unit)
                        if unit >= 1:
                            add_y(k, unit - 1, parity)
                    if finish:
                        if unit == 0:
                            add_y(k - 1, UNITS - 1, 1 - parity)
                        if unit in (3, 4):
                            skip(k - 1, 1 - parity, unit - 1)
                        if unit in (14, 16):
                            residual(k - 1, (unit - 14) // 2)
                        if unit == 20:
                            centre2(k - 1, not normalize)
                        if unit == 27:
                            scale2(k - 1)
                        if unit == 29:
                            sum_tokens(k - 1, b)
                    if prepare:
                        if unit == 1:
                            keep_tail(k + 1, isinstance(k, int) and (k + 1) % CPB == 0)
                        if unit in (5, 7, 11, 13):
                            conv(k + 1, (5, 7, 11, 13).index(unit))
                        if unit in (26, 28):
                            soften(k + 1, (unit - 26) // 2)
                    if scans:
                        if unit in (6, 8):
                            soften(k, 2 + (unit - 6) // 2)
                        if unit in (23, 26):
                            skip(k, parity, (unit - 23) // 3)
                    if normalize:
                        if unit == 20:
                            centre1(k + 2)
                        if unit == 26:
                            var_of_normed(k + 2)
                        if unit == 29:
                            scale1(k + 2)

            iterations(dve, body)


R_B1, R_RW, R_B2 = 0, FT, FT + KT * PARTS
R_SEL = R_B2 + DIM
R_PW = R_SEL + FT * P
R_REV = R_PW + EXPERTS
R_COLS = R_REV + PARTS + BATCH


def build_experts(nc, tsum, x2_scr, tn_scr, w1_in, w2_in, r_in, ident_in, out):
    with ExitStack() as ctx:
        def sb(name, shape, dt=F32):
            return ctx.enter_context(nc.sbuf_tensor(name, shape, dt))

        def sem(name):
            return ctx.enter_context(nc.semaphore(name))

        w1_hi = sb("w1_hi", [P, KT, FPAD], F32R)
        w1_lo = sb("w1_lo", [P, KT, FPAD], F32R)
        w2_hi = sb("w2_hi", [P, FT, DIM], F32R)
        w2_lo = sb("w2_lo", [P, FT, DIM], F32R)
        raw = sb("raw", [P, 2, TF])
        tn = sb("tn", [P, KT, TF])
        t_hi = sb("t_hi", [P, 2, KT, TF], F32R)
        t_lo = sb("t_lo", [P, 2, KT, TF], F32R)
        x2t = sb("x2t", [P, 2, KT, TF])
        g = sb("g", [P, 2, TF])
        g_hi = sb("g_hi", [P, 2, TF], F32R)
        g_lo = sb("g_lo", [P, 2, TF], F32R)
        wf = sb("wf", [P, FT + KT, BATCH])
        b1 = sb("b1", [P, FT])
        h_ps = ctx.enter_context(nc.psum_tensor("h_ps", [P, 4, TF], F32))
        acc = ctx.enter_context(nc.psum_tensor("acc", [P, KT, TF], F32))
        r_all = x2t[:, :, :, :].rearrange("p a k t -> p (a k t)")

        r_sem, tn_in, raw_read, router_pe, router_dve, router_act, routed = (
            sem("r_sem"), sem("tn_in"), sem("raw_read"), sem("router_pe"), sem("router_dve"),
            sem("router_act"), sem("routed"))
        raw_in = [sem(f"raw_in{i}") for i in range(2)]
        x2_in = [sem(f"x2_in{i}") for i in range(2)]
        out_stored = [sem(f"out_stored{i}") for i in range(2)]
        raw_scaled, split_hi = sem("raw_scaled"), sem("split_hi")
        tok_hi, tok_split = sem("tok_hi"), sem("tok_split")
        h_mm, h_read, g_hi_ready, g_lo_ready, o_mm, acc_read = (
            sem("h_mm"), sem("h_read"), sem("g_hi_ready"), sem("g_lo_ready"), sem("o_mm"), sem("acc_read"))
        last = BATCH * FCPB - 1

        def chunks(eng, body):
            body(0, 0, 0, False, True, False, False)
            with eng.Fori(0, FCPB // 2 - 1) as i:
                body(i * 2 + 1, 1, 0, True, True, False, False)
                body(i * 2 + 2, 0, 0, True, True, False, False)
            body(FCPB - 1, 1, 0, True, True, True, False)
            body(FCPB, 0, 1, True, True, False, True)
            with eng.Fori(0, FCPB // 2 - 1) as i:
                body(i * 2 + FCPB + 1, 1, 1, True, True, False, False)
                body(i * 2 + FCPB + 2, 0, 1, True, True, False, False)
            body(last, 1, 1, True, False, False, False)

        block = ctx.enter_context(nc.Block())

        @block.sync
        def _(sp):
            def chunk_of(dram, b, c):
                t0 = (c - b * FCPB) * TF
                view = dram[b].rearrange("(k p) t -> p k t", p=P)
                return view[:, :, t0:t0 + TF] if isinstance(c, int) else view[:, :, bass.ds(t0, TF)]

            def chunk_at(dram, c):
                return dram[c] if isinstance(c, int) else dram[bass.ds(c, 1)].rearrange("a p k t -> (a p) k t")

            def load_piece(r):
                ge(sp, raw_read, r - 1)
                src = w1_in[:, r // KT, (r % KT) * TF:(r % KT + 1) * TF] if r < FT else w2_in[:, r % FT, :]
                sp.dma_start(raw[:, r % 2, :], src).then_inc(raw_in[r % 2], 16)

            def load_tn(b, c):
                ge(sp, tok_split, c * KT)
                for i in range(TF // T):
                    sp.dma_start(tn[:, :, i * T:i * T + T], chunk_at(tn_scr, 2 * c + i)).then_inc(tn_in, 16)

            def load_x2(b, c, parity):
                ge(sp, out_stored[parity], (c - parity) // 2 * 16 if isinstance(c, int) else (c - parity) * 8)
                for i in range(TF // T):
                    sp.dma_start(x2t[:, parity, :, i * T:i * T + T],
                                 chunk_at(x2_scr, 2 * c + i)).then_inc(x2_in[parity], 16)

            def store(b, c, parity):
                sp.wait_ge(acc_read, (c + 1) * KT)
                sp.dma_start(chunk_of(out, b, c), x2t[:, parity]).then_inc(out_stored[parity], 16)

            sp.dma_start(r_all[:, 0:R_COLS - FT], r_in[:, FT:R_COLS]).then_inc(r_sem, 16)
            sp.dma_start(b1[:, :], r_in[:, R_B1:R_B1 + FT]).then_inc(r_sem, 16)
            load_tn(0, 0)
            for r in range(2 * FT):
                load_piece(r)
            sp.wait_ge(routed, 2)
            load_x2(0, 0, 0)

            def body(c, parity, image, prev, nxt, closing, opening):
                after = image if not isinstance(c, int) else (c + 1) // FCPB
                before = image if not isinstance(c, int) else (c - 1) // FCPB
                if opening:
                    for r in range(3 * FT - 2, 3 * FT):
                        load_piece(r)
                if prev:
                    store(before, c - 1, 1 - parity)
                if nxt:
                    load_tn(after, c + 1)
                    load_x2(after, c + 1, 1 - parity)
                if closing:
                    for r in range(2 * FT, 3 * FT - 2):
                        load_piece(r)

            chunks(sp, body)
            store(1, last, 1)
            sp.wait_ge(out_stored[0], (last + 1) * 8)
            sp.wait_ge(out_stored[1], (last + 1) * 8)

        def table(col, width, rows):
            return r_all[0:rows, col - FT:col - FT + width]

        def small(i, rows=BATCH, cols=PARTS):
            return g[0:rows, 0, 16 * i:16 * i + cols]

        logits, probs, sel1, sel2, mix, hot, rest = (small(i) for i in range(7))
        top, neg_top, total, m1, m2, r1, r2 = (small(7 + i, cols=1) for i in range(7))
        mix_t, w_e = small(14, PARTS, BATCH), small(15, EXPERTS, BATCH)

        @block.tensor
        def _(pe):
            pe.wait_ge(r_sem, 32)
            for kt in range(KT):
                mm = pe.matmul(h_ps[0:BATCH, 0, 0:PARTS], tsum[:, kt, :], table(R_RW + kt * PARTS, PARTS, P),
                               start=kt == 0, stop=kt == KT - 1)
            mm.then_inc(router_pe, 1)
            pe.wait_ge(routed, 1)
            pe.transpose(h_ps[0:PARTS, 1, 0:BATCH], mix, table(R_REV + PARTS, BATCH, BATCH)).then_inc(router_pe, 1)
            pe.wait_ge(router_act, 2)
            pe.matmul(h_ps[0:EXPERTS, 2, 0:BATCH], table(R_PW, EXPERTS, PARTS), mix_t, start=True,
                      stop=True).then_inc(router_pe, 1)
            pe.wait_ge(router_act, 3)
            for f in range(FT):
                pe.matmul(h_ps[:, 3, 2 * f:2 * f + 2], table(R_SEL + f * P, P, EXPERTS), w_e, start=True, stop=True)
            for m in range(KT):
                mm = pe.matmul(h_ps[:, 3, 2 * (FT + m):2 * (FT + m) + 2], table(R_B2 + m * P, P, EXPERTS), w_e,
                               start=True, stop=True)
            mm.then_inc(router_pe, 1)
            pe.wait_ge(raw_read, FT)
            pe.wait_ge(routed, 2)

            def hidden(c, parity, f):
                ge(pe, h_read, c * FT + f - 3)
                if f == 0:
                    pe.wait_ge(tok_split, (c + 1) * KT)
                cols = slice(f * P, f * P + P)
                terms = [(w, t, kt) for w, t in ((w1_hi, t_hi), (w1_lo, t_hi), (w1_hi, t_lo)) for kt in range(KT)]
                for i, (w, t, kt) in enumerate(terms):
                    mm = pe.matmul(h_ps[:, f % 4, :], w[:, kt, cols], t[:, parity, kt, :], start=i == 0,
                                   stop=i == len(terms) - 1)
                mm.then_inc(h_mm, 1)

            def project(c, image, f):
                pe.wait_ge(g_lo_ready, c * FT + f + 1)
                pe.wait_ge(raw_read, (image + 1) * FT + f + 1)
                for m in range(KT):
                    if f == 0:
                        ge(pe, acc_read, (c - 1) * KT + m + 1)
                    cols = slice(m * P, m * P + P)
                    for i, (w, t) in enumerate(((w2_hi, g_hi), (w2_lo, g_hi), (w2_hi, g_lo))):
                        mm = pe.matmul(acc[:, m, :], w[:, f, cols], t[:, f % 2, :], start=f == 0 and i == 0,
                                       stop=f == FT - 1 and i == 2)
                mm.then_inc(o_mm, 1)

            def body(c, parity, image, prev, nxt, closing, opening):
                before = image if not isinstance(c, int) else (c - 1) // FCPB
                for f in range(FT):
                    hidden(c, parity, f)
                    if f:
                        project(c, image, f - 1)
                    elif prev:
                        project(c - 1, before, FT - 1)

            chunks(pe, body)
            project(last, 1, FT - 1)

        @block.scalar
        def _(act):
            act.wait_ge(router_dve, 3)
            act.activation(probs, logits, ACT.Exp, bias=neg_top).then_inc(router_act, 1)
            act.wait_ge(router_pe, 2)
            act.activation(mix_t, h_ps[0:PARTS, 1, 0:BATCH], ACT.Copy).then_inc(router_act, 1)
            act.wait_ge(router_dve, 20)
            act.activation(w_e, small(16, EXPERTS, BATCH), ACT.Copy).then_inc(router_act, 1)
            act.wait_ge(routed, 2)
            act.preload_act_table_set("gelu_and_others")

            def gelu(c, f):
                ge(act, g_lo_ready, c * FT + f - 1)
                act.wait_ge(h_mm, c * FT + f + 1)
                act.activation(g[:, f % 2, :], h_ps[:, f % 4, :], ACT.Gelu, bias=b1[:, f:f + 1]).then_inc(h_read, 1)
                ge(act, o_mm, c * FT + f - 1)
                act.wait_ge(h_read, c * FT + f + 1)
                act.activation(g_hi[:, f % 2, :], g[:, f % 2, :], ACT.Copy).then_inc(g_hi_ready, 1)

            def body(c, parity, image, prev, nxt, closing, opening):
                for f in range(FT):
                    gelu(c, f)

            chunks(act, body)

        @block.vector
        def _(dve):
            steps = [0]

            def step(ins):
                steps[0] += 1
                ins.then_inc(router_dve, 1)
                dve.wait_ge(router_dve, steps[0])

            dve.wait_ge(router_pe, 1)
            rev = table(R_REV, PARTS, BATCH)
            step(dve.tensor_scalar(logits, h_ps[0:BATCH, 0, 0:PARTS], 1.0 / TOKENS, None, ALU.mult))
            step(dve.tensor_reduce(top, logits, AX_X, ALU.max))
            step(dve.tensor_scalar(neg_top, top, -1.0, None, ALU.mult))
            dve.wait_ge(router_act, 1)
            step(dve.tensor_reduce(total, probs, AX_X, ALU.add))
            step(dve.reciprocal(total, total))
            step(dve.tensor_scalar(probs, probs, total, None, ALU.mult))
            step(dve.tensor_reduce(m1, probs, AX_X, ALU.max))
            step(dve.scalar_tensor_tensor(hot, probs, m1, rev, ALU.is_equal, ALU.mult))
            step(dve.tensor_reduce(r1, hot, AX_X, ALU.max))
            step(dve.tensor_scalar(sel1, rev, r1, None, ALU.is_equal))
            step(dve.scalar_tensor_tensor(rest, sel1, -2.0, probs, ALU.mult, ALU.add))
            step(dve.tensor_reduce(m2, rest, AX_X, ALU.max))
            step(dve.scalar_tensor_tensor(hot, rest, m2, rev, ALU.is_equal, ALU.mult))
            step(dve.tensor_reduce(r2, hot, AX_X, ALU.max))
            step(dve.tensor_scalar(sel2, rev, r2, m2, ALU.is_equal, ALU.mult))
            step(dve.scalar_tensor_tensor(mix, sel1, m1, sel2, ALU.mult, ALU.add))
            step(dve.tensor_tensor(m1, m1, m2, ALU.add))
            step(dve.reciprocal(m1, m1))
            dve.tensor_scalar(mix, mix, m1, None, ALU.mult).then_inc(routed, 1)
            dve.wait_ge(router_pe, 3)
            raw_w = small(17, EXPERTS, BATCH)
            step(dve.tensor_copy(raw_w, h_ps[0:EXPERTS, 2, 0:BATCH]))
            step(dve.scalar_tensor_tensor(small(16, EXPERTS, BATCH), raw_w, 1e-6, raw_w, ALU.is_gt, ALU.mult))
            assert steps[0] == 20
            dve.wait_ge(router_pe, 4)
            dve.tensor_copy(wf[:, :, :], h_ps[:, 3, 0:2 * (FT + KT)].rearrange("p (f b) -> p f b", b=2))\
               .then_inc(routed, 1)

            def split_w1(r):
                kt, col = r // KT, (r % KT) * TF
                hi, lo = w1_hi[:, kt, col:col + TF], w1_lo[:, kt, col:col + TF]
                dve.wait_ge(raw_in[r % 2], (r // 2 + 1) * 16)
                dve.tensor_copy(hi, raw[:, r % 2, :]).then_inc(split_hi, 1)
                dve.wait_ge(split_hi, r + 1)
                dve.tensor_tensor(lo, raw[:, r % 2, :], hi, ALU.subtract).then_inc(raw_read, 1)

            def split_w2(image, f):
                r = FT * (1 + image) + f
                slot = raw[:, r % 2, :]
                dve.wait_ge(raw_in[r % 2], (r // 2 + 1) * 16)
                ge(dve, o_mm, (image * FCPB - 1) * FT + f + 1)
                dve.tensor_scalar(slot, slot, wf[:, f, image:image + 1], None, ALU.mult).then_inc(raw_scaled, 1)
                dve.wait_ge(raw_scaled, image * FT + f + 1)
                dve.tensor_copy(w2_hi[:, f, :], slot).then_inc(split_hi, 1)
                dve.wait_ge(split_hi, r + 1)
                dve.tensor_tensor(w2_lo[:, f, :], slot, w2_hi[:, f, :], ALU.subtract).then_inc(raw_read, 1)

            def split_tokens(c, parity, kt):
                if kt == 0:
                    ge(dve, h_mm, (c - 1) * FT)
                    dve.wait_ge(tn_in, (c + 1) * 32)
                dve.tensor_copy(t_hi[:, parity, kt, :], tn[:, kt, :]).then_inc(tok_hi, 1)
                dve.wait_ge(tok_hi, c * KT + kt + 1)
                dve.tensor_tensor(t_lo[:, parity, kt, :], tn[:, kt, :], t_hi[:, parity, kt, :],
                                  ALU.subtract).then_inc(tok_split, 1)

            def low_half(c, f):
                dve.wait_ge(g_hi_ready, c * FT + f + 1)
                dve.tensor_tensor(g_lo[:, f % 2, :], g[:, f % 2, :], g_hi[:, f % 2, :],
                                  ALU.subtract).then_inc(g_lo_ready, 1)

            def drain(c, parity, image, m):
                if m == 0:
                    dve.wait_ge(o_mm, (c + 1) * FT)
                    dve.wait_ge(x2_in[parity], (c - parity) * 16 + 32)
                x = x2t[:, parity, m, :]
                dve.scalar_tensor_tensor(x, acc[:, m, :], wf[:, FT + m, image:image + 1], x, ALU.add,
                                         ALU.add).then_inc(acc_read, 1)

            for r in range(FT):
                split_w1(r)
            dve.wait_ge(routed, 2)
            for kt in range(KT):
                split_tokens(0, 0, kt)
            for f in range(FT):
                split_w2(0, f)

            def body(c, parity, image, prev, nxt, closing, opening):
                before = image if not isinstance(c, int) else (c - 1) // FCPB
                for f in range(FT):
                    low_half(c, f)
                    if f == 1 and prev:
                        for m in range(KT):
                            drain(c - 1, 1 - parity, before, m)
                    if 4 <= f < 4 + KT and nxt:
                        split_tokens(c + 1, 1 - parity, f - 4)
                    if closing and f >= 2:
                        split_w2(1, f - 2)
                    if opening and f < 2:
                        split_w2(1, FT - 2 + f)

            chunks(dve, body)
            for m in range(KT):
                drain(last, 1, 1, m)


def build(nc, x, vecs, ident, mean_w, wi, wo, wx, wdt, w1, w2, router, out):
    b_scr = nc.dram_tensor("b_scr", (CHUNKS, STATES, T), F32, kind="Internal").ap()
    x2_scr = nc.dram_tensor("x2_scr", (CHUNKS, P, KT, T), F32, kind="Internal").ap()
    tn_scr = nc.dram_tensor("tn_scr", (CHUNKS, P, KT, T), F32, kind="Internal").ap()
    with nc.sbuf_tensor("tsum", [P, KT, BATCH], F32) as tsum:
        build_mixer(nc, x, vecs, ident, mean_w, wi, wo, wx, wdt, tsum, b_scr, x2_scr, tn_scr)
        build_experts(nc, tsum, x2_scr, tn_scr, w1, w2, router, ident, out)


def kernel(x, L0_conv_ln_w, L0_conv_ln_b, L0_conv_in_proj_w, L0_conv_conv_w, L0_conv_conv_b, L0_conv_x_proj_w,
           L0_conv_dt_proj_w, L0_conv_dt_proj_b, L0_conv_A_log, L0_conv_D_skip, L0_conv_out_proj_w,
           L0_ffn_router_w, L0_ffn_W1, L0_ffn_b1, L0_ffn_W2, L0_ffn_b2):
    import concourse.bacc as bacc
    from concourse.bass_utils import run_bass_kernel_spmd

    f32 = np.float32

    def tiles(a, rows):
        a = np.asarray(a, f32)
        return np.ascontiguousarray(a.reshape(rows // P, P, -1).transpose(1, 0, 2))

    xb = np.zeros((P, 1), f32)
    xb[ONE_ROW] = 1.0
    vecs = np.concatenate([tiles(L0_conv_ln_w, DIM).reshape(P, -1), tiles(L0_conv_ln_b, DIM).reshape(P, -1),
                           tiles(L0_conv_conv_w, INNER).reshape(P, -1), tiles(L0_conv_conv_b, INNER).reshape(P, -1),
                           tiles(L0_conv_D_skip, INNER).reshape(P, -1), tiles(L0_conv_A_log, INNER).reshape(P, -1),
                           xb], axis=1)
    xp = np.asarray(L0_conv_x_proj_w, f32)
    wx = np.zeros((INNER, XR), f32)
    wx[:, 0:RANK] = xp[0:RANK].T
    wx[:, B_ROW:B_ROW + STATES] = xp[RANK:RANK + STATES].T
    wx[:, C_ROW:C_ROW + STATES] = xp[RANK + STATES:].T
    wdt = np.concatenate([np.asarray(L0_conv_dt_proj_w, f32).T, np.asarray(L0_conv_dt_proj_b, f32)[None]], axis=0)
    w1 = np.zeros((DIM, FPAD), f32)
    w1[:, :EXPERTS * HIDDEN] = np.asarray(L0_ffn_W1, f32).transpose(1, 0, 2).reshape(DIM, -1)
    w2 = np.zeros((FPAD, DIM), f32)
    w2[:EXPERTS * HIDDEN] = np.asarray(L0_ffn_W2, f32).reshape(-1, DIM)
    b1 = np.zeros((FPAD, 1), f32)
    b1[:EXPERTS * HIDDEN, 0] = np.asarray(L0_ffn_b1, f32).reshape(-1)

    partitions = [(6,), (5, 1), (4, 2), (4, 1, 1), (3, 3), (3, 2, 1), (3, 1, 1, 1), (2, 2, 2), (2, 2, 1, 1),
                  (2, 1, 1, 1, 1), (1, 1, 1, 1, 1, 1)]
    router = np.zeros((P, R_COLS), f32)
    router[:, R_B1:R_B1 + FT] = tiles(b1, FPAD).reshape(P, -1)
    router[:, R_RW:R_RW + KT * PARTS] = tiles(np.asarray(L0_ffn_router_w, f32).T, DIM).reshape(P, -1)
    router[0:EXPERTS, R_B2:R_B2 + DIM] = np.asarray(L0_ffn_b2, f32)
    for e in range(EXPERTS):
        router[e, R_SEL + e * HIDDEN:R_SEL + (e + 1) * HIDDEN] = 1.0
    for i, parts in enumerate(partitions):
        for j, part in enumerate(parts):
            router[i, R_PW + j] = f32(part / 6)
    router[0:BATCH, R_REV:R_REV + PARTS] = np.arange(PARTS, 0, -1, dtype=f32)
    router[0:BATCH, R_REV + PARTS:R_REV + PARTS + BATCH] = np.eye(BATCH, dtype=f32)

    arrays = {
        "x": np.ascontiguousarray(np.asarray(x, f32).reshape(BATCH, KT, P, CPB, T).transpose(0, 3, 2, 1, 4)
                                  .reshape(CHUNKS, P, KT, T)), "vecs": vecs,
        "ident": np.eye(P, dtype=f32), "mean_w": np.full((P, P), 1.0 / DIM, f32),
        "wi": tiles(np.asarray(L0_conv_in_proj_w, f32).T, DIM), "wo": tiles(np.asarray(L0_conv_out_proj_w, f32).T, INNER),
        "wx": tiles(wx, INNER), "wdt": np.ascontiguousarray(wdt), "w1": tiles(w1, DIM), "w2": tiles(w2, FPAD),
        "router": router,
    }
    nc = bacc.Bacc("TRN2", target_bir_lowering=False, num_devices=1)
    args = [nc.dram_tensor("in_" + name, a.shape, F32, kind="ExternalInput").ap() for name, a in arrays.items()]
    out = nc.dram_tensor("out", (BATCH, DIM, TOKENS), F32, kind="ExternalOutput").ap()
    build(nc, *args, out)
    r = run_bass_kernel_spmd(nc, [{"in_" + name: a for name, a in arrays.items()}], core_ids=[0])
    return r.results[0]["out"].reshape(BATCH, DIM, 64, 64)
```

```python
from contextlib import ExitStack

import numpy as np

import concourse.bass as bass
from concourse import mybir

P = 128
BATCH, DIM, TOKENS = 2, 512, 4096
INNER, STATES, TAPS, RANK = 1024, 16, 4, 32
EXPERTS, HIDDEN, PARTS = 6, 341, 11
KT = DIM // P
DT = INNER // P
HT = DT // 2
T = 256
TS = T // P
CPB = TOKENS // T
CHUNKS = BATCH * CPB
UNITS = 2 * STATES
XR = 96
ONE_ROW, C_ROW, B_ROW = 32, 64, 80
SEG = T + 1
HS = 4
DS = 4
LAG = 2
SAVE_LAGS = {15: (), 16: (3,), 17: (3, 2)}
BP = 2
TF = 512
FCPB = TOKENS // TF
FT = 16
FPAD = FT * P
RS = 4

F32 = mybir.dt.float32
F32R = mybir.dt.float32r
ACT = mybir.ActivationFunctionType
ALU = mybir.AluOpType
AX_X = mybir.AxisListType.X

V_LNW, V_LNB, V_CW, V_CB, V_D, V_AL, V_XB = 0, 4, 8, 40, 48, 56, 184
V_COLS = 185

CHANNEL_EPS, EPS = 1e-6, 1e-5
HALF_ROOT = 0.5 ** 0.5
XIN, Z01, DT0, DT1, Z23, Z45, Z67, DT2, DT3 = 0, 4, 5, 6, 7, 8, 9, 10, 11
PRE = 12
Z_GROUP = (Z01, Z23, Z45, Z67)
DT_GROUP = (DT0, DT1, DT2, DT3)
TB2, TB3, OUT01, OUT23, X_PROJ, MEANS, TB0, VARS, TB1, TURN_C = range(10)
FIN = 10


def ge(eng, sem, value):
    if isinstance(value, int) and value <= 0:
        return
    eng.wait_ge(sem, value)


def build_mixer(nc, w_in, w1_in, w1_loaded, x, vecs, ident_in, mean_in, wi_in, wo_in, wx_in, wdt_in, tsum, b_scr,
                x2_scr, tn_scr):
    with ExitStack() as ctx:
        def sb(name, shape, dt=F32):
            return ctx.enter_context(nc.sbuf_tensor(name, shape, dt))

        def sem(name):
            return ctx.enter_context(nc.semaphore(name))

        w_out = sb("w_out", [P, DT, DIM])
        w_x = sb("w_x", [P, DT, XR])
        w_dt = sb("w_dt", [RANK + 1, INNER])
        vec = sb("vec", [P, V_COLS])
        ident = sb("ident", [P, P])
        mean_w = sb("mean_w", [P, P])
        diag_d = sb("diag_d", [P, DT, P])
        neg_a = sb("neg_a", [P, DT, STATES])
        eps = sb("eps", [P, 2])
        x_t = sb("x_t", [P, KT, T])
        xn = sb("xn", [P, KT, T])
        cv = sb("cv", [P, DT, T])
        sq, sq2 = cv[:, 0:KT, :], cv[:, KT:2 * KT, :]
        ln_l = sb("ln_l", [P, T])
        ln_r1 = sb("ln_r1", [P, T])
        xin = sb("xin", [P, DT, TAPS - 1 + T])
        u = sb("u", [P, 2, DT, T])
        zs = sb("zs", [P, 2, DT, T])
        xd = sb("xd", [XR, 2, T])
        sp_t = sb("sp_t", [P, 2, 2 * T])
        sp_l = sb("sp_l", [P, 2, 2 * T])
        sp_w = sb("sp_w", [P, 2, 2 * T])
        sp_q = sb("sp_q", [P, 2, 2 * T])
        delta = sb("delta", [P, 2, HT, T])
        du = sb("du", [P, HT, T])
        b_rep = sb("b_rep", [P, BP, 2, T])
        c_tok = sb("c_tok", [P, 2, TS, STATES])
        da = sb("da", [P, DS, HT, SEG])
        dbh = sb("dbh", [P, HS, HT, SEG])
        state = sb("state", [P, 2, STATES, HT])
        y_t = sb("y_t", [P, 2, TS, HT * P])
        x2 = sb("x2", [P, KT, T])
        d2 = sb("d2", [P, KT, T])
        ln2_l = sb("ln2_l", [P, T])
        ln2_r = sb("ln2_r", [P, T])
        t_red = sb("t_red", [P, KT])

        h_tok = ctx.enter_context(nc.psum_tensor("h_tok", [P, 4, HT * P], F32))
        pre = ctx.enter_context(nc.psum_tensor("pre", [P, 2, 2 * T], F32))
        fin = ctx.enter_context(nc.psum_tensor("fin", [P, 2, 2 * T], F32))

        consts_in, wi_sem, wrest_in = sem("consts_in"), sem("wi_sem"), sem("wrest_in")
        set_dve, set_act = sem("set_dve"), sem("set_act")
        x_in, xres_in, stored = sem("x_in"), sem("xres_in"), sem("stored")
        b_stored = sem("b_stored")
        b_in = [sem(f"b_in{i}") for i in range(BP)]
        pre_mm, fin_mm = sem("pre_mm"), sem("fin_mm")
        pre_read = [sem(f"pre_read{i}") for i in range(2)]
        fin_read = [sem(f"fin_read{i}") for i in range(2)]
        squared, rstd_act, x_scaled, xn_ready = sem("squared"), sem("rstd_act"), sem("x_scaled"), sem("xn_ready")
        centred2, ln2_log = sem("centred2"), sem("ln2_log")
        tail_kept, conv_step, u_ready = sem("tail_kept"), sem("conv_step"), sem("u_ready")
        soft_act = [sem(f"soft_act{i}") for i in range(2)]
        soft_dve, soft_pool, delta_ready = sem("soft_dve"), sem("soft_pool"), sem("delta_ready")
        z_ready, du_ready = sem("z_ready"), sem("du_ready")
        da_ready, db_ready, h_ready, h_turned, y_added, state_saved = (
            sem("da_ready"), sem("db_ready"), sem("h_ready"), sem("h_turned"), sem("y_added"), sem("state_saved"))
        y_gated = sem("y_gated")
        squared2, ln2_ready, tok_step = sem("squared2"), sem("ln2_ready"), sem("tok_step")

        def pre_made(c, j):
            return c * PRE + j + 1

        def pre_bank_read(c, j):
            return pre_read[j % 2], c * (PRE // 2) + j // 2 + 1

        def absent(k):
            if not isinstance(k, int):
                return ()
            return (CHUNKS - 1, X_PROJ), (CHUNKS - 1, TURN_C), (CHUNKS, X_PROJ), (CHUNKS, TB0)

        def fin_made(k, j):
            if isinstance(k, int) and k < 0:
                return {(-2, MEANS): 1, (-2, VARS): 2, (-1, X_PROJ): 3, (-1, TURN_C): 4, (-1, MEANS): 5,
                        (-1, VARS): 6}[k, j]
            return k * FIN + j + 3 - sum(a < (k, j) for a in absent(k))

        def fin_bank(k, j):
            return (fin_made(k, j) - 1) % 2 if isinstance(k, int) and k < 0 else j % 2

        def fin_bank_read(k, j):
            if isinstance(k, int) and k < 0:
                return fin_read[fin_bank(k, j)], (fin_made(k, j) + 1) // 2
            return (fin_read[j % 2],
                    k * (FIN // 2) + j // 2 + 2 - sum(a < (k, j) and a[1] % 2 == j % 2 for a in absent(k)))

        def iterations(eng, body):
            for k in range(2):
                body(k, k, 0)
            with eng.Fori(0, CPB // 2 - 2) as i:
                body(i * 2 + 2, 0, 0)
                body(i * 2 + 3, 1, 0)
            for k in range(CPB - 2, CPB + 1):
                body(k, k % 2, 0)
            with eng.Fori(0, CPB // 2 - 2) as i:
                body(i * 2 + CPB + 1, 1, 1)
                body(i * 2 + CPB + 2, 0, 1)
            for k in range(CHUNKS - 3, CHUNKS + 1):
                body(k, k % 2, 1)

        def runs(k):
            if not isinstance(k, int):
                return True, True, True, True
            return k < CHUNKS, k + 1 < CHUNKS, k + 2 < CHUNKS, k >= 1

        block = ctx.enter_context(nc.Block())

        @block.sync
        def _(sp):
            sp.dma_start(vec[:, :], vecs).then_inc(consts_in, 16)
            sp.dma_start(mean_w[:, :], mean_in).then_inc(consts_in, 16)
            sp.dma_start(ident[:, :], ident_in).then_inc(consts_in, 16)

            def chunk_at(dram, c):
                return dram[c] if isinstance(c, int) else dram[bass.ds(c, 1)].rearrange("a p k t -> (a p) k t")

            def load_x(c):
                ge(sp, x_scaled, c)
                sp.dma_start(x_t[:, :, :], chunk_at(x, c)).then_inc(x_in, 16)

            def load_residual(c):
                ge(sp, stored, c * 32)
                sp.dma_start(x2[:, :, :], chunk_at(x, c)).then_inc(xres_in, 16)

            def store_x2(c):
                sp.wait_ge(tok_step, c * 2 + 1)
                sp.dma_start(chunk_at(x2_scr, c), x2[:, :, :]).then_inc(stored, 16)

            def store_tn(c):
                sp.dma_start(chunk_at(tn_scr, c), d2[:, :, :]).then_inc(stored, 16)

            def b_rows(c):
                return b_scr[c] if isinstance(c, int) else b_scr[bass.ds(c, 1)].rearrange("a n t -> (a n) t")

            def store_b(c, parity):
                sp.wait_ge(*fin_bank_read(c - 1, X_PROJ))
                sp.dma_start(b_rows(c), xd[B_ROW:B_ROW + STATES, parity, :]).then_inc(b_stored, 16)

            def load_b_piece(c, p):
                if p == 0:
                    sp.wait_ge(b_stored, (c + 1) * 16)
                else:
                    ge(sp, db_ready, c * UNITS + 2 * p - 2)
                n = 2 * p % STATES
                rows = b_rows(c)[n:n + 2, :]
                src = bass.AP(tensor=rows.tensor, offset=rows.offset, ap=[[0, P]] + list(rows.ap))
                sp.dma_start(b_rep[:, p % BP], src).then_inc(b_in[p % BP], 16)

            load_x(0)
            sp.dma_start(w_in[:, :, :], wi_in).then_inc(wi_sem, 16)
            sp.dma_start(w_x[:, :, :], wx_in).then_inc(wrest_in, 16)
            sp.dma_start(w_dt[:, :], wdt_in).then_inc(wrest_in, 16)
            sp.dma_start(w_out[:, :, :], wo_in).then_inc(wrest_in, 16)
            load_x(1)
            store_b(0, 0)

            def body(k, parity, image):
                scan, prepare, normalize, finish = runs(k)
                for p in range(UNITS // 2):
                    if scan:
                        load_b_piece(k, p)
                    if p == 1 and normalize:
                        load_x(k + 2)
                    if p == 2 and finish:
                        load_residual(k - 1)
                    if p == 2 and not scan:
                        sp.wait_ge(pre_mm, pre_made(CHUNKS - 1, Z67))
                        sp.dma_start(w_in[:, :, :], w1_in).then_inc(w1_loaded, 16)
                    if p == 12 and prepare:
                        store_b(k + 1, 1 - parity)
                if finish:
                    store_x2(k - 1)
                if prepare:
                    sp.wait_ge(db_ready, k * UNITS + UNITS - 2)
                if finish:
                    store_tn(k - 1)

            iterations(sp, body)
            sp.wait_ge(stored, CHUNKS * 32)

        @block.gpsimd
        def _(pool):
            def soften(c, q, step):
                half, pair = q // 2, q % 2
                d = delta[:, half, 2 * pair:2 * pair + 2, :].rearrange("p a t -> p (a t)")
                if step == 0:
                    pool.wait_ge(soft_act[pair], (c * 2 + half) * 4 + 2)
                    pool.tensor_tensor(d, d, sp_t[:, q % 2, :], ALU.add).then_inc(soft_pool, 1)
                else:
                    pool.wait_ge(soft_pool, c * 4 + q + 1)
                    pool.wait_ge(soft_dve, (c * 4 + q) * 2 + 2)
                    pool.tensor_tensor(d, d, sp_l[:, q % 2, :], ALU.subtract).then_inc(delta_ready, 1)

            def make_du(c, parity, half):
                ge(pool, db_ready, c * UNITS + STATES * half)
                pool.wait_ge(delta_ready, c * 4 + 2 * half + 2)
                pool.wait_ge(u_ready, c + 1)
                pool.tensor_tensor(du[:, :, :], delta[:, half], u[:, parity, HT * half:HT * half + HT, :],
                                   ALU.mult).then_inc(du_ready, 1)

            def gate(c, parity, j):
                k, group = (c, (TB0, TB1)[j]) if j < 2 else (c + 1, (TB2, TB3)[j - 2])
                pool.wait_ge(*fin_bank_read(k, group))
                if j == 0:
                    pool.wait_ge(z_ready, c + 1)
                y = u[:, parity, 2 * j:2 * j + 2, :]
                pool.tensor_tensor(y, y, zs[:, parity, 2 * j:2 * j + 2, :], ALU.mult).then_inc(y_gated, 1)

            def inject(k, unit, first):
                half, n = unit // STATES, unit % STATES
                g = k * UNITS + unit
                slot = dbh[:, unit % HS]
                ge(pool, h_turned, g * 2 - 6)
                ge(pool, state_saved, g - 3)
                if n == 0:
                    pool.wait_ge(du_ready, k * 2 + half + 1)
                if n % 2 == 0:
                    pool.wait_ge(b_in[(unit // 2) % BP], (k * (UNITS // 2 // BP) + unit // 2 // BP + 1) * 16)
                rep = b_rep[:, (unit // 2) % BP, n % 2:n % 2 + 1, :].broadcast_to((P, HT, T))
                pool.tensor_tensor(slot[:, :, 1:SEG], du[:, :, :], rep, ALU.mult)
                if first:
                    pool.memset(slot[:, :, 0:1], 0.0).then_inc(db_ready, 1)
                else:
                    pool.tensor_copy(slot[:, :, 0:1], state[:, half, n, :].rearrange("p (a b) -> p a b", b=1))\
                        .then_inc(db_ready, 1)

            for q in range(2):
                soften(0, q, 0)
                soften(0, q, 1)

            def body(k, parity, image):
                scan, prepare, normalize, finish = runs(k)
                for unit in range(UNITS):
                    if scan:
                        if unit % STATES == 0:
                            make_du(k, parity, unit // STATES)
                        inject(k, unit, isinstance(k, int) and k % CPB == 0)
                        if unit in (9, 12):
                            soften(k, unit // 3 - 1, 0)
                        if unit in (10, 14):
                            soften(k, unit // 4, 1)
                        if unit == 28:
                            gate(k, parity, 0)
                    if finish:
                        if unit == 1:
                            gate(k - 1, 1 - parity, 1)
                        if unit in (7, 8):
                            gate(k - 1, 1 - parity, unit - 5)
                    if prepare:
                        if unit in (27, 29):
                            soften(k + 1, (unit - 27) // 2, 0)
                        if unit in (28, 31):
                            soften(k + 1, (unit - 28) // 3, 1)

            iterations(pool, body)

        @block.tensor
        def _(pe):
            def pre_free(c, j):
                s, count = pre_bank_read(c, j)
                ge(pe, s, count - 1)
                return pre[:, j % 2, :]

            def fin_free(k, j):
                s, count = fin_bank_read(k, j)
                ge(pe, s, count - 1)
                return fin[:, fin_bank(k, j), :]

            def token_mean(dst, src, last):
                for kt in range(KT):
                    mm = pe.matmul(dst, mean_w[:, :], src[:, kt, :], start=kt == 0, stop=kt == KT - 1)
                if last:
                    mm.then_inc(fin_mm, 1)

            def means(k, finish, normalize):
                bank = fin_free(k, MEANS)
                if finish:
                    pe.wait_ge(*fin_bank_read(k, OUT01))
                    pe.wait_ge(*fin_bank_read(k, OUT23))
                    token_mean(bank[:, 0:T], x2, not normalize)
                if normalize:
                    pe.wait_ge(x_in, (k + 3) * 16)
                    token_mean(bank[:, T:2 * T], x_t, True)

            def variances(k, finish, normalize, chunk):
                bank = fin_free(k, VARS) if chunk == 2 or not finish else fin[:, fin_bank(k, VARS), :]
                if chunk == 2:
                    pe.wait_ge(squared2, k)
                    token_mean(bank[:, 0:T], sq2, not normalize)
                else:
                    pe.wait_ge(squared, k + 3)
                    token_mean(bank[:, T:2 * T], sq, True)

            def in_tile(c, m):
                j, tile = XIN + m // 2 if m < DT else Z_GROUP[(m - DT) // 2], m % 2
                bank = pre[:, j % 2, :] if tile else pre_free(c, j)
                pe.wait_ge(xn_ready, c + 1)
                for kt in range(KT):
                    mm = pe.matmul(bank[:, tile * T:tile * T + T], w_in[:, kt, m * P:m * P + P], xn[:, kt, :],
                                   start=kt == 0, stop=kt == KT - 1)
                if tile == 1:
                    mm.then_inc(pre_mm, 1)

            def x_proj(c, parity, half):
                bank = fin[:, fin_bank(c - 1, X_PROJ), :] if half else fin_free(c - 1, X_PROJ)
                pe.wait_ge(u_ready, c + 1)
                for d in range(HT * half, HT * half + HT):
                    mm = pe.matmul(bank[0:XR, 0:T], w_x[:, d, :], u[:, parity, d, :], start=d == 0, stop=d == DT - 1)
                if half:
                    mm.then_inc(fin_mm, 1)

            def turn_c(c, parity):
                bank = fin_free(c - 1, TURN_C)
                pe.wait_ge(*fin_bank_read(c - 1, X_PROJ))
                for ts in range(TS):
                    mm = pe.transpose(bank[:, ts * XR:ts * XR + XR], xd[:, parity, ts * P:ts * P + P],
                                      ident[0:XR, 0:XR])
                mm.then_inc(fin_mm, 1)

            def dt_pair(c, parity, q):
                bank = pre_free(c, DT_GROUP[q])
                pe.wait_ge(*fin_bank_read(c - 1, X_PROJ))
                for tile in range(2):
                    m = 2 * q + tile
                    mm = pe.matmul(bank[:, tile * T:tile * T + T], w_dt[:, m * P:m * P + P],
                                   xd[0:RANK + 1, parity, :], start=True, stop=True)
                mm.then_inc(pre_mm, 1)

            def turn_h(k, unit):
                g = k * UNITS + unit
                pe.wait_ge(h_ready, g + 1)
                for ts in range(TS):
                    ge(pe, y_added, g * 2 + ts - 3)
                    for d in range(HT):
                        mm = pe.transpose(h_tok[:, (2 * unit + ts) % 4, d * P:d * P + P],
                                          dbh[:, unit % HS, d, 1 + ts * P:1 + ts * P + P], ident[:, :])
                    mm.then_inc(h_turned, 1)

            def turn_back(c, parity, j):
                half, pair = j // 2, j % 2
                bank = fin_free(c, (TB0, TB1)[j]) if j < 2 else fin_free(c + 1, (TB2, TB3)[j - 2])
                for tile in range(2):
                    pe.matmul(bank[:, tile * T:tile * T + T], diag_d[:, 2 * j + tile, :], u[:, parity, 2 * j + tile, :],
                              start=tile == 0, stop=False)
                pe.wait_ge(y_added, (c * UNITS + STATES * (half + 1)) * 2)
                for tile in range(2):
                    for ts in range(TS):
                        mm = pe.matmul(bank[:, tile * T + ts * P:tile * T + ts * P + P],
                                       y_t[:, half, ts, (2 * pair + tile) * P:(2 * pair + tile + 1) * P], ident[:, :],
                                       start=False, stop=tile == 1 and ts == TS - 1)
                mm.then_inc(fin_mm, 1)

            def out_tile(c, parity, m, half):
                j = OUT01 if m < 2 else OUT23
                bank = fin_free(c + 1, j) if m % 2 == 0 and half == 0 else fin[:, j % 2, :]
                pe.wait_ge(y_gated, c * 4 + 2 * half + 2)
                for d in range(HT * half, HT * half + HT):
                    mm = pe.matmul(bank[:, (m % 2) * T:(m % 2) * T + T], w_out[:, d, m * P:m * P + P],
                                   u[:, parity, d, :], start=m % 2 == 0 and d == 0,
                                   stop=m % 2 == 1 and d == DT - 1)
                if m % 2 == 1 and half:
                    mm.then_inc(fin_mm, 1)

            pe.wait_ge(consts_in, 48)
            pe.wait_ge(set_dve, 4 + DS + DT)
            means(-2, False, True)
            variances(-2, False, True, 1)
            pe.wait_ge(wi_sem, 16)
            for m in range(10):
                in_tile(0, m)
            pe.wait_ge(wrest_in, 48)
            x_proj(0, 0, 0)
            x_proj(0, 0, 1)
            turn_c(0, 0)
            dt_pair(0, 0, 0)
            dt_pair(0, 0, 1)
            for m in range(10, 16):
                in_tile(0, m)
            means(-1, False, True)
            variances(-1, False, True, 1)
            dt_pair(0, 0, 2)
            dt_pair(0, 0, 3)

            in_at = {0: (0,), 1: (1,), 2: (2,), 3: (3,), 4: (4,), 6: (5,), 7: (6,), 8: (7,), 14: (8,), 15: (9,),
                     24: (10,), 25: (11,), 26: (12,), 27: (13,), 28: (14, 15)}
            out_at = {5: (0, 0), 6: (1, 0), 8: (2, 0), 9: (3, 0), 10: (0, 1), 11: (1, 1), 12: (2, 1), 13: (3, 1)}

            def body(k, parity, image):
                scan, prepare, normalize, finish = runs(k)
                for unit in range(UNITS):
                    if scan:
                        turn_h(k, unit)
                        if unit in (21, 24):
                            turn_back(k, parity, (unit - 21) // 3)
                    if finish:
                        if unit in (2, 3):
                            turn_back(k - 1, 1 - parity, unit)
                        if unit in out_at:
                            out_tile(k - 1, 1 - parity, *out_at[unit])
                    if prepare:
                        for m in in_at.get(unit, ()):
                            in_tile(k + 1, m)
                        if unit in (16, 17):
                            x_proj(k + 1, 1 - parity, unit - 16)
                        if unit == 20:
                            dt_pair(k + 1, 1 - parity, 0)
                            dt_pair(k + 1, 1 - parity, 1)
                        if unit == 29:
                            turn_c(k + 1, 1 - parity)
                        if unit in (29, 31):
                            dt_pair(k + 1, 1 - parity, (unit - 25) // 2)
                    if unit == 18 and (finish or normalize):
                        means(k, finish, normalize)
                    if unit == 22 and finish:
                        variances(k, finish, normalize, 2)
                    if unit == 23 and normalize:
                        variances(k, finish, normalize, 1)

            iterations(pe, body)

        @block.scalar
        def _(act):
            act.wait_ge(consts_in, 48)
            act.preload_act_table_set("natural_log_exp_and_others")
            act.activation(neg_a[:, :, :], vec[:, V_AL:V_AL + DT * STATES].rearrange("p (d n) -> p d n", d=DT),
                           ACT.Exp).then_inc(set_act, 1)
            act.wait_ge(set_act, 1)
            act.activation(neg_a[:, :, :], neg_a[:, :, :], ACT.Copy, scale=-1.0).then_inc(set_act, 1)
            act.wait_ge(set_act, 2)
            act.wait_ge(set_dve, 4 + DS)

            def square1(c):
                act.wait_ge(*fin_bank_read(c - 2, MEANS))
                act.activation(sq, x_t[:, :, :], ACT.Square).then_inc(squared, 1)

            def rstd1(c):
                act.wait_ge(fin_mm, fin_made(c - 2, VARS))
                bank = fin_bank(c - 2, VARS)
                act.activation(ln_l[:, :], fin[:, bank, T:2 * T], ACT.Ln, bias=eps[:, 0:1],
                               scale=1.0 + EPS).then_inc(fin_read[bank], 1)
                act.wait_ge(*fin_bank_read(c - 2, VARS))
                act.activation(ln_r1[:, :], ln_l[:, :], ACT.Exp, scale=-0.5).then_inc(rstd_act, 1)

            def affine(c):
                act.wait_ge(x_scaled, c + 1)
                for kt in range(KT):
                    last = act.activation(xn[:, kt, :], xn[:, kt, :], ACT.Identity,
                                          bias=vec[:, V_LNB + kt:V_LNB + kt + 1],
                                          scale=vec[:, V_LNW + kt:V_LNW + kt + 1])
                last.then_inc(xn_ready, 1)

            def take_xin(c, q):
                act.wait_ge(tail_kept, c + 1)
                act.wait_ge(pre_mm, pre_made(c, XIN + q))
                if q == 0:
                    ge(act, u_ready, c)
                    act.wait_ge(fin_mm, fin_made(c - 2, VARS))
                for d in (2 * q, 2 * q + 1):
                    act.activation(cv[:, d, :], pre[:, q % 2, (d % 2) * T:(d % 2) * T + T], ACT.Identity,
                                   bias=vec[:, V_CB + d:V_CB + d + 1],
                                   scale=vec[:, V_CW + d * TAPS + TAPS - 1:V_CW + d * TAPS + TAPS])
                act.activation(xin[:, 2 * q:2 * q + 2, TAPS - 1:TAPS - 1 + T],
                               pre[:, q % 2, :].rearrange("p (a t) -> p a t", a=2), ACT.Copy).then_inc(pre_read[q % 2], 1)

            def silu_u(c, parity):
                act.wait_ge(conv_step, (c + 1) * 24)
                if not isinstance(c, int) or c >= 2:
                    act.wait_ge(fin_mm, fin_made(c - 1, OUT23))
                act.activation(u[:, parity], cv[:, :, :], ACT.Silu).then_inc(u_ready, 1)

            def take_z(c, parity, q):
                if not isinstance(c, int) or c >= 2:
                    act.wait_ge(y_gated, (c - 1) * 4)
                j = Z_GROUP[q]
                act.wait_ge(pre_mm, pre_made(c, j))
                act.activation(zs[:, parity, 2 * q:2 * q + 2, :],
                               pre[:, j % 2, :].rearrange("p (a t) -> p a t", a=2),
                               ACT.Copy).then_inc(pre_read[j % 2], 1)

            def silu_z(c, parity):
                act.wait_ge(*pre_bank_read(c, Z45))
                act.wait_ge(*pre_bank_read(c, Z67))
                act.activation(zs[:, parity], zs[:, parity], ACT.Silu).then_inc(z_ready, 1)

            def take_xd(c, parity):
                ge(act, b_stored, (c - 1) * 16)
                act.wait_ge(fin_mm, fin_made(c - 1, X_PROJ))
                bank = fin_bank(c - 1, X_PROJ)
                act.activation(xd[:, parity, :], fin[0:XR, bank, 0:T], ACT.Identity,
                               bias=vec[0:XR, V_XB:V_XB + 1]).then_inc(fin_read[bank], 1)

            def take_c(c, parity):
                ge(act, y_added, (c - 1) * UNITS * 2)
                act.wait_ge(fin_mm, fin_made(c - 1, TURN_C))
                bank = fin_bank(c - 1, TURN_C)
                src = fin[:, bank, 0:TS * XR].rearrange("p (s r) -> p s r", s=TS)[:, :, C_ROW:C_ROW + STATES]
                act.activation(c_tok[:, parity], src, ACT.Copy).then_inc(fin_read[bank], 1)

            def soft(c, q, step):
                half, pair = q // 2, q % 2
                t, l, w = sp_t[:, q % 2, :], sp_l[:, q % 2, :], sp_w[:, q % 2, :]
                j = DT_GROUP[q]
                steps = (c * 2 + half) * 4
                if step == 0:
                    ge(act, delta_ready, c * 4 + q - 1)
                    ge(act, da_ready, (c - 1) * UNITS + STATES * (half + 1))
                    ge(act, du_ready, (c - 1) * 2 + half + 1)
                    act.wait_ge(pre_mm, pre_made(c, j))
                    act.activation(t, pre[:, j % 2, :], ACT.Abs).then_inc(soft_act[pair], 1)
                    act.activation(delta[:, half, 2 * pair:2 * pair + 2, :].rearrange("p a t -> p (a t)"),
                                   pre[:, j % 2, :], ACT.Relu).then_inc(pre_read[j % 2], 1)
                elif step == 1:
                    act.wait_ge(soft_act[pair], steps + 1)
                    act.activation(t, t, ACT.Exp, scale=-1.0).then_inc(soft_act[pair], 1)
                    act.wait_ge(soft_act[pair], steps + 2)
                    act.activation(w, t, ACT.Identity, bias=1.0).then_inc(soft_act[pair], 1)
                else:
                    act.activation(sp_q[:, q % 2, :], t, ACT.Square, scale=HALF_ROOT)
                    act.wait_ge(soft_act[pair], steps + 3)
                    act.activation(l, w, ACT.Ln).then_inc(soft_act[pair], 1)

            def save_state(unit):
                half, n = unit // STATES, unit % STATES
                act.activation(state[:, half, n, :].rearrange("p (a b) -> p a b", b=1),
                               dbh[:, unit % HS, :, T:T + 1], ACT.Copy).then_inc(state_saved, 1)

            def decay(k, unit):
                half, n = unit // STATES, unit % STATES
                g = k * UNITS + unit
                ge(act, h_ready, g - DS + 1)
                if n == 0:
                    act.wait_ge(delta_ready, k * 4 + 2 * half + 2)
                for d in range(HT):
                    last = act.activation(da[:, unit % DS, d, 1:SEG], delta[:, half, d, :], ACT.Exp,
                                          scale=neg_a[:, HT * half + d, n:n + 1])
                last.then_inc(da_ready, 1)
                for lag in SAVE_LAGS.get(unit, (2,)):
                    if unit >= lag or not (isinstance(k, int) and k == 0):
                        ge(act, h_ready, g - lag + 1)
                        save_state((unit - lag) % UNITS)

            def take_y(c, parity, j):
                k, group = (c, (TB0, TB1)[j]) if j < 2 else (c + 1, (TB2, TB3)[j - 2])
                act.wait_ge(fin_mm, fin_made(k, group))
                act.activation(u[:, parity, 2 * j:2 * j + 2, :],
                               fin[:, group % 2, :].rearrange("p (a t) -> p a t", a=2),
                               ACT.Copy).then_inc(fin_read[group % 2], 1)

            def square2(c, alone):
                if alone:
                    act.wait_ge(*fin_bank_read(c + 1, MEANS))
                else:
                    act.wait_ge(centred2, c + 1)
                act.activation(sq2, d2[:, :, :], ACT.Square).then_inc(squared2, 1)

            def rstd2(c, alone):
                act.wait_ge(fin_mm, fin_made(c + 1, VARS))
                act.activation(ln2_l[:, :], fin[:, 1, 0:T], ACT.Ln,
                               bias=eps[:, 1:2]).then_inc(fin_read[1] if alone else ln2_log, 1)
                if alone:
                    act.wait_ge(*fin_bank_read(c + 1, VARS))
                else:
                    act.wait_ge(ln2_log, c + 1)
                act.activation(ln2_r[:, :], ln2_l[:, :], ACT.Exp, scale=-0.5).then_inc(ln2_ready, 1)

            def norm1(c):
                square1(c)
                rstd1(c)

            exps = "natural_log_exp_and_others"
            norm1(0)
            affine(0)
            for q in range(4):
                take_xin(0, q)
            take_z(0, 0, 0)
            silu_u(0, 0)
            take_xd(0, 0)
            take_c(0, 0)
            act.preload_act_table_set(exps)
            for q in range(2):
                for step in range(3):
                    soft(0, q, step)
            for q in range(1, 4):
                take_z(0, 0, q)
            norm1(1)

            soft_at = {23: ((0, 0),), 24: ((0, 1),), 25: ((0, 2), (1, 0)), 26: ((1, 1),), 27: ((1, 2),)}
            late_at = {0: ((2, 0),), 1: ((2, 1),), 2: ((3, 0),), 3: ((2, 2),), 4: ((3, 1),), 7: ((3, 2),)}
            xin_at = {4: 0, 6: 1, 9: 2, 11: 3}
            z_at = {18: 0, 28: 1, 29: 2, 31: 3}

            def body(k, parity, image):
                scan, prepare, normalize, finish = runs(k)
                for unit in range(UNITS):
                    if scan:
                        decay(k, unit)
                        for q, step in late_at.get(unit, ()):
                            soft(k, q, step)
                        if unit == 16 and not prepare:
                            silu_z(k, parity)
                        if unit in (24, 30):
                            take_y(k, parity, (unit - 24) // 6)
                    if prepare:
                        if unit == 0:
                            affine(k + 1)
                        if unit in xin_at:
                            take_xin(k + 1, xin_at[unit])
                        if unit == 16:
                            silu_u(k + 1, 1 - parity)
                            silu_z(k, parity)
                            act.preload_act_table_set(exps)
                        if unit in z_at:
                            take_z(k + 1, 1 - parity, z_at[unit])
                        if unit == 20:
                            take_xd(k + 1, 1 - parity)
                        for q, step in soft_at.get(unit, ()):
                            soft(k + 1, q, step)
                        if unit == 31:
                            take_c(k + 1, 1 - parity)
                    if normalize and unit == 23:
                        square1(k + 2)
                    if finish:
                        if unit in (5, 6):
                            take_y(k - 1, 1 - parity, unit - 3)
                        if unit == 22:
                            square2(k - 1, not normalize)
                        if unit == 26:
                            rstd2(k - 1, not normalize)
                    if normalize:
                        if unit == 28:
                            rstd1(k + 2)

            iterations(act, body)

        @block.vector
        def _(dve):
            for i, (dst, value) in enumerate(((eps[:, 0:1], CHANNEL_EPS * EPS), (eps[:, 1:2], EPS), (tsum[:, :, :], 0.0),
                                              (t_red[:, :], 0.0))):
                dve.memset(dst, value).then_inc(set_dve, 1)
            for slot in range(DS):
                dve.memset(da[:, slot, :, 0:1], 0.0).then_inc(set_dve, 1)
            dve.wait_ge(set_dve, 4 + DS)
            dve.wait_ge(consts_in, 48)
            for d in range(DT):
                dve.tensor_scalar(diag_d[:, d, :], ident[:, :], vec[:, V_D + d:V_D + d + 1], None,
                                  ALU.mult).then_inc(set_dve, 1)

            def centre1(c):
                dve.wait_ge(fin_mm, fin_made(c - 2, MEANS))
                bank = fin_bank(c - 2, MEANS)
                dve.tensor_tensor(x_t[:, :, :], x_t[:, :, :], fin[:, bank:bank + 1, T:2 * T].broadcast_to((P, KT, T)),
                                  ALU.subtract).then_inc(fin_read[bank], 1)

            def scale1(c):
                dve.wait_ge(rstd_act, c + 1)
                ge(dve, pre_mm, pre_made(c - 1, Z67))
                dve.tensor_tensor(xn[:, :, :], x_t[:, :, :],
                                  ln_r1[:, :].rearrange("p (a t) -> p a t", a=1).broadcast_to((P, KT, T)),
                                  ALU.mult).then_inc(x_scaled, 1)

            def keep_tail(c, first):
                ge(dve, conv_step, c * 24)
                if first:
                    dve.memset(xin[:, :, 0:TAPS - 1], 0.0).then_inc(tail_kept, 1)
                else:
                    dve.tensor_copy(xin[:, :, 0:TAPS - 1], xin[:, :, T:T + TAPS - 1]).then_inc(tail_kept, 1)

            def conv(c, q, half):
                if half == 0:
                    dve.wait_ge(*pre_bank_read(c, XIN + q))
                if q == 0 and half == 0:
                    dve.wait_ge(tail_kept, c + 1)
                for j in ((0, 1), (2,))[half]:
                    for tile in range(2):
                        d = 2 * q + tile
                        if j:
                            dve.wait_ge(conv_step, c * 24 + q * 6 + 2 * j - 1 + tile)
                        dve.scalar_tensor_tensor(cv[:, d, :], xin[:, d, j:j + T],
                                                 vec[:, V_CW + d * TAPS + j:V_CW + d * TAPS + j + 1], cv[:, d, :],
                                                 ALU.mult, ALU.add).then_inc(conv_step, 1)

            def soften(c, q):
                l = sp_l[:, q % 2, :]
                steps = (c * 4 + q) * 2
                dve.wait_ge(soft_act[q % 2], (c * 2 + q // 2) * 4 + 4)
                dve.scalar_tensor_tensor(l, sp_w[:, q % 2, :], -1.0, l, ALU.add, ALU.subtract).then_inc(soft_dve, 1)
                dve.wait_ge(soft_dve, steps + 1)
                dve.scalar_tensor_tensor(l, l, 0.0, sp_q[:, q % 2, :], ALU.max, ALU.min).then_inc(soft_dve, 1)

            def scan(k, unit):
                g = k * UNITS + unit
                h = dbh[:, unit % HS].rearrange("p a t -> p (a t)")
                dve.wait_ge(da_ready, g + 1)
                dve.wait_ge(db_ready, g + 1)
                dve.tensor_tensor_scan(h, da[:, unit % DS].rearrange("p a t -> p (a t)"), h, 0.0, ALU.mult,
                                       ALU.add).then_inc(h_ready, 1)

            def add_y(k, unit, parity):
                half, n = unit // STATES, unit % STATES
                g = k * UNITS + unit
                if unit == 0:
                    dve.wait_ge(*fin_bank_read(k - 1, TURN_C))
                for ts in range(TS):
                    dve.wait_ge(h_turned, g * 2 + ts + 1)
                    src, acc, cn = h_tok[:, (2 * unit + ts) % 4, :], y_t[:, half, ts, :], c_tok[:, parity, ts, n:n + 1]
                    if n == 0:
                        if ts == 0:
                            if not isinstance(k, int) or k:
                                dve.wait_ge(fin_mm, fin_made(k, TB3) if half else fin_made(k - 1, TB1))
                        dve.tensor_scalar(acc, src, cn, None, ALU.mult).then_inc(y_added, 1)
                    else:
                        dve.wait_ge(y_added, g * 2 + ts - 1)
                        dve.scalar_tensor_tensor(acc, src, cn, acc, ALU.mult, ALU.add).then_inc(y_added, 1)

            def residual(c, i):
                j = (OUT01, OUT23)[i]
                dve.wait_ge(xres_in, (c + 1) * 16)
                dve.wait_ge(fin_mm, fin_made(c + 1, j))
                xr = x2[:, 2 * i:2 * i + 2, :].rearrange("p a t -> p (a t)")
                dve.tensor_tensor(xr, xr, fin[:, j % 2, :], ALU.add).then_inc(fin_read[j % 2], 1)

            def centre2(c, alone):
                dve.wait_ge(fin_mm, fin_made(c + 1, MEANS))
                dve.wait_ge(*fin_bank_read(c + 1, OUT01))
                dve.wait_ge(*fin_bank_read(c + 1, OUT23))
                ge(dve, stored, c * 32)
                dve.tensor_tensor(d2[:, :, :], x2[:, :, :], fin[:, 1:2, 0:T].broadcast_to((P, KT, T)),
                                  ALU.subtract).then_inc(fin_read[1] if alone else centred2, 1)

            def scale2(c):
                dve.wait_ge(ln2_ready, c + 1)
                ge(dve, tok_step, c * 2)
                for kt in range(KT):
                    last = dve.scalar_tensor_tensor(d2[:, kt, :], d2[:, kt, :], 1.0, ln2_r[:, :], ALU.mult, ALU.mult,
                                                    accum_out=t_red[:, kt:kt + 1])
                last.then_inc(tok_step, 1)

            def sum_tokens(c, b):
                dve.wait_ge(tok_step, c * 2 + 1)
                dve.tensor_tensor(tsum[:, :, b], tsum[:, :, b], t_red[:, :], ALU.add).then_inc(tok_step, 1)

            def norm1(c):
                centre1(c)
                scale1(c)

            norm1(0)
            keep_tail(0, True)
            for q in range(4):
                conv(0, q, 0)
                conv(0, q, 1)
            soften(0, 0)
            soften(0, 1)
            norm1(1)

            conv_at = (5, 6, 7, 8, 10, 11, 12, 13)

            def body(k, parity, image):
                scans, prepare, normalize, finish = runs(k)
                b = image if not isinstance(k, int) else (k - 1) // CPB
                for unit in range(UNITS):
                    if scans:
                        scan(k, unit)
                        if unit >= LAG:
                            add_y(k, unit - LAG, parity)
                    if finish:
                        if unit < LAG:
                            add_y(k - 1, UNITS - LAG + unit, 1 - parity)
                        if unit in (13, 15):
                            residual(k - 1, (unit - 13) // 2)
                        if unit == 20:
                            centre2(k - 1, not normalize)
                        if unit == 28:
                            scale2(k - 1)
                        if unit == 29:
                            sum_tokens(k - 1, b)
                    if prepare:
                        if unit == 1:
                            keep_tail(k + 1, isinstance(k, int) and (k + 1) % CPB == 0)
                        if unit in conv_at:
                            conv(k + 1, conv_at.index(unit) // 2, conv_at.index(unit) % 2)
                        if unit in (26, 28):
                            soften(k + 1, (unit - 26) // 2)
                    if scans:
                        if unit in (4, 9):
                            soften(k, 2 + (unit - 4) // 5)
                    if normalize:
                        if unit == 21:
                            centre1(k + 2)
                        if unit == 30:
                            scale1(k + 2)

            iterations(dve, body)


R_B1, R_RW, R_B2 = 0, FT, FT + KT * PARTS
R_SEL = R_B2 + DIM
R_PW = R_SEL + FT * P
R_REV = R_PW + EXPERTS
R_COLS = R_REV + PARTS + BATCH


def build_experts(nc, w1_raw, w1_loaded, tsum, x2_scr, tn_scr, w2_in, r_in, out):
    with ExitStack() as ctx:
        def sb(name, shape, dt=F32):
            return ctx.enter_context(nc.sbuf_tensor(name, shape, dt))

        def sem(name):
            return ctx.enter_context(nc.semaphore(name))

        w2_lo = sb("w2_lo", [P, FT, DIM], F32R)
        w1_hi = sb("w1_hi", [P, KT, FPAD], F32R)
        w1_lo = sb("w1_lo", [P, KT, FPAD], F32R)
        w2_hi = sb("w2_hi", [P, FT, DIM], F32R)
        raw = sb("raw", [P, RS, TF])
        tn = sb("tn", [P, KT, TF])
        t_hi = sb("t_hi", [P, 2, KT, TF], F32R)
        t_lo = sb("t_lo", [P, 2, KT, TF], F32R)
        x2t = sb("x2t", [P, 2, KT, TF])
        g = sb("g", [P, 2, TF])
        g_hi = sb("g_hi", [P, 2, TF], F32R)
        g_lo = sb("g_lo", [P, 2, TF], F32R)
        wf = sb("wf", [P, FT + KT, BATCH])
        b1 = sb("b1", [P, FT])
        h_ps = ctx.enter_context(nc.psum_tensor("h_ps", [P, 4, TF], F32))
        acc = ctx.enter_context(nc.psum_tensor("acc", [P, KT, TF], F32))
        r_all = x2t[:, :, :, :].rearrange("p a k t -> p (a k t)")

        r_sem, tn_in, raw_read, router_pe, router_dve, router_act, routed = (
            sem("r_sem"), sem("tn_in"), sem("raw_read"), sem("router_pe"), sem("router_dve"),
            sem("router_act"), sem("routed"))
        raw_in = [sem(f"raw_in{i}") for i in range(RS)]
        w1_high, w1_split = sem("w1_high"), sem("w1_split")
        x2_in = [sem(f"x2_in{i}") for i in range(2)]
        out_stored = [sem(f"out_stored{i}") for i in range(2)]
        raw_scaled, split_hi = sem("raw_scaled"), sem("split_hi")
        tok_hi, tok_split = sem("tok_hi"), sem("tok_split")
        h_mm, h_read, g_hi_ready, g_lo_ready, o_mm, acc_read = (
            sem("h_mm"), sem("h_read"), sem("g_hi_ready"), sem("g_lo_ready"), sem("o_mm"), sem("acc_read"))
        last = BATCH * FCPB - 1

        def chunks(eng, body):
            body(0, 0, 0, False, True, False, False)
            with eng.Fori(0, FCPB // 2 - 1) as i:
                body(i * 2 + 1, 1, 0, True, True, False, False)
                body(i * 2 + 2, 0, 0, True, True, False, False)
            body(FCPB - 1, 1, 0, True, True, True, False)
            body(FCPB, 0, 1, True, True, False, True)
            with eng.Fori(0, FCPB // 2 - 1) as i:
                body(i * 2 + FCPB + 1, 1, 1, True, True, False, False)
                body(i * 2 + FCPB + 2, 0, 1, True, True, False, False)
            body(last, 1, 1, True, False, False, False)

        block = ctx.enter_context(nc.Block())

        @block.sync
        def _(sp):
            def chunk_of(dram, b, c):
                t0 = (c - b * FCPB) * TF
                view = dram[b].rearrange("(k p) t -> p k t", p=P)
                return view[:, :, t0:t0 + TF] if isinstance(c, int) else view[:, :, bass.ds(t0, TF)]

            def chunk_at(dram, c):
                return dram[c] if isinstance(c, int) else dram[bass.ds(c, 1)].rearrange("a p k t -> (a p) k t")

            def load_piece(r):
                ge(sp, raw_read, r - RS + 1)
                sp.dma_start(raw[:, r % RS, :], w2_in[:, r % FT, :]).then_inc(raw_in[r % RS], 16)

            def load_tn(b, c):
                ge(sp, tok_split, c * KT)
                for i in range(TF // T):
                    sp.dma_start(tn[:, :, i * T:i * T + T], chunk_at(tn_scr, 2 * c + i)).then_inc(tn_in, 16)

            def load_x2(b, c, parity):
                ge(sp, out_stored[parity], (c - parity) // 2 * 16 if isinstance(c, int) else (c - parity) * 8)
                for i in range(TF // T):
                    sp.dma_start(x2t[:, parity, :, i * T:i * T + T],
                                 chunk_at(x2_scr, 2 * c + i)).then_inc(x2_in[parity], 16)

            def store(b, c, parity):
                sp.wait_ge(acc_read, (c + 1) * KT)
                sp.dma_start(chunk_of(out, b, c), x2t[:, parity]).then_inc(out_stored[parity], 16)

            sp.dma_start(r_all[:, 0:R_COLS - FT], r_in[:, FT:R_COLS]).then_inc(r_sem, 16)
            sp.dma_start(b1[:, :], r_in[:, R_B1:R_B1 + FT]).then_inc(r_sem, 16)
            load_tn(0, 0)
            for r in range(FT):
                load_piece(r)
            sp.wait_ge(routed, 2)
            load_x2(0, 0, 0)

            def body(c, parity, image, prev, nxt, closing, opening):
                after = image if not isinstance(c, int) else (c + 1) // FCPB
                before = image if not isinstance(c, int) else (c - 1) // FCPB
                if opening:
                    for r in range(2 * FT - 2, 2 * FT):
                        load_piece(r)
                if prev:
                    store(before, c - 1, 1 - parity)
                if nxt:
                    load_tn(after, c + 1)
                    load_x2(after, c + 1, 1 - parity)
                if closing:
                    for r in range(FT, 2 * FT - 2):
                        load_piece(r)

            chunks(sp, body)
            store(1, last, 1)
            sp.wait_ge(out_stored[0], (last + 1) * 8)
            sp.wait_ge(out_stored[1], (last + 1) * 8)

        def table(col, width, rows):
            return r_all[0:rows, col - FT:col - FT + width]

        def small(i, rows=BATCH, cols=PARTS):
            return g[0:rows, 0, 16 * i:16 * i + cols]

        logits, probs, sel1, sel2, mix, hot, rest = (small(i) for i in range(7))
        top, neg_top, total, m1, m2, r1, r2 = (small(7 + i, cols=1) for i in range(7))
        mix_t, w_e = small(14, PARTS, BATCH), small(15, EXPERTS, BATCH)

        @block.gpsimd
        def _(pool):
            pool.wait_ge(w1_loaded, 16)
            for block_ in range(KT):
                for kt in range(KT):
                    cols = slice(block_ * TF, block_ * TF + TF)
                    pool.wait_ge(w1_high, block_ * KT + kt + 1)
                    pool.tensor_tensor(w1_lo[:, kt, cols], w1_raw[:, kt, cols], w1_hi[:, kt, cols],
                                       ALU.subtract).then_inc(w1_split, 1)

        @block.tensor
        def _(pe):
            pe.wait_ge(r_sem, 32)
            for kt in range(KT):
                mm = pe.matmul(h_ps[0:BATCH, 0, 0:PARTS], tsum[:, kt, :], table(R_RW + kt * PARTS, PARTS, P),
                               start=kt == 0, stop=kt == KT - 1)
            mm.then_inc(router_pe, 1)
            pe.wait_ge(routed, 1)
            pe.transpose(h_ps[0:PARTS, 1, 0:BATCH], mix, table(R_REV + PARTS, BATCH, BATCH)).then_inc(router_pe, 1)
            pe.wait_ge(router_act, 2)
            pe.matmul(h_ps[0:EXPERTS, 2, 0:BATCH], table(R_PW, EXPERTS, PARTS), mix_t, start=True,
                      stop=True).then_inc(router_pe, 1)
            pe.wait_ge(router_act, 3)
            for f in range(FT):
                pe.matmul(h_ps[:, 3, 2 * f:2 * f + 2], table(R_SEL + f * P, P, EXPERTS), w_e, start=True, stop=True)
            for m in range(KT):
                mm = pe.matmul(h_ps[:, 3, 2 * (FT + m):2 * (FT + m) + 2], table(R_B2 + m * P, P, EXPERTS), w_e,
                               start=True, stop=True)
            mm.then_inc(router_pe, 1)
            pe.wait_ge(routed, 2)

            def hidden(c, parity, f):
                ge(pe, h_read, c * FT + f - 3)
                if f == 0:
                    pe.wait_ge(tok_split, (c + 1) * KT)
                if isinstance(c, int) and c == 0 and f % KT == 0:
                    pe.wait_ge(w1_split, f + KT)
                cols = slice(f * P, f * P + P)
                terms = [(w, t, kt) for w, t in ((w1_hi, t_hi), (w1_lo, t_hi), (w1_hi, t_lo)) for kt in range(KT)]
                for i, (w, t, kt) in enumerate(terms):
                    mm = pe.matmul(h_ps[:, f % 4, :], w[:, kt, cols], t[:, parity, kt, :], start=i == 0,
                                   stop=i == len(terms) - 1)
                mm.then_inc(h_mm, 1)

            def project(c, image, f):
                pe.wait_ge(g_lo_ready, c * FT + f + 1)
                pe.wait_ge(raw_read, image * FT + f + 1)
                for m in range(KT):
                    if f == 0:
                        ge(pe, acc_read, (c - 1) * KT + m + 1)
                    cols = slice(m * P, m * P + P)
                    for i, (w, t) in enumerate(((w2_hi, g_hi), (w2_lo, g_hi), (w2_hi, g_lo))):
                        mm = pe.matmul(acc[:, m, :], w[:, f, cols], t[:, f % 2, :], start=f == 0 and i == 0,
                                       stop=f == FT - 1 and i == 2)
                mm.then_inc(o_mm, 1)

            def body(c, parity, image, prev, nxt, closing, opening):
                before = image if not isinstance(c, int) else (c - 1) // FCPB
                for f in range(FT):
                    hidden(c, parity, f)
                    if f:
                        project(c, image, f - 1)
                    elif prev:
                        project(c - 1, before, FT - 1)

            chunks(pe, body)
            project(last, 1, FT - 1)

        @block.scalar
        def _(act):
            def high_w1(block):
                for kt in range(KT):
                    cols = slice(block * TF, block * TF + TF)
                    act.activation(w1_hi[:, kt, cols], w1_raw[:, kt, cols], ACT.Copy).then_inc(w1_high, 1)

            act.wait_ge(w1_loaded, 16)
            high_w1(0)
            act.wait_ge(router_dve, 3)
            act.activation(probs, logits, ACT.Exp, bias=neg_top).then_inc(router_act, 1)
            high_w1(1)
            act.wait_ge(router_pe, 2)
            act.activation(mix_t, h_ps[0:PARTS, 1, 0:BATCH], ACT.Copy).then_inc(router_act, 1)
            high_w1(2)
            act.wait_ge(router_dve, 20)
            act.activation(w_e, small(16, EXPERTS, BATCH), ACT.Copy).then_inc(router_act, 1)
            high_w1(3)
            act.wait_ge(routed, 2)
            act.preload_act_table_set("gelu_and_others")

            def gelu(c, f):
                ge(act, g_lo_ready, c * FT + f - 1)
                act.wait_ge(h_mm, c * FT + f + 1)
                act.activation(g[:, f % 2, :], h_ps[:, f % 4, :], ACT.Gelu, bias=b1[:, f:f + 1]).then_inc(h_read, 1)
                ge(act, o_mm, c * FT + f - 1)
                act.wait_ge(h_read, c * FT + f + 1)
                act.activation(g_hi[:, f % 2, :], g[:, f % 2, :], ACT.Copy).then_inc(g_hi_ready, 1)

            def body(c, parity, image, prev, nxt, closing, opening):
                for f in range(FT):
                    gelu(c, f)

            chunks(act, body)

        @block.vector
        def _(dve):
            steps = [0]

            def step(ins):
                steps[0] += 1
                ins.then_inc(router_dve, 1)
                dve.wait_ge(router_dve, steps[0])

            def split_w2(image, f):
                r = FT * image + f
                slot = raw[:, r % RS, :]
                dve.wait_ge(raw_in[r % RS], (r // RS + 1) * 16)
                ge(dve, o_mm, (image * FCPB - 1) * FT + f + 1)
                dve.tensor_scalar(slot, slot, wf[:, f, image:image + 1], None, ALU.mult).then_inc(raw_scaled, 1)
                dve.wait_ge(raw_scaled, image * FT + f + 1)
                dve.tensor_copy(w2_hi[:, f, :], slot).then_inc(split_hi, 1)
                dve.wait_ge(split_hi, r + 1)
                dve.tensor_tensor(w2_lo[:, f, :], slot, w2_hi[:, f, :], ALU.subtract).then_inc(raw_read, 1)

            def split_tokens(c, parity, kt):
                if kt == 0:
                    ge(dve, h_mm, (c - 1) * FT)
                    dve.wait_ge(tn_in, (c + 1) * 32)
                dve.tensor_copy(t_hi[:, parity, kt, :], tn[:, kt, :]).then_inc(tok_hi, 1)
                dve.wait_ge(tok_hi, c * KT + kt + 1)
                dve.tensor_tensor(t_lo[:, parity, kt, :], tn[:, kt, :], t_hi[:, parity, kt, :],
                                  ALU.subtract).then_inc(tok_split, 1)

            def low_half(c, f):
                dve.wait_ge(g_hi_ready, c * FT + f + 1)
                dve.tensor_tensor(g_lo[:, f % 2, :], g[:, f % 2, :], g_hi[:, f % 2, :],
                                  ALU.subtract).then_inc(g_lo_ready, 1)

            def drain(c, parity, image, m):
                if m == 0:
                    dve.wait_ge(o_mm, (c + 1) * FT)
                    dve.wait_ge(x2_in[parity], (c - parity) * 16 + 32)
                x = x2t[:, parity, m, :]
                dve.scalar_tensor_tensor(x, acc[:, m, :], wf[:, FT + m, image:image + 1], x, ALU.add,
                                         ALU.add).then_inc(acc_read, 1)

            for kt in range(KT):
                split_tokens(0, 0, kt)
            dve.wait_ge(router_pe, 1)
            rev = table(R_REV, PARTS, BATCH)
            step(dve.tensor_scalar(logits, h_ps[0:BATCH, 0, 0:PARTS], 1.0 / TOKENS, None, ALU.mult))
            step(dve.tensor_reduce(top, logits, AX_X, ALU.max))
            step(dve.tensor_scalar(neg_top, top, -1.0, None, ALU.mult))
            dve.wait_ge(router_act, 1)
            step(dve.tensor_reduce(total, probs, AX_X, ALU.add))
            step(dve.reciprocal(total, total))
            step(dve.tensor_scalar(probs, probs, total, None, ALU.mult))
            step(dve.tensor_reduce(m1, probs, AX_X, ALU.max))
            step(dve.scalar_tensor_tensor(hot, probs, m1, rev, ALU.is_equal, ALU.mult))
            step(dve.tensor_reduce(r1, hot, AX_X, ALU.max))
            step(dve.tensor_scalar(sel1, rev, r1, None, ALU.is_equal))
            step(dve.scalar_tensor_tensor(rest, sel1, -2.0, probs, ALU.mult, ALU.add))
            step(dve.tensor_reduce(m2, rest, AX_X, ALU.max))
            step(dve.scalar_tensor_tensor(hot, rest, m2, rev, ALU.is_equal, ALU.mult))
            step(dve.tensor_reduce(r2, hot, AX_X, ALU.max))
            step(dve.tensor_scalar(sel2, rev, r2, m2, ALU.is_equal, ALU.mult))
            step(dve.scalar_tensor_tensor(mix, sel1, m1, sel2, ALU.mult, ALU.add))
            step(dve.tensor_tensor(m1, m1, m2, ALU.add))
            step(dve.reciprocal(m1, m1))
            dve.tensor_scalar(mix, mix, m1, None, ALU.mult).then_inc(routed, 1)
            dve.wait_ge(router_pe, 3)
            raw_w = small(17, EXPERTS, BATCH)
            step(dve.tensor_copy(raw_w, h_ps[0:EXPERTS, 2, 0:BATCH]))
            step(dve.scalar_tensor_tensor(small(16, EXPERTS, BATCH), raw_w, 1e-6, raw_w, ALU.is_gt, ALU.mult))
            assert steps[0] == 20
            dve.wait_ge(router_pe, 4)
            dve.tensor_copy(wf[:, :, :], h_ps[:, 3, 0:2 * (FT + KT)].rearrange("p (f b) -> p f b", b=2))\
               .then_inc(routed, 1)

            dve.wait_ge(routed, 2)
            dve.wait_ge(w1_split, FT)
            for f in range(FT):
                split_w2(0, f)

            def body(c, parity, image, prev, nxt, closing, opening):
                before = image if not isinstance(c, int) else (c - 1) // FCPB
                for f in range(FT):
                    if f == 1 and prev:
                        for m in range(KT):
                            drain(c - 1, 1 - parity, before, m)
                    low_half(c, f)
                    if 4 <= f < 4 + KT and nxt:
                        split_tokens(c + 1, 1 - parity, f - 4)
                    if closing and f >= 2:
                        split_w2(1, f - 2)
                    if opening and f < 2:
                        split_w2(1, FT - 2 + f)

            chunks(dve, body)
            for m in range(KT):
                drain(last, 1, 1, m)


def build(nc, x, vecs, ident, mean_w, wi, wo, wx, wdt, w1, w2, router, out):
    b_scr = nc.dram_tensor("b_scr", (CHUNKS, STATES, T), F32, kind="Internal").ap()
    x2_scr = nc.dram_tensor("x2_scr", (CHUNKS, P, KT, T), F32, kind="Internal").ap()
    tn_scr = nc.dram_tensor("tn_scr", (CHUNKS, P, KT, T), F32, kind="Internal").ap()
    with nc.sbuf_tensor("tsum", [P, KT, BATCH], F32) as tsum, nc.semaphore("w1_loaded") as w1_loaded:
        with nc.sbuf_tensor("w_big", [P, KT, FPAD], F32) as w_big:
            build_mixer(nc, w_big, w1, w1_loaded, x, vecs, ident, mean_w, wi, wo, wx, wdt, tsum, b_scr, x2_scr, tn_scr)
        build_experts(nc, w_big, w1_loaded, tsum, x2_scr, tn_scr, w2, router, out)


def kernel(x, L0_conv_ln_w, L0_conv_ln_b, L0_conv_in_proj_w, L0_conv_conv_w, L0_conv_conv_b, L0_conv_x_proj_w,
           L0_conv_dt_proj_w, L0_conv_dt_proj_b, L0_conv_A_log, L0_conv_D_skip, L0_conv_out_proj_w,
           L0_ffn_router_w, L0_ffn_W1, L0_ffn_b1, L0_ffn_W2, L0_ffn_b2):
    import concourse.bacc as bacc
    from concourse.bass_utils import run_bass_kernel_spmd

    f32 = np.float32

    def tiles(a, rows):
        a = np.asarray(a, f32)
        return np.ascontiguousarray(a.reshape(rows // P, P, -1).transpose(1, 0, 2))

    xb = np.zeros((P, 1), f32)
    xb[ONE_ROW] = 1.0
    vecs = np.concatenate([tiles(L0_conv_ln_w, DIM).reshape(P, -1), tiles(L0_conv_ln_b, DIM).reshape(P, -1),
                           tiles(L0_conv_conv_w, INNER).reshape(P, -1), tiles(L0_conv_conv_b, INNER).reshape(P, -1),
                           tiles(L0_conv_D_skip, INNER).reshape(P, -1), tiles(L0_conv_A_log, INNER).reshape(P, -1),
                           xb], axis=1)
    xp = np.asarray(L0_conv_x_proj_w, f32)
    wx = np.zeros((INNER, XR), f32)
    wx[:, 0:RANK] = xp[0:RANK].T
    wx[:, B_ROW:B_ROW + STATES] = xp[RANK:RANK + STATES].T
    wx[:, C_ROW:C_ROW + STATES] = xp[RANK + STATES:].T
    wdt = np.concatenate([np.asarray(L0_conv_dt_proj_w, f32).T, np.asarray(L0_conv_dt_proj_b, f32)[None]], axis=0)
    w1 = np.zeros((DIM, FPAD), f32)
    w1[:, :EXPERTS * HIDDEN] = np.asarray(L0_ffn_W1, f32).transpose(1, 0, 2).reshape(DIM, -1)
    w2 = np.zeros((FPAD, DIM), f32)
    w2[:EXPERTS * HIDDEN] = np.asarray(L0_ffn_W2, f32).reshape(-1, DIM)
    b1 = np.zeros((FPAD, 1), f32)
    b1[:EXPERTS * HIDDEN, 0] = np.asarray(L0_ffn_b1, f32).reshape(-1)

    partitions = [(6,), (5, 1), (4, 2), (4, 1, 1), (3, 3), (3, 2, 1), (3, 1, 1, 1), (2, 2, 2), (2, 2, 1, 1),
                  (2, 1, 1, 1, 1), (1, 1, 1, 1, 1, 1)]
    router = np.zeros((P, R_COLS), f32)
    router[:, R_B1:R_B1 + FT] = tiles(b1, FPAD).reshape(P, -1)
    router[:, R_RW:R_RW + KT * PARTS] = tiles(np.asarray(L0_ffn_router_w, f32).T, DIM).reshape(P, -1)
    router[0:EXPERTS, R_B2:R_B2 + DIM] = np.asarray(L0_ffn_b2, f32)
    for e in range(EXPERTS):
        router[e, R_SEL + e * HIDDEN:R_SEL + (e + 1) * HIDDEN] = 1.0
    for i, parts in enumerate(partitions):
        for j, part in enumerate(parts):
            router[i, R_PW + j] = f32(part / 6)
    router[0:BATCH, R_REV:R_REV + PARTS] = np.arange(PARTS, 0, -1, dtype=f32)
    router[0:BATCH, R_REV + PARTS:R_REV + PARTS + BATCH] = np.eye(BATCH, dtype=f32)

    arrays = {
        "x": np.ascontiguousarray(np.asarray(x, f32).reshape(BATCH, KT, P, CPB, T).transpose(0, 3, 2, 1, 4)
                                  .reshape(CHUNKS, P, KT, T)), "vecs": vecs,
        "ident": np.eye(P, dtype=f32), "mean_w": np.full((P, P), 1.0 / DIM, f32),
        "wi": tiles(np.asarray(L0_conv_in_proj_w, f32).T, DIM), "wo": tiles(np.asarray(L0_conv_out_proj_w, f32).T, INNER),
        "wx": tiles(wx, INNER), "wdt": np.ascontiguousarray(wdt), "w1": tiles(w1, DIM), "w2": tiles(w2, FPAD),
        "router": router,
    }
    nc = bacc.Bacc("TRN2", target_bir_lowering=False, num_devices=1)
    args = [nc.dram_tensor("in_" + name, a.shape, F32, kind="ExternalInput").ap() for name, a in arrays.items()]
    out = nc.dram_tensor("out", (BATCH, DIM, TOKENS), F32, kind="ExternalOutput").ap()
    build(nc, *args, out)
    r = run_bass_kernel_spmd(nc, [{"in_" + name: a for name, a in arrays.items()}], core_ids=[0])
    return r.results[0]["out"].reshape(BATCH, DIM, 64, 64)
```
